# Optimizing a Trainium2 kernel written in Bass

```python
import numpy as np
import jax
import jax.numpy as jnp

def _softmax(x, axis=-1):
    return jax.nn.softmax(x, axis=axis)

def _gelu(x):
    return jax.nn.gelu(x, approximate=True)

def _silu(x):
    return jax.nn.silu(x)

def _sigmoid(x):
    return jax.nn.sigmoid(x)

def _layernorm(x, axis=-1, eps=1e-05):
    m = jnp.mean(x, axis=axis, keepdims=True)
    v = jnp.var(x, axis=axis, keepdims=True)
    return (x - m) / jnp.sqrt(v + eps)

def _scatter_add(tgt, idx, src, axis=0):
    return tgt.at[idx].add(src)

def _segment_sum(src, seg, n):
    return jax.ops.segment_sum(src, seg, n)
kernel_name = 'mk_decoder_preln_d4_seqx_r8_0bc415'

def setup_inputs(seed: int=0):
    np.random.seed(seed)
    _w = jnp.asarray

    def _rec_inputs():
        import jax
        import jax.numpy as jnp
        _rk = jax.random.key(seed)
        x = -0.0002928 + 1 * jax.random.normal(jax.random.fold_in(_rk, 1), (8, 56, 128), jnp.float32)
        _lenS = 56 - jax.random.randint(jax.random.fold_in(_rk, 7), (8,), 0, max(1, 56 // 4) + 1, jnp.int32)
        _lenS2 = 1500 - jax.random.randint(jax.random.fold_in(_rk, 8), (8,), 0, max(1, 1500 // 4) + 1, jnp.int32)
        _ctx_1024P = jax.random.normal(jax.random.fold_in(_rk, 11), (8, 16, 128), jnp.float32)
        _ctx_1024c = jax.random.dirichlet(jax.random.fold_in(_rk, 511), 0.3 * jnp.ones((16,), jnp.float32), (8, 1500))
        _ctx_1024t = jnp.einsum('bsk,bkd->bsd', _ctx_1024c, _ctx_1024P)
        _ctx_1024t = _ctx_1024t * jax.lax.rsqrt(jnp.mean(jnp.square(_ctx_1024t)) + 1e-12) * 0.953939
        ctx_1024 = -0.000137203 + 0.999727 * (_ctx_1024t + 0.3 * jax.random.normal(jax.random.fold_in(_rk, 611), (8, 1500, 128), jnp.float32))
        _validS = jnp.arange(56)[None, :] < _lenS[:, None]
        _validS2 = jnp.arange(1500)[None, :] < _lenS2[:, None]
        _causal = jnp.tril(jnp.ones((56, 56), dtype=bool))
        mask_BxS2_ik0 = jnp.where(jnp.broadcast_to(_validS2[:, :], (8, 1500)), 0, 1).astype(jnp.int32)
        return (x, ctx_1024, mask_BxS2_ik0)
    x, ctx_1024, mask_BxS2_ik0 = _rec_inputs()

    def _L0_attn_setup():
        import math
        import jax, jax.numpy as jnp
        import numpy as np
        D_MODEL = 128
        N_HEADS = 16
        HEAD_DIM = D_MODEL // N_HEADS
        D_FF = 512
        LN_EPS = 1e-05

        def _layer_norm(x, g, b):
            mu = jnp.mean(x, axis=-1, keepdims=True)
            var = jnp.var(x, axis=-1, keepdims=True)
            return (x - mu) * jax.lax.rsqrt(var + LN_EPS) * g + b
        key = jax.random.key(seed)
        ks = jax.random.split(key, 8)
        s = 0.02
        d, dff = (D_MODEL, D_FF)
        return {'src': jax.random.normal(ks[0], (2, 256, d), dtype=jnp.float32), 'in_proj_w': jax.random.normal(ks[1], (3 * d, d), dtype=jnp.float32) * s, 'in_proj_b': jnp.zeros((3 * d,), dtype=jnp.float32), 'out_w': jax.random.normal(ks[2], (d, d), dtype=jnp.float32) * s, 'out_b': jnp.zeros((d,), dtype=jnp.float32), 'lin1_w': jax.random.normal(ks[3], (dff, d), dtype=jnp.float32) * s, 'lin1_b': jnp.zeros((dff,), dtype=jnp.float32), 'lin2_w': jax.random.normal(ks[4], (d, dff), dtype=jnp.float32) * s, 'lin2_b': jnp.zeros((d,), dtype=jnp.float32), 'ln1_g': jnp.ones((d,), dtype=jnp.float32), 'ln1_b': jnp.zeros((d,), dtype=jnp.float32), 'ln2_g': jnp.ones((d,), dtype=jnp.float32), 'ln2_b': jnp.zeros((d,), dtype=jnp.float32)}
    _L0_attn_all = _L0_attn_setup()
    _L0_attn_in = {k: v for k, v in _L0_attn_all.items() if k in ('in_proj_w', 'in_proj_b', 'out_w', 'out_b', 'lin1_w', 'lin1_b', 'lin2_w', 'lin2_b', 'ln1_g', 'ln1_b', 'ln2_g', 'ln2_b')}
    del _L0_attn_all

    def _L0_xattn_setup():
        import jax, jax.numpy as jnp
        import numpy as np
        DIM = 128
        NHEADS = 8
        HEAD_DIM = DIM // NHEADS
        ROPE_BASE = 10000.0

        def _rope(t, positions):
            d = t.shape[-1]
            inv_freq = 1.0 / ROPE_BASE ** (jnp.arange(0, d, 2, dtype=jnp.float32) / d)
            freqs = positions[:, None].astype(jnp.float32) * inv_freq
            emb = jnp.concatenate([freqs, freqs], axis=-1)
            cos = jnp.cos(emb)[None, :, None, :].astype(t.dtype)
            sin = jnp.sin(emb)[None, :, None, :].astype(t.dtype)
            t1, t2 = jnp.split(t, 2, axis=-1)
            rot = jnp.concatenate([-t2, t1], axis=-1)
            return t * cos + rot * sin
        key = jax.random.key(seed)
        k1, k2, k3, k4, k5 = jax.random.split(key, 5)
        B, T, S = (2, 256, 375)
        w_std = 1.0 / np.sqrt(DIM)
        return {'x': jax.random.normal(k1, (B, T, DIM), dtype=jnp.float32), 'xmel': jax.random.normal(k2, (B, S, DIM), dtype=jnp.float32), 'Wq': jax.random.normal(k3, (DIM, DIM), dtype=jnp.float32) * w_std, 'Wkv': jax.random.normal(k4, (2 * DIM, DIM), dtype=jnp.float32) * w_std, 'Wout': jax.random.normal(k5, (DIM, DIM), dtype=jnp.float32) * w_std}
    _L0_xattn_all = _L0_xattn_setup()
    _L0_xattn_in = {k: v for k, v in _L0_xattn_all.items() if k in ('Wq', 'Wkv', 'Wout')}
    del _L0_xattn_all

    def _L0_ffn_setup():
        import jax, jax.numpy as jnp
        import numpy as np
        QK_SCALE = 10.0
        NEG_INF = -1000000000.0

        def layernorm(x, g, b, eps=1e-05):
            mu = jnp.mean(x, axis=-1, keepdims=True)
            var = jnp.var(x, axis=-1, keepdims=True)
            return (x - mu) * jax.lax.rsqrt(var + eps) * g + b

        def l2norm(x, eps=1e-12):
            return x / jnp.sqrt(jnp.sum(x * x, axis=-1, keepdims=True) + eps)
        key = jax.random.key(seed)
        ks = jax.random.split(key, 10)
        B, S, D, H, DH, E, FF = (2, 128, 128, 16, 64, 8, 512)
        sd = lambda fan: 1.0 / np.sqrt(fan)
        return {'x': jax.random.normal(ks[0], (B, S, D), jnp.float32), 'ln_g': jnp.ones((D,), jnp.float32), 'ln_b': jnp.zeros((D,), jnp.float32), 'Wq': jax.random.normal(ks[1], (D, H * DH), jnp.float32) * sd(D), 'Wk': jax.random.normal(ks[2], (D, H * DH), jnp.float32) * sd(D), 'Wv': jax.random.normal(ks[3], (D, H * DH), jnp.float32) * sd(D), 'q_scale': jnp.ones((H, 1, DH), jnp.float32), 'k_scale': jnp.ones((H, 1, DH), jnp.float32), 'Wo': jax.random.normal(ks[4], (H * DH, D), jnp.float32) * sd(H * DH), 'gate_w': jax.random.normal(ks[5], (D, E), jnp.float32) * sd(D), 'gate_b': jnp.zeros((E,), jnp.float32), 'w1': jax.random.normal(ks[6], (E, D, FF), jnp.float32) * sd(D), 'b1': jnp.zeros((E, FF), jnp.float32), 'w2': jax.random.normal(ks[7], (E, FF, D), jnp.float32) * sd(FF), 'b2': jnp.zeros((E, D), jnp.float32)}
    _L0_ffn_all = _L0_ffn_setup()
    _L0_ffn_in = {k: v for k, v in _L0_ffn_all.items() if k in ('ln_g', 'ln_b', 'Wq', 'Wk', 'Wv', 'q_scale', 'k_scale', 'Wo', 'gate_w', 'gate_b', 'w1', 'b1', 'w2', 'b2')}
    del _L0_ffn_all

    def _L1_attn_setup():
        import jax, jax.numpy as jnp
        import numpy as np
        B, T, D = (4, 256, 128)
        HID = 2 * D
        EPS = 1e-06

        def _rmsnorm(x, w):
            return x * jax.lax.rsqrt(jnp.mean(x * x, axis=-1, keepdims=True) + EPS) * w

        def _ema_scan(v, alpha):

            def step(prev, v_t):
                cur = alpha * v_t + (1.0 - alpha) * prev
                return (cur, cur)
            v_tm = jnp.swapaxes(v, 0, 1)
            _, out = jax.lax.scan(step, jnp.zeros(v.shape[::2], v.dtype), v_tm)
            return jnp.swapaxes(out, 0, 1)

        def _delta_scan(q, k, v, beta):

            def step(S, inp):
                q_t, k_t, v_t, b_t = inp
                Sk = jnp.einsum('bij,bj->bi', S, k_t)
                S = S + b_t[:, None, None] * (v_t - Sk)[:, :, None] * k_t[:, None, :]
                o_t = jnp.einsum('bij,bj->bi', S, q_t)
                return (S, o_t)
            tm = lambda a: jnp.swapaxes(a, 0, 1)
            S0 = jnp.zeros((q.shape[0], q.shape[2], q.shape[2]), q.dtype)
            _, out = jax.lax.scan(step, S0, (tm(q), tm(k), tm(v), tm(beta)))
            return jnp.swapaxes(out, 0, 1)
        key = jax.random.key(seed)
        ks = jax.random.split(key, 12)
        s = 0.02
        return {'x': jax.random.normal(ks[0], (B, T, D), jnp.float32), 'norm1_w': jnp.ones((D,), jnp.float32), 'Wq': jax.random.normal(ks[1], (D, D), jnp.float32) * s, 'Wk': jax.random.normal(ks[2], (D, D), jnp.float32) * s, 'Wv': jax.random.normal(ks[3], (D, D), jnp.float32) * s, 'beta_w': jax.random.normal(ks[4], (D, 1), jnp.float32) * s, 'beta_b': jnp.zeros((1,), jnp.float32), 'Wo': jax.random.normal(ks[5], (D, D), jnp.float32) * s, 'alpha_logit': jnp.full((D,), float(np.log(0.1 / 0.9)), jnp.float32), 'norm2_w': jnp.ones((D,), jnp.float32), 'w_gate': jax.random.normal(ks[6], (D, HID), jnp.float32) * s, 'w_up': jax.random.normal(ks[7], (D, HID), jnp.float32) * s, 'w_down': jax.random.normal(ks[8], (HID, D), jnp.float32) * s}
    _L1_attn_all = _L1_attn_setup()
    _L1_attn_in = {k: v for k, v in _L1_attn_all.items() if k in ('norm1_w', 'Wq', 'Wk', 'Wv', 'beta_w', 'beta_b', 'Wo', 'alpha_logit', 'norm2_w', 'w_gate', 'w_up', 'w_down')}
    del _L1_attn_all

    def _L1_xattn_setup():
        import jax, jax.numpy as jnp
        import numpy as np
        B, S, D = (8, 256, 128)
        key = jax.random.key(seed)
        kq, kk, kv = jax.random.split(key, 3)
        qm = jax.random.normal(kq, (B, S, D), dtype=jnp.float32)
        km = jax.random.normal(kk, (B, S, D), dtype=jnp.float32)
        vm = jax.random.normal(kv, (B, S, D), dtype=jnp.float32)
        return {'qm': qm, 'km': km, 'vm': vm}
    _L1_xattn_all = _L1_xattn_setup()
    _L1_xattn_in = {k: v for k, v in _L1_xattn_all.items() if k in ()}
    del _L1_xattn_all

    def _L1_ffn_setup():
        import jax, jax.numpy as jnp
        import numpy as np
        B, S, D, F, E, K = (2, 256, 128, 512, 8, 2)
        key = jax.random.key(seed)
        ks = jax.random.split(key, 5)
        x = jax.random.normal(ks[0], (B, S, D), dtype=jnp.float32)
        Wg = jax.random.normal(ks[1], (D, E), dtype=jnp.float32) * 0.02
        W1 = jax.random.normal(ks[2], (E, D, F), dtype=jnp.float32) * 0.02
        b1 = jnp.zeros((E, F), dtype=jnp.float32)
        W2 = jax.random.normal(ks[3], (E, F, D), dtype=jnp.float32) * 0.02
        b2 = jnp.zeros((E, D), dtype=jnp.float32)
        return {'x': x, 'Wg': Wg, 'W1': W1, 'b1': b1, 'W2': W2, 'b2': b2}
    _L1_ffn_all = _L1_ffn_setup()
    _L1_ffn_in = {k: v for k, v in _L1_ffn_all.items() if k in ('Wg', 'W1', 'b1', 'W2', 'b2')}
    del _L1_ffn_all

    def _L2_attn_setup():
        import jax, jax.numpy as jnp
        import numpy as np
        B, K, D = (8, 256, 128)
        INNER = 2 * D
        EPS = 1e-05

        def _silu(x):
            return x * jax.nn.sigmoid(x)
        key = jax.random.key(seed)
        k0, k1, k2, k3 = jax.random.split(key, 4)
        s_in = 1.0 / np.sqrt(D)
        s_inner = 1.0 / np.sqrt(INNER)
        return {'x': jax.random.normal(k0, (B, K, D), dtype=jnp.float32), 'w_norm': jnp.ones((D,), dtype=jnp.float32), 'W_in': (jax.random.normal(k1, (2 * INNER, D)) * s_in).astype(jnp.float32), 'W_dt': (jax.random.normal(k2, (INNER, INNER)) * s_inner).astype(jnp.float32), 'b_dt': jnp.zeros((INNER,), dtype=jnp.float32), 'W_out': (jax.random.normal(k3, (D, INNER)) * s_inner).astype(jnp.float32)}
    _L2_attn_all = _L2_attn_setup()
    _L2_attn_in = {k: v for k, v in _L2_attn_all.items() if k in ('w_norm', 'W_in', 'W_dt', 'b_dt', 'W_out')}
    del _L2_attn_all

    def _L2_xattn_setup():
        import jax, jax.numpy as jnp
        import numpy as np
        B, LQ, LK, D = (4, 256, 256, 128)
        H = 16
        HD = D // H

        def _split_heads(x):
            b, l, _ = x.shape
            return x.reshape(b, l, H, HD).transpose(0, 2, 1, 3)
        key = jax.random.key(seed)
        ks = jax.random.split(key, 10)
        s = 0.02
        return {'hidden_states': jax.random.normal(ks[0], (B, LQ, D), jnp.float32), 'context': jax.random.normal(ks[1], (B, LK, D), jnp.float32), 'attention_mask': jax.random.randint(ks[2], (B, LK), 0, 2, jnp.int32), 'q_w': jax.random.normal(ks[3], (D, D), jnp.float32) * s, 'q_b': jnp.zeros((D,), jnp.float32), 'k_w': jax.random.normal(ks[4], (D, D), jnp.float32) * s, 'k_b': jnp.zeros((D,), jnp.float32), 'v_w': jax.random.normal(ks[5], (D, D), jnp.float32) * s, 'v_b': jnp.zeros((D,), jnp.float32)}
    _L2_xattn_all = _L2_xattn_setup()
    _L2_xattn_in = {k: v for k, v in _L2_xattn_all.items() if k in ('q_w', 'q_b', 'k_w', 'k_b', 'v_w', 'v_b')}
    del _L2_xattn_all

    def _L2_ffn_setup():
        import jax, jax.numpy as jnp
        import numpy as np
        IN_FEATURES = 128
        ACT_BITS = 4

        def _hadamard(size: int) -> np.ndarray:
            h = np.array([[1.0]], dtype=np.float64)
            while h.shape[0] < size:
                h = np.block([[h, h], [h, -h]])
            return (h / np.sqrt(size)).astype(np.float32)

        def _quantize_activations(x, bits=ACT_BITS):
            pos = 2 ** (bits - 1) - 1
            neg = 2 ** (bits - 1)
            scale = jnp.clip(jnp.max(jnp.abs(jax.lax.stop_gradient(x)), axis=-1, keepdims=True), 1e-05) / pos
            q = jnp.clip(jnp.round(x / scale), -neg, pos) * scale
            return x + jax.lax.stop_gradient(q - x)

        def _ternary_quantize_ste(w):
            scale = jnp.clip(jnp.mean(jnp.abs(jax.lax.stop_gradient(w)), axis=1, keepdims=True), 1e-05)
            n = w / scale
            tern = jnp.where(n > 0.5, 1.0, jnp.where(n < -0.5, -1.0, 0.0))
            q = tern * scale
            return w + jax.lax.stop_gradient(q - w)
        key = jax.random.key(seed)
        k1, k2 = jax.random.split(key)
        x = jax.random.normal(k1, (8, 1024, IN_FEATURES), dtype=jnp.float32)
        bound = 1.0 / np.sqrt(IN_FEATURES)
        weight = jax.random.uniform(k2, (128, IN_FEATURES), dtype=jnp.float32, minval=-bound, maxval=bound)
        return {'x': x, 'weight': weight}
    _L2_ffn_all = _L2_ffn_setup()
    _L2_ffn_in = {k: v for k, v in _L2_ffn_all.items() if k in ('weight',)}
    del _L2_ffn_all

    def _L3_attn_setup():
        import jax, jax.numpy as jnp
        import numpy as np
        EPS = 1e-05

        def _forward(x, time_decay, time_first, W_key, W_value, W_output, W_shift, shift_gate, ln_w, ln_b):
            B, T, D = x.shape
            S = time_decay.shape[0]
            shift_len = max(1, int(T * 0.5))
            x_cat = jnp.concatenate([x[:, shift_len:], x[:, :-shift_len]], axis=1)
            gate = jax.nn.sigmoid(shift_gate)
            x_shift = jnp.einsum('btd,ed->bte', x_cat, W_shift) * gate + x * (1.0 - gate)
            mu = jnp.mean(x_shift, axis=-1, keepdims=True)
            var = jnp.mean(jnp.square(x_shift - mu), axis=-1, keepdims=True)
            xn = (x_shift - mu) * jax.lax.rsqrt(var + EPS) * ln_w + ln_b
            k = jnp.einsum('btd,sd->bts', xn, W_key)
            v = jnp.einsum('btd,sd->bts', xn, W_value)
            wkv = jnp.exp(-jnp.exp(time_first) * jax.nn.sigmoid(k)) * v
            w = jnp.exp(time_decay)

            def step(state, wkv_t):
                state = state * w + wkv_t
                return (state, state)
            init = jnp.zeros((B, S), dtype=x.dtype)
            last_state, states = jax.lax.scan(step, init, jnp.swapaxes(wkv, 0, 1))
            states = jnp.swapaxes(states, 0, 1)
            output = jnp.einsum('bts,ds->btd', states, W_output)
            return (output, last_state)

        def _reference_tuple_inner(x, time_decay, time_first, W_key, W_value, W_output, W_shift, shift_gate, ln_w, ln_b):
            out, last_state = _forward(x, time_decay, time_first, W_key, W_value, W_output, W_shift, shift_gate, ln_w, ln_b)
            return (out, jax.lax.stop_gradient(last_state))
        key = jax.random.key(seed)
        ks = jax.random.split(key, 8)
        B, T, D, S = (8, 512, 128, 64)
        return {'x': jax.random.normal(ks[0], (B, T, D), dtype=jnp.float32), 'time_decay': jax.random.normal(ks[1], (S,), dtype=jnp.float32) * 0.1 - 0.5, 'time_first': jax.random.normal(ks[2], (S,), dtype=jnp.float32) * 0.1, 'W_key': jax.random.normal(ks[3], (S, D), dtype=jnp.float32) * 0.02, 'W_value': jax.random.normal(ks[4], (S, D), dtype=jnp.float32) * 0.02, 'W_output': jax.random.normal(ks[5], (D, S), dtype=jnp.float32) * 0.02, 'W_shift': jax.random.normal(ks[6], (D, D), dtype=jnp.float32) * 0.02, 'shift_gate': jnp.ones((D,), dtype=jnp.float32), 'ln_w': jnp.ones((D,), dtype=jnp.float32), 'ln_b': jnp.zeros((D,), dtype=jnp.float32)}
    _L3_attn_all = _L3_attn_setup()
    _L3_attn_in = {k: v for k, v in _L3_attn_all.items() if k in ('time_decay', 'time_first', 'W_key', 'W_value', 'W_output', 'W_shift', 'shift_gate', 'ln_w', 'ln_b')}
    del _L3_attn_all

    def _L3_xattn_setup():
        import jax, jax.numpy as jnp
        import numpy as np
        H = 128
        NH = 16
        HD = H // NH
        key = jax.random.key(seed)
        ks = jax.random.split(key, 12)
        inp = {'query': jax.random.normal(ks[0], (4, 128, H), dtype=jnp.float32), 'key': jax.random.normal(ks[1], (4, 256, H), dtype=jnp.float32), 'value': jax.random.normal(ks[2], (4, 256, H), dtype=jnp.float32), 'key_padding_mask': jax.random.randint(ks[3], (4, 256), 0, 2, dtype=jnp.int32), 'Wq': jax.random.normal(ks[4], (H, H), dtype=jnp.float32) * (1.0 / np.sqrt(H)), 'bq': jnp.zeros((H,), dtype=jnp.float32), 'Wk': jax.random.normal(ks[5], (H, H), dtype=jnp.float32) * (1.0 / np.sqrt(H)), 'bk': jnp.zeros((H,), dtype=jnp.float32), 'Wv': jax.random.normal(ks[6], (H, H), dtype=jnp.float32) * (1.0 / np.sqrt(H)), 'bv': jnp.zeros((H,), dtype=jnp.float32), 'Wo': jax.random.normal(ks[7], (H, H), dtype=jnp.float32) * (1.0 / np.sqrt(H)), 'bo': jnp.zeros((H,), dtype=jnp.float32)}
        return inp
    _L3_xattn_all = _L3_xattn_setup()
    _L3_xattn_in = {k: v for k, v in _L3_xattn_all.items() if k in ('Wq', 'bq', 'Wk', 'bk', 'Wv', 'bv', 'Wo', 'bo')}
    del _L3_xattn_all

    def _L3_ffn_setup():
        import jax, jax.numpy as jnp
        import numpy as np
        TOP_K = 2
        NUM_EXPERTS = 8
        key = jax.random.key(seed)
        ks = jax.random.split(key, 8)
        h, d, ds, E = (128, 64, 128, NUM_EXPERTS)
        s = 1.0 / np.sqrt(h)
        return {'x': jax.random.normal(ks[0], (2, 256, h), jnp.float32), 'router': jax.random.normal(ks[1], (h, E), jnp.float32) * s, 'experts_gate': jax.random.normal(ks[2], (E, h, d), jnp.float32) * s, 'experts_up': jax.random.normal(ks[3], (E, h, d), jnp.float32) * s, 'experts_down': jax.random.normal(ks[4], (E, d, h), jnp.float32) * (1.0 / np.sqrt(d)), 'shared_gate': jax.random.normal(ks[5], (h, ds), jnp.float32) * s, 'shared_up': jax.random.normal(ks[6], (h, ds), jnp.float32) * s, 'shared_down': jax.random.normal(ks[7], (ds, h), jnp.float32) * (1.0 / np.sqrt(ds))}
    _L3_ffn_all = _L3_ffn_setup()
    _L3_ffn_in = {k: v for k, v in _L3_ffn_all.items() if k in ('router', 'experts_gate', 'experts_up', 'experts_down', 'shared_gate', 'shared_up', 'shared_down')}
    del _L3_ffn_all
    return {'x': x, 'ctx_1024': ctx_1024, 'mask_BxS2_ik0': mask_BxS2_ik0, 'L0_attn_in_proj_w': _L0_attn_in['in_proj_w'], 'L0_attn_in_proj_b': _L0_attn_in['in_proj_b'], 'L0_attn_out_w': _L0_attn_in['out_w'], 'L0_attn_out_b': _L0_attn_in['out_b'], 'L0_attn_lin1_w': _L0_attn_in['lin1_w'], 'L0_attn_lin1_b': _L0_attn_in['lin1_b'], 'L0_attn_lin2_w': _L0_attn_in['lin2_w'], 'L0_attn_lin2_b': _L0_attn_in['lin2_b'], 'L0_attn_ln1_g': _L0_attn_in['ln1_g'], 'L0_attn_ln1_b': _L0_attn_in['ln1_b'], 'L0_attn_ln2_g': _L0_attn_in['ln2_g'], 'L0_attn_ln2_b': _L0_attn_in['ln2_b'], 'L0_xattn_Wq': _L0_xattn_in['Wq'], 'L0_xattn_Wkv': _L0_xattn_in['Wkv'], 'L0_xattn_Wout': _L0_xattn_in['Wout'], 'L0_ffn_ln_g': _L0_ffn_in['ln_g'], 'L0_ffn_ln_b': _L0_ffn_in['ln_b'], 'L0_ffn_Wq': _L0_ffn_in['Wq'], 'L0_ffn_Wk': _L0_ffn_in['Wk'], 'L0_ffn_Wv': _L0_ffn_in['Wv'], 'L0_ffn_q_scale': _L0_ffn_in['q_scale'], 'L0_ffn_k_scale': _L0_ffn_in['k_scale'], 'L0_ffn_Wo': _L0_ffn_in['Wo'], 'L0_ffn_gate_w': _L0_ffn_in['gate_w'], 'L0_ffn_gate_b': _L0_ffn_in['gate_b'], 'L0_ffn_w1': _L0_ffn_in['w1'], 'L0_ffn_b1': _L0_ffn_in['b1'], 'L0_ffn_w2': _L0_ffn_in['w2'], 'L0_ffn_b2': _L0_ffn_in['b2'], 'L1_attn_norm1_w': _L1_attn_in['norm1_w'], 'L1_attn_Wq': _L1_attn_in['Wq'], 'L1_attn_Wk': _L1_attn_in['Wk'], 'L1_attn_Wv': _L1_attn_in['Wv'], 'L1_attn_beta_w': _L1_attn_in['beta_w'], 'L1_attn_beta_b': _L1_attn_in['beta_b'], 'L1_attn_Wo': _L1_attn_in['Wo'], 'L1_attn_alpha_logit': _L1_attn_in['alpha_logit'], 'L1_attn_norm2_w': _L1_attn_in['norm2_w'], 'L1_attn_w_gate': _L1_attn_in['w_gate'], 'L1_attn_w_up': _L1_attn_in['w_up'], 'L1_attn_w_down': _L1_attn_in['w_down'], 'L1_ffn_Wg': _L1_ffn_in['Wg'], 'L1_ffn_W1': _L1_ffn_in['W1'], 'L1_ffn_b1': _L1_ffn_in['b1'], 'L1_ffn_W2': _L1_ffn_in['W2'], 'L1_ffn_b2': _L1_ffn_in['b2'], 'L2_attn_w_norm': _L2_attn_in['w_norm'], 'L2_attn_W_in': _L2_attn_in['W_in'], 'L2_attn_W_dt': _L2_attn_in['W_dt'], 'L2_attn_b_dt': _L2_attn_in['b_dt'], 'L2_attn_W_out': _L2_attn_in['W_out'], 'L2_xattn_q_w': _L2_xattn_in['q_w'], 'L2_xattn_q_b': _L2_xattn_in['q_b'], 'L2_xattn_k_w': _L2_xattn_in['k_w'], 'L2_xattn_k_b': _L2_xattn_in['k_b'], 'L2_xattn_v_w': _L2_xattn_in['v_w'], 'L2_xattn_v_b': _L2_xattn_in['v_b'], 'L2_ffn_weight': _L2_ffn_in['weight'], 'L3_attn_time_decay': _L3_attn_in['time_decay'], 'L3_attn_time_first': _L3_attn_in['time_first'], 'L3_attn_W_key': _L3_attn_in['W_key'], 'L3_attn_W_value': _L3_attn_in['W_value'], 'L3_attn_W_output': _L3_attn_in['W_output'], 'L3_attn_W_shift': _L3_attn_in['W_shift'], 'L3_attn_shift_gate': _L3_attn_in['shift_gate'], 'L3_attn_ln_w': _L3_attn_in['ln_w'], 'L3_attn_ln_b': _L3_attn_in['ln_b'], 'L3_xattn_Wq': _L3_xattn_in['Wq'], 'L3_xattn_bq': _L3_xattn_in['bq'], 'L3_xattn_Wk': _L3_xattn_in['Wk'], 'L3_xattn_bk': _L3_xattn_in['bk'], 'L3_xattn_Wv': _L3_xattn_in['Wv'], 'L3_xattn_bv': _L3_xattn_in['bv'], 'L3_xattn_Wo': _L3_xattn_in['Wo'], 'L3_xattn_bo': _L3_xattn_in['bo'], 'L3_ffn_router': _L3_ffn_in['router'], 'L3_ffn_experts_gate': _L3_ffn_in['experts_gate'], 'L3_ffn_experts_up': _L3_ffn_in['experts_up'], 'L3_ffn_experts_down': _L3_ffn_in['experts_down'], 'L3_ffn_shared_gate': _L3_ffn_in['shared_gate'], 'L3_ffn_shared_up': _L3_ffn_in['shared_up'], 'L3_ffn_shared_down': _L3_ffn_in['shared_down']}

def reference(x, ctx_1024, mask_BxS2_ik0, L0_attn_in_proj_w, L0_attn_in_proj_b, L0_attn_out_w, L0_attn_out_b, L0_attn_lin1_w, L0_attn_lin1_b, L0_attn_lin2_w, L0_attn_lin2_b, L0_attn_ln1_g, L0_attn_ln1_b, L0_attn_ln2_g, L0_attn_ln2_b, L0_xattn_Wq, L0_xattn_Wkv, L0_xattn_Wout, L0_ffn_ln_g, L0_ffn_ln_b, L0_ffn_Wq, L0_ffn_Wk, L0_ffn_Wv, L0_ffn_q_scale, L0_ffn_k_scale, L0_ffn_Wo, L0_ffn_gate_w, L0_ffn_gate_b, L0_ffn_w1, L0_ffn_b1, L0_ffn_w2, L0_ffn_b2, L1_attn_norm1_w, L1_attn_Wq, L1_attn_Wk, L1_attn_Wv, L1_attn_beta_w, L1_attn_beta_b, L1_attn_Wo, L1_attn_alpha_logit, L1_attn_norm2_w, L1_attn_w_gate, L1_attn_w_up, L1_attn_w_down, L1_ffn_Wg, L1_ffn_W1, L1_ffn_b1, L1_ffn_W2, L1_ffn_b2, L2_attn_w_norm, L2_attn_W_in, L2_attn_W_dt, L2_attn_b_dt, L2_attn_W_out, L2_xattn_q_w, L2_xattn_q_b, L2_xattn_k_w, L2_xattn_k_b, L2_xattn_v_w, L2_xattn_v_b, L2_ffn_weight, L3_attn_time_decay, L3_attn_time_first, L3_attn_W_key, L3_attn_W_value, L3_attn_W_output, L3_attn_W_shift, L3_attn_shift_gate, L3_attn_ln_w, L3_attn_ln_b, L3_xattn_Wq, L3_xattn_bq, L3_xattn_Wk, L3_xattn_bk, L3_xattn_Wv, L3_xattn_bv, L3_xattn_Wo, L3_xattn_bo, L3_ffn_router, L3_ffn_experts_gate, L3_ffn_experts_up, L3_ffn_experts_down, L3_ffn_shared_gate, L3_ffn_shared_up, L3_ffn_shared_down):
    import jax
    import jax.numpy as jnp

    def _L0_attn_ref(src, in_proj_w, in_proj_b, out_w, out_b, lin1_w, lin1_b, lin2_w, lin2_b, ln1_g, ln1_b, ln2_g, ln2_b):
        import math
        import jax, jax.numpy as jnp
        import numpy as np
        D_MODEL = 128
        N_HEADS = 16
        HEAD_DIM = D_MODEL // N_HEADS
        D_FF = 512
        LN_EPS = 1e-05

        def _layer_norm(x, g, b):
            mu = jnp.mean(x, axis=-1, keepdims=True)
            var = jnp.var(x, axis=-1, keepdims=True)
            return (x - mu) * jax.lax.rsqrt(var + LN_EPS) * g + b
        B, S, d = src.shape
        q = src @ in_proj_w[:d].T + in_proj_b[:d]
        kv = src @ in_proj_w[d:].T + in_proj_b[d:]
        q = q.reshape(B, S, N_HEADS, HEAD_DIM)
        kv = kv.reshape(B, S, 2, N_HEADS, HEAD_DIM)
        k, v = (kv[:, :, 0], kv[:, :, 1])
        softmax_scale = 1.0 / math.sqrt(HEAD_DIM)
        scores = jnp.einsum('bthd,bshd->bhts', q, k) * softmax_scale
        attention = jax.nn.softmax(scores, axis=-2)
        post = jnp.einsum('bhts,bshd->bthd', attention, v)
        post = jax.nn.gelu(post, approximate=False)
        post = post / math.sqrt(S)
        attn_out = post.reshape(B, S, d) @ out_w.T + out_b
        x = _layer_norm(src + attn_out, ln1_g, ln1_b)
        ff = jax.nn.gelu(x @ lin1_w.T + lin1_b, approximate=False) @ lin2_w.T + lin2_b
        return _layer_norm(x + ff, ln2_g, ln2_b)

    def _L0_xattn_ref(x, xmel, Wq, Wkv, Wout):
        import jax, jax.numpy as jnp
        import numpy as np
        DIM = 128
        NHEADS = 8
        HEAD_DIM = DIM // NHEADS
        ROPE_BASE = 10000.0

        def _rope(t, positions):
            d = t.shape[-1]
            inv_freq = 1.0 / ROPE_BASE ** (jnp.arange(0, d, 2, dtype=jnp.float32) / d)
            freqs = positions[:, None].astype(jnp.float32) * inv_freq
            emb = jnp.concatenate([freqs, freqs], axis=-1)
            cos = jnp.cos(emb)[None, :, None, :].astype(t.dtype)
            sin = jnp.sin(emb)[None, :, None, :].astype(t.dtype)
            t1, t2 = jnp.split(t, 2, axis=-1)
            rot = jnp.concatenate([-t2, t1], axis=-1)
            return t * cos + rot * sin
        B, T, C = x.shape
        S = xmel.shape[1]
        H, D = (NHEADS, C // NHEADS)
        q = (x @ Wq.T).reshape(B, T, H, D)
        kv = (xmel @ Wkv.T).reshape(B, S, 2, H, D)
        q = _rope(q, jnp.arange(T))
        k = _rope(kv[:, :, 0], jnp.arange(S))
        v = kv[:, :, 1]
        scale = (C // H) ** (-0.25)
        q = q * scale
        k = k * scale
        scores = jnp.einsum('bthd,bshd->bhts', q, k)
        attn = jax.nn.softmax(scores, axis=-1)
        out = jnp.einsum('bhts,bshd->bthd', attn, v)
        out = out.reshape(B, T, C)
        return out @ Wout.T

    def _L0_ffn_ref(x, ln_g, ln_b, Wq, Wk, Wv, q_scale, k_scale, Wo, gate_w, gate_b, w1, b1, w2, b2):
        import jax, jax.numpy as jnp
        import numpy as np
        QK_SCALE = 10.0
        NEG_INF = -1000000000.0

        def layernorm(x, g, b, eps=1e-05):
            mu = jnp.mean(x, axis=-1, keepdims=True)
            var = jnp.var(x, axis=-1, keepdims=True)
            return (x - mu) * jax.lax.rsqrt(var + eps) * g + b

        def l2norm(x, eps=1e-12):
            return x / jnp.sqrt(jnp.sum(x * x, axis=-1, keepdims=True) + eps)
        B, S, D = x.shape
        H = q_scale.shape[0]
        DH = q_scale.shape[-1]
        h = layernorm(x, ln_g, ln_b)
        q = (h @ Wq).reshape(B, S, H, DH).transpose(0, 2, 1, 3)
        k = (h @ Wk).reshape(B, S, H, DH).transpose(0, 2, 1, 3)
        v = (h @ Wv).reshape(B, S, H, DH).transpose(0, 2, 1, 3)
        q = l2norm(q) * q_scale
        k = l2norm(k) * k_scale
        logits = jnp.einsum('bhid,bhjd->bhij', q, k) * QK_SCALE
        causal = jnp.tril(jnp.ones((S, S), bool))
        logits = jnp.where(causal, logits, NEG_INF)
        attn = jax.nn.softmax(logits, axis=-1)
        out = jnp.einsum('bhij,bhjd->bhid', attn, v)
        out = out.transpose(0, 2, 1, 3).reshape(B, S, H * DH) @ Wo
        h = layernorm(out, ln_g, ln_b)
        gate = jax.nn.softmax(h @ gate_w + gate_b, axis=-1)
        hid = jax.nn.gelu(jnp.einsum('bsd,edf->bsef', h, w1) + b1)
        exp_out = jnp.einsum('bsef,efd->bsed', hid, w2) + b2
        moe = jnp.einsum('bse,bsed->bsd', gate, exp_out)
        return layernorm(moe, ln_g, ln_b)

    def _L1_attn_ref(x, norm1_w, Wq, Wk, Wv, beta_w, beta_b, Wo, alpha_logit, norm2_w, w_gate, w_up, w_down):
        import jax, jax.numpy as jnp
        import numpy as np
        B, T, D = (4, 256, 128)
        HID = 2 * D
        EPS = 1e-06

        def _rmsnorm(x, w):
            return x * jax.lax.rsqrt(jnp.mean(x * x, axis=-1, keepdims=True) + EPS) * w

        def _ema_scan(v, alpha):

            def step(prev, v_t):
                cur = alpha * v_t + (1.0 - alpha) * prev
                return (cur, cur)
            v_tm = jnp.swapaxes(v, 0, 1)
            _, out = jax.lax.scan(step, jnp.zeros(v.shape[::2], v.dtype), v_tm)
            return jnp.swapaxes(out, 0, 1)

        def _delta_scan(q, k, v, beta):

            def step(S, inp):
                q_t, k_t, v_t, b_t = inp
                Sk = jnp.einsum('bij,bj->bi', S, k_t)
                S = S + b_t[:, None, None] * (v_t - Sk)[:, :, None] * k_t[:, None, :]
                o_t = jnp.einsum('bij,bj->bi', S, q_t)
                return (S, o_t)
            tm = lambda a: jnp.swapaxes(a, 0, 1)
            S0 = jnp.zeros((q.shape[0], q.shape[2], q.shape[2]), q.dtype)
            _, out = jax.lax.scan(step, S0, (tm(q), tm(k), tm(v), tm(beta)))
            return jnp.swapaxes(out, 0, 1)
        h = _rmsnorm(x, norm1_w)
        q = h @ Wq
        k = h @ Wk
        k = k / jnp.maximum(jnp.linalg.norm(k, axis=-1, keepdims=True), 1e-12)
        v = h @ Wv
        v = _ema_scan(v, jax.nn.sigmoid(alpha_logit))
        beta = jax.nn.sigmoid(h @ beta_w + beta_b)[..., 0]
        attn_out = _delta_scan(q, k, v, beta)
        x = x + attn_out @ Wo
        h2 = _rmsnorm(x, norm2_w)
        mlp = jax.nn.silu(h2 @ w_gate) * (h2 @ w_up) @ w_down
        return x + mlp

    def _L1_xattn_ref(qm, km, vm):
        import jax, jax.numpy as jnp
        import numpy as np
        B, S, D = (8, 256, 128)
        scale = 1.0 / jnp.sqrt(jnp.asarray(qm.shape[-1], dtype=qm.dtype))
        qkm = jnp.einsum('bqd,bkd->bqk', qm, km) * scale
        out = jnp.einsum('bqk,bkd->bqd', qkm, vm)
        return jax.nn.softmax(out, axis=-1)

    def _L1_ffn_ref(x, Wg, W1, b1, W2, b2):
        import jax, jax.numpy as jnp
        import numpy as np
        B, S, D, F, E, K = (2, 256, 128, 512, 8, 2)
        b, s, d = x.shape
        e = Wg.shape[1]
        T = b * s
        C = 2 * K * T // e
        xt = x.reshape(T, d)
        logits = xt.astype(jnp.float32) @ Wg.astype(jnp.float32)
        gates = jax.nn.softmax(logits, axis=-1)
        idx1 = jnp.argmax(gates, axis=-1)
        mask1 = jax.nn.one_hot(idx1, e, dtype=gates.dtype)
        gate1 = jnp.sum(gates * mask1, axis=-1)
        logits2 = jnp.where(mask1 > 0, -jnp.inf, logits)
        idx2 = jnp.argmax(logits2, axis=-1)
        mask2 = jax.nn.one_hot(idx2, e, dtype=gates.dtype)
        gate2 = jnp.sum(gates * mask2, axis=-1)
        denom = gate1 + gate2 + 1e-09
        w1 = gate1 / denom
        w2 = gate2 / denom
        p1 = jnp.cumsum(mask1, axis=0) - mask1
        pos1 = jnp.sum(p1 * mask1, axis=-1).astype(jnp.int32)
        off = jnp.sum(mask1, axis=0)
        p2 = jnp.cumsum(mask2, axis=0) - mask2 + off[None, :]
        pos2 = jnp.sum(p2 * mask2, axis=-1).astype(jnp.int32)
        keep1 = (pos1 < C).astype(xt.dtype)
        keep2 = (pos2 < C).astype(xt.dtype)
        pos1 = jnp.clip(pos1, 0, C - 1)
        pos2 = jnp.clip(pos2, 0, C - 1)
        xe = jnp.zeros((e, C, d), dtype=xt.dtype)
        xe = xe.at[idx1, pos1].add(xt * keep1[:, None])
        xe = xe.at[idx2, pos2].add(xt * keep2[:, None])
        h = jax.nn.gelu(jnp.einsum('ecd,edf->ecf', xe, W1) + b1[:, None, :], approximate=False)
        ye = jnp.einsum('ecf,efd->ecd', h, W2) + b2[:, None, :]
        out = ye[idx1, pos1] * (w1 * keep1)[:, None] + ye[idx2, pos2] * (w2 * keep2)[:, None]
        return out.reshape(b, s, d)

    def _L2_attn_ref(x, w_norm, W_in, W_dt, b_dt, W_out):
        import jax, jax.numpy as jnp
        import numpy as np
        B, K, D = (8, 256, 128)
        INNER = 2 * D
        EPS = 1e-05

        def _silu(x):
            return x * jax.nn.sigmoid(x)
        h = x * jax.lax.rsqrt(jnp.mean(x * x, axis=-1, keepdims=True) + EPS) * w_norm
        uv = jnp.einsum('bkd,ed->bke', h, W_in)
        u, z = (uv[..., :INNER], uv[..., INNER:])
        u = _silu(u)
        lam = jax.nn.sigmoid(jnp.einsum('bki,ji->bkj', u, W_dt) + b_dt)

        def step(s, inp):
            lam_t, u_t = inp
            s = lam_t * s + (1.0 - lam_t) * u_t
            return (s, s)
        lam_k = jnp.moveaxis(lam, 1, 0)
        u_k = jnp.moveaxis(u, 1, 0)
        s0 = jnp.zeros((x.shape[0], INNER), dtype=x.dtype)
        _, ys = jax.lax.scan(step, s0, (lam_k, u_k))
        s = jnp.moveaxis(ys, 0, 1)
        s = s * _silu(z)
        y = jnp.einsum('bki,di->bkd', s, W_out)
        return x + y

    def _L2_xattn_ref(hidden_states, context, attention_mask, q_w, q_b, k_w, k_b, v_w, v_b):
        import jax, jax.numpy as jnp
        import numpy as np
        B, LQ, LK, D = (4, 256, 256, 128)
        H = 16
        HD = D // H

        def _split_heads(x):
            b, l, _ = x.shape
            return x.reshape(b, l, H, HD).transpose(0, 2, 1, 3)
        q = _split_heads(hidden_states @ q_w.T + q_b)
        k = _split_heads(context @ k_w.T + k_b)
        v = _split_heads(context @ v_w.T + v_b)
        scores = jnp.einsum('bhqd,bhkd->bhqk', q, k) / jnp.sqrt(jnp.float32(HD))
        mask = (attention_mask > 0)[:, None, None, :]
        scores = jnp.where(mask, -jnp.inf, scores)
        probs = jax.nn.softmax(scores, axis=-1)
        ctx = jnp.einsum('bhqk,bhkd->bhqd', probs, v)
        ctx = ctx.transpose(0, 2, 1, 3).reshape(ctx.shape[0], ctx.shape[2], H * HD)
        return ctx

    def _L2_ffn_ref(x, weight):
        import jax, jax.numpy as jnp
        import numpy as np
        IN_FEATURES = 128
        ACT_BITS = 4

        def _hadamard(size: int) -> np.ndarray:
            h = np.array([[1.0]], dtype=np.float64)
            while h.shape[0] < size:
                h = np.block([[h, h], [h, -h]])
            return (h / np.sqrt(size)).astype(np.float32)

        def _quantize_activations(x, bits=ACT_BITS):
            pos = 2 ** (bits - 1) - 1
            neg = 2 ** (bits - 1)
            scale = jnp.clip(jnp.max(jnp.abs(jax.lax.stop_gradient(x)), axis=-1, keepdims=True), 1e-05) / pos
            q = jnp.clip(jnp.round(x / scale), -neg, pos) * scale
            return x + jax.lax.stop_gradient(q - x)

        def _ternary_quantize_ste(w):
            scale = jnp.clip(jnp.mean(jnp.abs(jax.lax.stop_gradient(w)), axis=1, keepdims=True), 1e-05)
            n = w / scale
            tern = jnp.where(n > 0.5, 1.0, jnp.where(n < -0.5, -1.0, 0.0))
            q = tern * scale
            return w + jax.lax.stop_gradient(q - w)
        H = jnp.asarray(_hadamard(IN_FEATURES))
        xh = x @ H
        xq = _quantize_activations(xh)
        wq = _ternary_quantize_ste(weight)
        return jnp.einsum('bsi,oi->bso', xq, wq)

    def _L3_attn_ref(x, time_decay, time_first, W_key, W_value, W_output, W_shift, shift_gate, ln_w, ln_b):
        import jax, jax.numpy as jnp
        import numpy as np
        EPS = 1e-05

        def _forward(x, time_decay, time_first, W_key, W_value, W_output, W_shift, shift_gate, ln_w, ln_b):
            B, T, D = x.shape
            S = time_decay.shape[0]
            shift_len = max(1, int(T * 0.5))
            x_cat = jnp.concatenate([x[:, shift_len:], x[:, :-shift_len]], axis=1)
            gate = jax.nn.sigmoid(shift_gate)
            x_shift = jnp.einsum('btd,ed->bte', x_cat, W_shift) * gate + x * (1.0 - gate)
            mu = jnp.mean(x_shift, axis=-1, keepdims=True)
            var = jnp.mean(jnp.square(x_shift - mu), axis=-1, keepdims=True)
            xn = (x_shift - mu) * jax.lax.rsqrt(var + EPS) * ln_w + ln_b
            k = jnp.einsum('btd,sd->bts', xn, W_key)
            v = jnp.einsum('btd,sd->bts', xn, W_value)
            wkv = jnp.exp(-jnp.exp(time_first) * jax.nn.sigmoid(k)) * v
            w = jnp.exp(time_decay)

            def step(state, wkv_t):
                state = state * w + wkv_t
                return (state, state)
            init = jnp.zeros((B, S), dtype=x.dtype)
            last_state, states = jax.lax.scan(step, init, jnp.swapaxes(wkv, 0, 1))
            states = jnp.swapaxes(states, 0, 1)
            output = jnp.einsum('bts,ds->btd', states, W_output)
            return (output, last_state)

        def _reference_tuple_inner(x, time_decay, time_first, W_key, W_value, W_output, W_shift, shift_gate, ln_w, ln_b):
            out, last_state = _forward(x, time_decay, time_first, W_key, W_value, W_output, W_shift, shift_gate, ln_w, ln_b)
            return (out, jax.lax.stop_gradient(last_state))
        return _reference_tuple_inner(x, time_decay, time_first, W_key, W_value, W_output, W_shift, shift_gate, ln_w, ln_b)[0]

    def _L3_xattn_ref(query, key, value, key_padding_mask, Wq, bq, Wk, bk, Wv, bv, Wo, bo):
        import jax, jax.numpy as jnp
        import numpy as np
        H = 128
        NH = 16
        HD = H // NH
        B, Sq, _ = query.shape
        Sk = key.shape[1]
        scaling = HD ** (-0.5)
        q = (query @ Wq + bq).reshape(B, Sq, NH, HD).transpose(0, 2, 1, 3)
        k = (key @ Wk + bk).reshape(B, Sk, NH, HD).transpose(0, 2, 1, 3)
        v = (value @ Wv + bv).reshape(B, Sk, NH, HD).transpose(0, 2, 1, 3)
        scores = jnp.einsum('bhqd,bhkd->bhqk', q, k) * scaling
        scores = jnp.where((key_padding_mask == 0)[:, None, None, :], -jnp.inf, scores)
        attn = jax.nn.softmax(scores, axis=-1)
        out = jnp.einsum('bhqk,bhkd->bhqd', attn, v)
        out = out.transpose(0, 2, 1, 3).reshape(B, Sq, H)
        return out @ Wo + bo

    def _L3_ffn_ref(x, router, experts_gate, experts_up, experts_down, shared_gate, shared_up, shared_down):
        import jax, jax.numpy as jnp
        import numpy as np
        TOP_K = 2
        NUM_EXPERTS = 8
        b, s, h = x.shape
        E = router.shape[1]
        shared_act = jax.nn.silu(jnp.einsum('bsh,hd->bsd', x, shared_gate))
        shared_up_out = jnp.einsum('bsh,hd->bsd', x, shared_up)
        shared_out = jnp.einsum('bsd,dh->bsh', shared_act * shared_up_out, shared_down)
        router_probs = jax.nn.softmax(jnp.einsum('bsh,he->bse', x, router), axis=-1)
        topk_probs, topk_idx = jax.lax.top_k(router_probs, TOP_K)
        coef = jnp.sum(jax.nn.one_hot(topk_idx, E, dtype=x.dtype) * topk_probs[..., None], axis=2)
        coef = coef.reshape(b * s, E)
        x_flat = x.reshape(b * s, h)
        gate = jnp.einsum('th,ehd->etd', x_flat, experts_gate)
        up = jnp.einsum('th,ehd->etd', x_flat, experts_up)
        expert_out = jnp.einsum('etd,edh->eth', jax.nn.silu(gate) * up, experts_down)
        routed = jnp.einsum('eth,te->th', expert_out, coef)
        return routed.reshape(b, s, h) + shared_out
    x = x + _L0_attn_ref(_layernorm(x, axis=-1), L0_attn_in_proj_w, L0_attn_in_proj_b, L0_attn_out_w, L0_attn_out_b, L0_attn_lin1_w, L0_attn_lin1_b, L0_attn_lin2_w, L0_attn_lin2_b, L0_attn_ln1_g, L0_attn_ln1_b, L0_attn_ln2_g, L0_attn_ln2_b)
    x = x + _L0_xattn_ref(_layernorm(x, axis=-1), ctx_1024, L0_xattn_Wq, L0_xattn_Wkv, L0_xattn_Wout)
    x = x + _L0_ffn_ref(_layernorm(x, axis=-1), L0_ffn_ln_g, L0_ffn_ln_b, L0_ffn_Wq, L0_ffn_Wk, L0_ffn_Wv, L0_ffn_q_scale, L0_ffn_k_scale, L0_ffn_Wo, L0_ffn_gate_w, L0_ffn_gate_b, L0_ffn_w1, L0_ffn_b1, L0_ffn_w2, L0_ffn_b2)
    x = x + _L1_attn_ref(_layernorm(x, axis=-1), L1_attn_norm1_w, L1_attn_Wq, L1_attn_Wk, L1_attn_Wv, L1_attn_beta_w, L1_attn_beta_b, L1_attn_Wo, L1_attn_alpha_logit, L1_attn_norm2_w, L1_attn_w_gate, L1_attn_w_up, L1_attn_w_down)
    x = x + _L1_xattn_ref(_layernorm(x, axis=-1), ctx_1024, ctx_1024)
    x = x + _L1_ffn_ref(_layernorm(x, axis=-1), L1_ffn_Wg, L1_ffn_W1, L1_ffn_b1, L1_ffn_W2, L1_ffn_b2)
    x = x + _L2_attn_ref(_layernorm(x, axis=-1), L2_attn_w_norm, L2_attn_W_in, L2_attn_W_dt, L2_attn_b_dt, L2_attn_W_out)
    x = x + _L2_xattn_ref(_layernorm(x, axis=-1), ctx_1024, mask_BxS2_ik0, L2_xattn_q_w, L2_xattn_q_b, L2_xattn_k_w, L2_xattn_k_b, L2_xattn_v_w, L2_xattn_v_b)
    x = x + _L2_ffn_ref(_layernorm(x, axis=-1), L2_ffn_weight)
    x = x + _L3_attn_ref(_layernorm(x, axis=-1), L3_attn_time_decay, L3_attn_time_first, L3_attn_W_key, L3_attn_W_value, L3_attn_W_output, L3_attn_W_shift, L3_attn_shift_gate, L3_attn_ln_w, L3_attn_ln_b)
    x = x + _L3_xattn_ref(_layernorm(x, axis=-1), ctx_1024, ctx_1024, mask_BxS2_ik0, L3_xattn_Wq, L3_xattn_bq, L3_xattn_Wk, L3_xattn_bk, L3_xattn_Wv, L3_xattn_bv, L3_xattn_Wo, L3_xattn_bo)
    x = x + _L3_ffn_ref(_layernorm(x, axis=-1), L3_ffn_router, L3_ffn_experts_gate, L3_ffn_experts_up, L3_ffn_experts_down, L3_ffn_shared_gate, L3_ffn_shared_up, L3_ffn_shared_down)
    return x

_drawn_inputs = setup_inputs


def setup_inputs(seed=0):
    import zlib

    import numpy as np

    out = dict(_drawn_inputs(seed))
    spreads = {'L0_attn_in_proj_b': (0.0, 0.8),
     'L0_attn_out_b': (0.0, 0.1),
     'L0_attn_lin1_b': (0.0, 0.396),
     'L0_attn_lin2_b': (0.0, 0.1),
     'L0_attn_ln1_g': (1.0, 0.2),
     'L0_attn_ln1_b': (0.0, 0.1),
     'L0_attn_ln2_g': (1.0, 0.2),
     'L0_attn_ln2_b': (0.0, 0.1),
     'L0_ffn_ln_g': (1.0, 0.2),
     'L0_ffn_ln_b': (0.0, 0.1),
     'L0_ffn_q_scale': (1.0, 0.2),
     'L0_ffn_k_scale': (1.0, 0.2),
     'L0_ffn_gate_b': (0.0, 0.1),
     'L0_ffn_b1': (0.0, 0.1),
     'L0_ffn_b2': (0.0, 0.1),
     'L1_attn_norm1_w': (1.0, 0.6),
     'L1_attn_alpha_logit': (-2.1972246170043945, 0.6),
     'L1_attn_norm2_w': (1.0, 0.6),
     'L1_ffn_b1': (0.0, 0.8),
     'L1_ffn_b2': (0.0, 2.0),
     'L2_attn_w_norm': (1.0, 0.6),
     'L2_attn_b_dt': (0.0, 2.0),
     'L2_xattn_q_b': (0.0, 2.0),
     'L2_xattn_k_b': (0.0, 2.0),
     'L2_xattn_v_b': (0.0, 1.577),
     'L3_attn_shift_gate': (1.0, 0.6),
     'L3_attn_ln_w': (1.0, 0.6),
     'L3_attn_ln_b': (0.0, 0.8),
     'L3_xattn_bq': (0.0, 2.0),
     'L3_xattn_bk': (0.0, 2.0),
     'L3_xattn_bv': (0.0, 1.65),
     'L3_xattn_bo': (0.0, 1.545)}
    factors = {'L0_attn_in_proj_w': 8.0,
     'L0_attn_out_w': 8.0,
     'L1_attn_Wq': 8.0,
     'L1_attn_Wk': 8.0,
     'L1_attn_Wv': 8.0,
     'L1_attn_beta_w': 8.0,
     'L1_attn_Wo': 8.0,
     'L1_attn_w_gate': 8.0,
     'L1_attn_w_up': 8.0,
     'L1_attn_w_down': 8.0,
     'L1_ffn_W1': 4.435,
     'L1_ffn_W2': 4.045,
     'L2_xattn_q_w': 54.248,
     'L2_xattn_k_w': 50.657,
     'L3_attn_time_decay': 200.0,
     'L3_attn_time_first': 8.0,
     'L3_attn_W_key': 8.0,
     'L3_attn_W_value': 6.795,
     'L3_attn_W_output': 6.707,
     'L3_attn_W_shift': 8.0,
     'L2_attn_W_dt': 4.999,
     'L2_xattn_v_w': 5.183,
     'L3_xattn_Wq': 4.35,
     'L3_xattn_Wk': 3.854,
     'L3_ffn_router': 4.559,
     'L3_ffn_experts_gate': 4.492,
     'L3_ffn_experts_up': 4.125,
     'L3_ffn_experts_down': 4.273,
     'L3_ffn_shared_gate': 5.092,
     'L3_ffn_shared_up': 4.657,
     'L3_ffn_shared_down': 4.76}
    for name, (base, spread) in spreads.items():
        noise = np.random.default_rng([zlib.crc32(name.encode()), seed]).standard_normal(out[name].shape)
        drawn = base * np.exp(spread * noise) if base else spread * noise
        out[name] = jnp.asarray(drawn.astype(out[name].dtype))
    for name, factor in factors.items():
        out[name] = (out[name] * factor).astype(out[name].dtype)
    return out
```

```python
import concourse.bass as bass
from concourse import mybir
from contextlib import ExitStack
import math
import numpy as np

B, S, D = 8, 56, 128
T = B * S
SK = 1500
KP, KJ = 125, 12
E, F = 8, 512
FC = F // 128
TT, NT = 112, 4
SP2 = 64
ONE_ONE = float(np.array([1, 1], np.float16).view(np.float32)[0])
BIG = 60000.0

SMALL = [
    ("x", T),
    ("ident", 128), ("mean", 128), ("ones", 128), ("half", 128),
    ("fold", S), ("blk8", 16), ("blk16", 32), ("headmask", 16), ("causal", S),
    ("iota", 8), ("reset", T), ("inlow", TT), ("inup", TT), ("offlow", TT), ("upper", TT),
    ("hadamard", 128),
    ("l0a_q", 128), ("l0a_k", 128), ("l0a_v", 128), ("l0a_out", 128), ("l0a_w1", F), ("l0a_w2", F),
    ("l0x_q", 128), ("l0x_qr", 128), ("l0x_k", 128), ("l0x_kr", 128), ("l0x_v", 128), ("l0x_out", 128),
    ("l0f_gate", 8), ("l0f_b1", E * FC),
    ("l1a_q", 128), ("l1a_k", 128), ("l1a_v", 128), ("l1a_beta", 128), ("l1a_o", 128),
    ("l1a_gate", 256), ("l1a_up", 256), ("l1a_down", 256),
    ("l1f_g", 8), ("l1f_b1", E * FC),
    ("l2f_w", 128), ("l2x_k", 128), ("l3f_sd", 128), ("l3f_router", 8), ("l3x_o", 128),
    ("l0a_bq", 1), ("l0a_bk", 1), ("l0a_bout", 1), ("l0a_b1", FC), ("l0a_b2", 1),
    ("l0a_g1", 1), ("l0a_c1", 1), ("l0a_g2", 1), ("l0a_c2", 1),
    ("l0f_g", 1), ("l0f_c", 1), ("l0f_qs", 8), ("l0f_ks", 8),
    ("l1a_n1", 1), ("l1a_n2", 1), ("l1a_bb", 1), ("l1a_alpha", 1),
    ("l2a_n", 1), ("l2a_bdt", 2), ("l2x_bq", 1), ("l2x_bk", 1), ("l2x_bv", 1),
    ("l3a_decay", 1), ("l3a_first", 1), ("l3a_gate", 1), ("l3a_g", 1), ("l3a_c", 1),
    ("l3x_bq", 1), ("l3x_bk", 1), ("l3x_bv", 1), ("l3x_bo", 1),
    ("row_bv", 128), ("row_gb", 8), ("l0f_b2", 128), ("l1f_b2", 128),
]
LATE = [
    ("l2a_in", 512), ("l2a_dt", 512), ("l2a_out", 256), ("l2x_q", 128), ("l2x_v", 128),
    ("l3a_key", 64), ("l3a_value", 64), ("l3a_out", 128), ("l3a_shift", 128),
    ("l3x_q", 128), ("l3x_k", 128), ("l3x_v", 128),
    ("l3f_eg", 512), ("l3f_eu", 512), ("l3f_ed", 512), ("l3f_sg", 128), ("l3f_su", 128),
]
LATE_AT, _at = {}, 0
for _name, _n in LATE:
    LATE_AT[_name] = (_at, _n)
    _at += _n
assert _at == 4096
AT, NSMALL = {}, 0
for _name, _n in SMALL:
    AT[_name] = (NSMALL, _n)
    NSMALL += _n
BIG0 = [("wq", 1024), ("wk", 1024), ("wv", 1024), ("wo", 1024), ("w1", E * F), ("w2", E * F)]
NBIG = sum(n for _, n in BIG0)

XL = [
    dict(name="l0x", hd=16, G=4, R=32, K1=128, K2=128, halves=1, rope=True, scale=0.25, valid=0),
    dict(name="l2x", hd=8, G=8, R=16, K1=65, K2=97, halves=2, rope=False, scale=1 / math.sqrt(8), valid=1),
    dict(name="l3x", hd=8, G=8, R=16, K1=65, K2=97, halves=2, rope=False, scale=8 ** -0.5, valid=2),
]
MASKROW, SHIFTROW = 64, 96


def slots(cfg):
    two = cfg["halves"] == 2
    out = []
    for s in range(KJ):
        scores = [2 * s, 2 * s + 1] if two else [s]
        if two:
            maxima = [3 * (s - 1) + k for k in range(3)] if 1 <= s <= 8 else []
        else:
            maxima = [2 * (s - 3) + k for k in range(2)] if 3 <= s <= 8 else []
        other = []
        if s < 3:
            other = [("V", s)] + ([("F", 0)] if s == 0 else [])
        elif cfg["rope"] and s < 6:
            other = [("T", s - 3)]
        elif cfg["rope"] and s < 9:
            other = [("K", s - 6), ("R", s - 6)]
        elif cfg["rope"] and s == 9:
            other = [("G", 0)]
        elif s < 6:
            other = [("K", s - 3)]
        if s == 9:
            other = other + [("DG", 0)]
        out.append((scores, maxima, other))
    out.append(([], [], [("SH", c) for c in range(cfg["G"] // 4)]))
    return out


def short_banks(cfg):
    order = [use for _, _, other in slots(cfg) for use in other if use[0] != "DG"]
    return {use: (7, 2)[n % 2] for n, use in enumerate(order)}


class Count:

    def __init__(self, *per):
        self.per = per

    def at(self, L, b, k=0):
        return b * self.per[L] + (B * sum(self.per[:L]) + k)


UNITS = Count(KJ, 2 * KJ, 2 * KJ)
MAXES = Count(12, 24, 24)
ONE, THREE, SHIFTS = Count(1, 1, 1), Count(3, 3, 3), Count(1, 2, 2)
LAG = 3
KUSES = Count(6, 3, 3)


NORMS = [("l0a", 1), ("l0a_1", 1), ("l0a_2", 1), ("l0x", 1), ("l0f", 1), ("l0f_1", 1), ("l0f_2", 1), ("l0f_3", 1),
         ("l1a", 1), ("l1a_1", 0), ("l1a_2", 0), ("l1x", 1), ("l1f", 1), ("l2a", 1), ("l2a_1", 0), ("l2x", 1),
         ("l2f", 1), ("l3a", 1), ("l3a_1", 1), ("l3x", 1), ("l3f", 1)]
NORM_AT = {name: n + 1 for n, (name, _) in enumerate(NORMS)}
MEAN_AT = {name: sum(c for _, c in NORMS[:n + 1]) for n, (name, _) in enumerate(NORMS)}


def build(nc, small, big0, big1, ctx, mrow, mcol, rope, out, scratch):
    f32, f16, bf16 = mybir.dt.float32, mybir.dt.float16, mybir.dt.bfloat16
    i32, u32 = mybir.dt.int32, mybir.dt.uint32
    ALU, ACT, AX = mybir.AluOpType, mybir.ActivationFunctionType, mybir.AxisListType
    kscr, qscr, mscr, cscr = scratch
    es = ExitStack()
    with es:
        def sb(name, shape, dt=f32):
            return es.enter_context(nc.sbuf_tensor(name, shape, dt))

        made = {}

        def sem(name):
            if name not in made:
                made[name] = es.enter_context(nc.semaphore(name))
            return made[name]

        W = sb("W", [128, NSMALL])
        WB = sb("WB", [128, NBIG])

        def w(name, a=0, n=None, p=128, p0=0):
            o, m = LATE_AT[name] if name in LATE_AT else AT[name]
            return (WB if name in LATE_AT else W)[p0:p, o + a:o + a + (m - a if n is None else n)]

        BAT, _o = {}, 0
        for _n, _m in BIG0:
            BAT[_n] = _o
            _o += _m

        def wb(name, a, n):
            return WB[:, BAT[name] + a:BAT[name] + a + n]

        X = w("x")
        IDN = w("ident")
        Y = sb("Y", [128, T])
        Z = sb("Z", [128, T])
        XC = sb("XC", [128, T])
        SQ = sb("SQ", [128, T])
        RS = sb("RS", [128, T])
        KS = sb("KS", [128, 2, 12000 + 288], f16)
        KS32 = KS[:, :, :].rearrange("p a n -> p (a n)").bitcast(f32)
        R = sb("R", [128, 2 * KJ * D + 2 * SK + SK])
        CT = R[0:KP, 0:2 * KJ * D].rearrange("p (a j d) -> p a j d", a=2, j=KJ)
        KHL = R[:, 2 * KJ * D:2 * KJ * D + 2 * SK].bitcast(f16).rearrange(
            "p (a h n) -> p a h n", a=2, h=2)
        CTT = R[:, 2 * KJ * D + 2 * SK:]
        VA = sb("VA", [KP, 2, KJ * 264], f16)
        QS = sb("QS", [128, 2, 1024], f16)
        QH = sb("QH", [128, 2, T], f16)
        PH = sb("PH", [KP, 4, 8, SP2], f16)
        PL = sb("PL", [KP, 4, 8, SP2], f16)
        PR = (XC, SQ)
        MX = sb("MX", [128, 2, 24])
        MM = sb("MM", [128, 2, 8])
        DG = sb("DG", [128, 1024], f16)
        RD = sb("RD", [128, 2, 8])
        OM = sb("OM", [128, 2, 2, 128])
        VC = sb("VC", [KP, 2, KJ])
        VALID = sb("VALID", [KP, 3, B, KJ])
        AO = sb("AO", [128, 1 + B, S])
        GC = sb("GC", [128, B, 128])
        SEL96 = sb("SEL96", [128, 128], f16)
        ONE16 = sb("ONE16", [128, KP], f16)
        IDH = sb("IDH", [128, 128], f16)
        PS = es.enter_context(nc.psum_tensor("PS", [128, 8, 512], f32))

        def bank(n, cols=T, p=128):
            return PS[0:p, n, 0:cols]

        chains = {}

        def link(eng, name, ins):
            chains[name] = chains.get(name, 0) + 1
            ins.then_inc(sem(name), 1)
            eng.wait_ge(sem(name), chains[name])

        def one(i):
            return bass.ds(i, 1)

        def bc(ap, *shape):
            return ap.broadcast_to(list(shape))

        block = es.enter_context(nc.Block())
        V, A, G, PE = nc.vector, nc.scalar, nc.gpsimd, nc.tensor

        def mm(out_, l, r, start=True, stop=True, skip=False):
            return PE.matmul(out_, l, r, start=start, stop=stop, skip_group_check=skip)

        CLEAR = 1

        def norm_pe(pe, name, src, ready):
            if dict(NORMS)[name]:
                pe.wait_ge(*ready)
                mm(bank(0), w("mean"), src).then_inc(sem("mean_ready"), 1)
            pe.wait_ge(sem("square_ready"), NORM_AT[name])
            mm(bank(1), w("mean"), SQ[:, :]).then_inc(sem("var_ready"), 1)

        def ln_exp():
            A.preload_act_table_set("natural_log_exp_and_others")

        def norm_act(act, name, src, eps, ready=None):
            ln_exp()
            if dict(NORMS)[name]:
                act.wait_ge(sem("centred"), MEAN_AT[name])
                src = XC[:, :]
            else:
                act.wait_ge(*ready)
            A.activation(SQ[:, :], src, ACT.Square).then_inc(sem("square_ready"), 1)
            act.wait_ge(sem("var_ready"), NORM_AT[name])
            link(act, "act_chain", A.activation(RS[:, :], bank(1), ACT.Ln, bias=eps))
            A.activation(RS[:, :], RS[:, :], ACT.Exp, scale=-0.5).then_inc(sem("rstd_ready"), 1)

        def norm_dve(dve, name, src, dst, gain=None, shift=None):
            if dict(NORMS)[name]:
                dve.wait_ge(sem("mean_ready"), MEAN_AT[name])
                V.tensor_tensor(XC[:, :], src, bank(0), ALU.subtract).then_inc(sem("centred"), 1)
                src = XC[:, :]
            dve.wait_ge(sem("rstd_ready"), NORM_AT[name])
            if gain is None:
                V.tensor_tensor(dst, src, RS[:, :], ALU.mult).then_inc(sem("norm_ready"), 1)
            elif shift is None:
                V.scalar_tensor_tensor(dst, src, gain, RS[:, :], ALU.mult, ALU.mult).then_inc(sem("norm_ready"), 1)
            else:
                link(dve, "dve_chain", V.tensor_tensor(dst, src, RS[:, :], ALU.mult))
                V.tensor_scalar(dst, dst, gain, shift, ALU.mult, ALU.add).then_inc(sem("norm_ready"), 1)

        def normed(eng, name):
            eng.wait_ge(sem("norm_ready"), NORM_AT[name])

        def x_is(n):
            return sem("x_ready"), n + 1

        q0, k0, v0 = R[:, 0:T], R[:, T:2 * T], R[0:S, 2 * T:2 * T + 1024]
        QB = R[:, 1920:1920 + 1792].rearrange("p (a n) -> p a n", a=2)
        SM = R[:, 3712:3712 + 1792].rearrange("p (a n) -> p a n", a=2)
        VN = Z[0:S, 0:256].rearrange("p (a n) -> p a n", a=2)
        OG = R[0:S, 1920:1920 + 1024]
        H4 = R[:, 0:4 * T].rearrange("p (f t) -> p f t", f=FC)
        M16 = OM[0:S, 0, 0, 0:16]
        D16 = OM[0:S, 0, 0, 16:32]

        def l0a_pe(pe):
            norm_pe(pe, "l0a", X, x_is(0))
            normed(pe, "l0a")
            mm(bank(2), w("l0a_q"), Y[:, :]).then_inc(sem("l0a_proj"), 1)
            mm(bank(3), w("l0a_k"), Y[:, :]).then_inc(sem("l0a_proj"), 1)
            for b in range(B):
                dst = PS[0:S, 4 + b // 4, b % 4 * 128:b % 4 * 128 + 128]
                mm(dst, Y[:, b * S:(b + 1) * S], w("l0a_v"), True, False)
                last = mm(dst, w("ones", 0, S, 1), w("row_bv", 0, 128, 1), False, True)
            last.then_inc(sem("l0a_proj"), 1)

            def scores(b):
                pe.wait_ge(sem("l0a_qblk"), b + 1)
                pe.wait_ge(sem("l0a_kv"), 2)
                if b:
                    pe.wait_ge(sem("l0a_less"), b)
                for n in range(2):
                    last = mm(PS[0:S, 6 + n, 0:T], k0[:, b * S:(b + 1) * S], QB[:, b % 2, n * T:(n + 1) * T])
                last.then_inc(sem("l0a_scores"), 1)

            scores(0)
            for b in range(B):
                if b + 1 < B:
                    scores(b + 1)
                pe.wait_ge(sem("l0a_vn"), b + 1)
                for h in range(16):
                    last = mm(PS[0:S, 2 + b // 4, b % 4 * 128 + h * 8:b % 4 * 128 + h * 8 + 8],
                              SM[0:S, b % 2, h * S:(h + 1) * S], VN[:, b % 2, h * 8:h * 8 + 8])
                last.then_inc(sem("l0a_pv"), 1)
            pe.wait_ge(sem("l0a_gelu"), 2)
            for b in range(B):
                last = PE.transpose(PS[:, 4, b * S:(b + 1) * S], OG[:, b * 128:(b + 1) * 128], IDN[0:S, 0:S])
            last.then_inc(sem("l0a_ot"), 1)
            pe.wait_ge(sem("l0a_a"), 1)
            mm(bank(5), w("l0a_out"), R[:, 4000:4000 + T]).then_inc(sem("l0a_o"), 1)
            norm_pe(pe, "l0a_1", Z[:, :], (sem("l0a_z"), 1))
            normed(pe, "l0a_1")
            for f in range(FC):
                mm(bank((2, 3, 6, 7)[f]), w("l0a_w1", f * 128, 128), Y[:, :]).then_inc(sem("l0a_up"), 1)
            for f in range(FC):
                pe.wait_ge(sem("l0a_h"), f + 1)
                last = mm(bank(4), w("l0a_w2", f * 128, 128), H4[:, f, :], f == 0, f == FC - 1)
            last.then_inc(sem("l0a_down"), 1)
            norm_pe(pe, "l0a_2", Z[:, :], (sem("l0a_z"), 2))

        def l0a_act(act):
            norm_act(act, "l0a", X, 1e-5)
            act.wait_ge(sem("l0a_proj"), 2)
            A.activation(k0, bank(3), ACT.Identity, bias=w("l0a_bk")).then_inc(sem("l0a_kv"), 1)
            act.wait_ge(sem("l0a_proj"), 3)
            A.activation(v0.rearrange("p (a n) -> p a n", a=2), PS[0:S, 4:6, :], ACT.Copy).then_inc(sem("l0a_kv"), 1)
            for b in range(B):
                act.wait_ge(sem("l0a_less"), b + 1)
                A.activation(SM[0:S, b % 2, :], SM[0:S, b % 2, :], ACT.Exp).then_inc(sem("l0a_exp"), 1)
            act.wait_ge(sem("l0a_pv"), B)
            for n in range(2):
                A.activation(OG[:, n * 512:(n + 1) * 512], PS[0:S, 2 + n, :], ACT.Gelu).then_inc(sem("l0a_gelu"), 1)
            norm_act(act, "l0a_1", None, 1e-5)
            for f in range(FC):
                act.wait_ge(sem("l0a_up"), f + 1)
                A.activation(H4[:, f, :], bank((2, 3, 6, 7)[f]), ACT.Gelu, bias=w("l0a_b1", f, 1)).then_inc(sem("l0a_h"), 1)
            norm_act(act, "l0a_2", None, 1e-5)

        def l0a_pool(pool):
            pool.wait_ge(sem("l0a_q"), 1)
            for b in range(B):
                if b >= 2:
                    pool.wait_ge(sem("l0a_scores"), b - 1)
                G.tensor_tensor(QB[:, b % 2, :].rearrange("p (h t) -> p h t", h=16),
                                bc(q0[:, b * S:(b + 1) * S].unsqueeze(1), 128, 16, S),
                                bc(w("headmask").unsqueeze(2), 128, 16, S), ALU.mult).then_inc(sem("l0a_qblk"), 1)

        def l0a_dve(dve):
            norm_dve(dve, "l0a", X, Y[:, :])
            dve.wait_ge(sem("l0a_proj"), 1)
            V.tensor_scalar(q0, bank(2), w("l0a_bq"), 1 / math.sqrt(8), ALU.add, ALU.mult).then_inc(sem("l0a_q"), 1)

            def less(b):
                dve.wait_ge(sem("l0a_scores"), b + 1)
                ps = PS[0:S, 6:8, 0:T].rearrange("p a (h t) -> p a h t", h=8)
                link(dve, "dve_chain", V.tensor_reduce(M16.rearrange("p (a h) -> p a h", a=2), ps, AX.X, ALU.max))
                if b >= 2:
                    dve.wait_ge(sem("l0a_pv"), b - 1)
                V.tensor_tensor(SM[0:S, b % 2, :].rearrange("p (a h t) -> p a h t", a=2, h=8), ps,
                                bc(M16.rearrange("p (a h) -> p a h", a=2).unsqueeze(3), S, 2, 8, S),
                                ALU.subtract).then_inc(sem("l0a_less"), 1)

            less(0)
            for b in range(B):
                if b + 1 < B:
                    less(b + 1)
                dve.wait_ge(sem("l0a_exp"), b + 1)
                if b:
                    dve.wait_ge(sem("l0a_vn"), b)
                link(dve, "dve_chain", V.tensor_reduce(
                    D16, SM[0:S, b % 2, :].rearrange("p (h t) -> p h t", h=16), AX.X, ALU.add))
                link(dve, "dve_chain", V.reciprocal(D16, D16))
                dve.wait_ge(sem("l0a_kv"), 2)
                V.tensor_tensor(VN[:, b % 2, :].rearrange("p (h d) -> p h d", h=16),
                                v0[:, b * 128:(b + 1) * 128].rearrange("p (h d) -> p h d", h=16),
                                bc(D16.unsqueeze(2), S, 16, 8), ALU.mult).then_inc(sem("l0a_vn"), 1)
            dve.wait_ge(sem("l0a_ot"), 1)
            V.tensor_scalar(R[:, 4000:4000 + T], bank(4), 1 / math.sqrt(S), None, ALU.mult).then_inc(sem("l0a_a"), 1)
            dve.wait_ge(sem("l0a_o"), 1)
            V.scalar_tensor_tensor(Z[:, :], bank(5), w("l0a_bout"), Y[:, :], ALU.add, ALU.add).then_inc(sem("l0a_z"), 1)
            norm_dve(dve, "l0a_1", Z[:, :], Y[:, :], w("l0a_g1"), w("l0a_c1"))
            dve.wait_ge(sem("l0a_down"), 1)
            V.scalar_tensor_tensor(Z[:, :], bank(4), w("l0a_b2"), Y[:, :], ALU.add, ALU.add).then_inc(sem("l0a_z"), 1)
            norm_dve(dve, "l0a_2", Z[:, :], Z[:, :], w("l0a_g2"), w("l0a_c2"))
            normed(dve, "l0a_2")
            V.tensor_tensor(X, X, Z[:, :], ALU.add).then_inc(sem("x_ready"), 1)

        ROPE_K = KS[:, 0, 6144:6144 + 6000].bitcast(f32)
        ROPE_Q = sb("ROPE_Q", [128, 2, S])
        SR = sb("SR", [128, 2, 512], f16)
        KT = KS[:, 1, 6144:6144 + 6000].bitcast(f32).rearrange("p (c r n) -> p c r n", c=3, r=2)

        def later(i, u, k):
            return i + (u + k) // 2, (u + k) % 2

        def dma_at(L, i, per):
            return (i + 1) * (16 * per[L]) + 16 * 4 * sum(per[:L])

        OM_STEPS = Count(2, 2, 2)

        def folds(L, n):
            return L * (B + 1) + n

        CTX = R[:, 0:2 * SK].rearrange("p (a k) -> p a k", a=2)

        def features(L, u):
            return CTX[:, u, :] if L else CTT

        K_HALF = [(4, 5, 5), (0, 5, 5)]
        Q_DMAS, C_DMAS = (8, 8, 8), (1, 1, 1)

        def va(cfg, u):
            return VA[:, u, 0:KJ * cfg["G"] * (4 * cfg["hd"] + 1)].rearrange(
                "p (j g n) -> p j g n", j=KJ, g=cfg["G"])

        def ks(cfg, u, k=128):
            return KS[0:k, u, 0:cfg["G"] * SK].rearrange("p (g n) -> p g n", g=cfg["G"])

        def qs(cfg, u):
            return QS[:, u, 0:cfg["G"] * 128].rearrange("p (g h t) -> p g h t", g=cfg["G"], h=2)

        def steps(eng, L, step):
            step(-1, 0, -2, False, False, True)
            step(-1, 1, -1, False, True, True)
            with eng.Fori(0, 3) as i:
                for u in range(2):
                    step(i, u, i * 2 + u, True, True, True)
            step(3, 0, 6, True, True, False)
            step(3, 1, 7, True, False, False)

        def low_unit(eng, unit, L, b, m):
            eng.wait_ge(sem("e_ready"), UNITS.at(L, b, m + 1 + 3))
            unit.tensor_tensor(PL[:, m % 4, :, 0:S], PR[m % 2][0:KP, :].rearrange("p (h t) -> p h t", h=8),
                               PH[:, m % 4, :, 0:S], ALU.subtract).then_inc(sem("l_ready"), 1)

        def x_sp(sp, L):
            cfg = XL[L]
            sp.wait_ge(sem("qs_clear"), L + 1)
            sp.wait_ge(sem("q_split"), L + 1)
            sp.dma_start(qscr, QH[:, :, :]).then_inc(sem("q_out"), 16)
            sp.wait_ge(sem("q_out"), 16 * (L + 1))

            def stack_k(i, u, b, half):
                gs = cfg["G"] // cfg["halves"]
                g0 = half * gs
                done = sem(f"k_in{u}{half}")
                for n in range(4):
                    sp.dma_start(ks(cfg, u)[cfg["R"] * n:cfg["R"] * (n + 1), g0:g0 + gs, :],
                                 kscr[u, :, n % 2, :].rearrange("(g p) n -> p g n", p=cfg["R"])[:, g0:g0 + gs, :]
                                 ).then_inc(done, 16)
                if cfg["valid"]:
                    sp.dma_start(ks(cfg, u)[MASKROW:MASKROW + 1, g0:g0 + gs, :],
                                 bc(mscr[cfg["valid"] - 1, one(b), :].unsqueeze(1), 1, gs, SK)).then_inc(done, 16)

            def step(i, u, b, has_d, has_c, has_b):
                if has_b:
                    ic, uc = later(i, u, 2)
                    if L == 0:
                        if has_d:
                            sp.wait_ge(sem("t_ready"), THREE.at(L, b + 1))
                            sp.wait_ge(sem("g_ready"), ONE.at(L, b + 1))
                        sp.dma_start(CT[:, uc, :, :], ctx[one(b + 2)].rearrange("o (p j) d -> (o p) j d", j=KJ)
                                     ).then_inc(sem(f"ctx_in{uc}"), 16)
                    else:
                        if has_d:
                            sp.wait_ge(sem("v_ready"), THREE.at(L, b + 1))
                        sp.dma_start(CTX[:, uc, :], cscr[one(b + 2)].rearrange("o d k -> (o d) k")
                                     ).then_inc(sem(f"ctx_in{uc}"), 16)
                if has_c:
                    ic, uc = later(i, u, 1)
                    if has_d:
                        sp.wait_ge(sem("s_ready"), UNITS.at(L, b, CLEAR))
                    if cfg["halves"] == 2:
                        stack_k(ic, uc, b + 1, 1)
                    else:
                        sp.wait_ge(sem(f"k_out{uc}"), dma_at(L, ic, C_DMAS))
                        stack_k(ic, uc, b + 1, 0)
                    for h in range(2):
                        for n in range(4):
                            r0 = cfg["R"] * n + cfg["hd"] * h
                            src = qscr[:, n // 2, bass.ds((b + 1) * S, S)].rearrange(
                                "(g h p) t -> h p g t", h=2, p=cfg["hd"])[h]
                            sp.dma_start(qs(cfg, uc)[r0:r0 + cfg["hd"], :, h, 0:S], src
                                         ).then_inc(sem(f"q_in{uc}"), 16)
                if has_b:
                    ic, uc = later(i, u, 2)
                    if L == 0:
                        sp.wait_ge(sem("t_copied"), THREE.at(L, b + 3))
                        sp.dma_start(cscr[one(b + 2)].rearrange("o d k -> (o d) k"), CTT).then_inc(sem("ctt_out"), 16)
                    if cfg["rope"]:
                        sp.wait_ge(sem("k_split"), THREE.at(L, b + 3))
                    else:
                        sp.wait_ge(sem("k_free"), KUSES.at(L, b + 3))
                    if has_d:
                        for half in range(cfg["halves"]):
                            sp.wait_ge(sem(f"k_in{u}{half}"), dma_at(L, i, K_HALF[half]))
                    sp.dma_start(kscr[uc], KHL[:, uc, :, :]).then_inc(sem(f"k_out{uc}"), 16)
                    if cfg["halves"] == 2:
                        sp.wait_ge(sem(f"k_out{uc}"), dma_at(L, ic, C_DMAS))
                        if has_d:
                            sp.wait_ge(sem("s_ready"), UNITS.at(L, b, KJ + CLEAR))
                        stack_k(ic, uc, b + 2, 0)

            for b in range(-2, B - 1):
                step(b // 2, b % 2, b, b >= 0, b >= -1, b < B - 2)
            if L == 0:
                sp.wait_ge(sem("ctt_out"), 16 * B)

        def x_pe(pe, L):
            cfg = XL[L]
            nm, hd, banks = cfg["name"], cfg["hd"], short_banks(cfg)
            wide = 4 * hd + 1
            norm_pe(pe, nm, X, x_is((1, 7, 10)[L]))
            normed(pe, nm)
            mm(bank(2), w(nm + "_q"), Y[:, :]).then_inc(sem("q_proj"), 1)
            if cfg["rope"]:
                mm(bank(3), w(nm + "_qr"), Y[:, :]).then_inc(sem("q_proj"), 1)
            pe.wait_ge(sem("q_split"), L + 1)
            if L == 0:
                pe.wait_ge(sem("sel_ready"), 1)

            def step(i, u, b, has_d, has_c, has_b):
                i1, u1 = later(i, u, 1)
                i2, u2 = later(i, u, 2)
                before = {7: [], 2: []}
                if has_d:
                    before[7] = [(sem("sh_copied"), SHIFTS.at(L, b + 1))]
                    before[2] = [(sem("g_copied"), ONE.at(L, b + 2))] if cfg["rope"] and has_c else before[7][:]
                elif has_c:
                    before[7] = [(sem("k_free"), KUSES.at(L, 1))]
                    before[2] = [(sem("g_copied"), ONE.at(L, 1)) if cfg["rope"] else before[7][0]]

                def short(kind, c):
                    n = banks[kind, c]
                    for k in before[n]:
                        pe.wait_ge(*k)
                    if kind == "V":
                        if L == 0:
                            pe.wait_ge(sem("t_copied"), THREE.at(L, b + 2))
                        for k in range(4):
                            j = 4 * c + k
                            last = mm(PS[0:KP, n, k * 128:(k + 1) * 128], features(L, u1)[:, j * KP:(j + 1) * KP],
                                      w(nm + "_v"))
                        last.then_inc(sem("v_ready"), 1)
                        before[n] = [(sem("v_copied"), THREE.at(L, b + 1, c + 1))]
                    elif kind == "T":
                        if c == 0:
                            pe.wait_ge(sem(f"ctx_in{u2}"), dma_at(L, i2, C_DMAS))
                        for k in range(4):
                            last = PE.transpose(PS[:, n, k * KP:(k + 1) * KP], CT[:, u2, 4 * c + k, :], IDN[0:KP, 0:KP])
                        last.then_inc(sem("t_ready"), 1)
                        before[n] = [(sem("t_copied"), THREE.at(L, b + 2, c + 1))]
                    elif kind in "KR":
                        if L == 0:
                            pe.wait_ge(sem("t_copied"), THREE.at(L, b + 2, c + 1))
                        elif c == 0:
                            pe.wait_ge(sem(f"ctx_in{u2}"), dma_at(L, i2, C_DMAS))
                        mm(PS[:, n, 0:500], w(nm + ("_k" if kind == "K" else "_kr")),
                           features(L, u2)[:, c * 500:(c + 1) * 500]).then_inc(sem("k_ready"), 1)
                        done = 2 * c + (kind == "R") + 1 if cfg["rope"] else c + 1
                        before[n] = [(sem("k_free"), KUSES.at(L, b + 2, done))]
                    elif kind == "G":
                        for j in range(KJ):
                            last = mm(PS[:, n, 0:128], CT[:, u2, j, :], CT[:, u2, j, :], j == 0, j == KJ - 1)
                        last.then_inc(sem("g_ready"), 1)
                        before[n] = [(sem("g_copied"), ONE.at(L, b + 3))]
                    elif kind == "SH":
                        pe.wait_ge(sem("dg_ready"), ONE.at(L, b + 2))
                        mm(PS[:, n, :], SEL96[:, :], DG[:, c * 512:(c + 1) * 512]).then_inc(sem("sh_ready"), 1)
                        before[n] = [(sem("sh_copied"), SHIFTS.at(L, b + 1, c + 1))]
                    elif kind == "F":
                        pe.wait_ge(sem("om_ready"), ONE.at(L, b, CLEAR))
                        mm(PS[:, n, 0:S], OM[:, 1 - u, 1, :], w("fold")).then_inc(sem("f_ready"), 1)
                        before[n] = [(sem("f_copied"), folds(L, b + 1))]

                def score_unit(m):
                    half, j = divmod(m, KJ)
                    pe.wait_ge(sem("e_ready"), UNITS.at(L, b, m - 2 + 3))
                    for k in range(4):
                        g = half * 4 + k
                        dst = PS[0:KP, 3 + m % 3, k * 112:(k + 1) * 112].rearrange("p (h t) -> p h t", h=2)
                        last = mm(dst, ks(cfg, u, cfg["K2"])[:, g, j * KP:(j + 1) * KP],
                                  qs(cfg, u)[0:cfg["K2"], g, :, 0:S], True, not cfg["rope"])
                        if cfg["rope"]:
                            last = mm(dst, ONE16[96:97, :], SR[96:97, u, g * 128:(g + 1) * 128].rearrange(
                                "p (h t) -> p h t", h=2)[:, :, 0:S], False, True)
                    last.then_inc(sem("s_ready"), 1)

                def pv_unit(m):
                    half, j = divmod(m, KJ)
                    pe.wait_ge(sem("l_ready"), UNITS.at(L, b, m + 1 + 2))
                    for k in range(4):
                        g = half * 4 + k
                        mm(PS[:, 6, g * wide:(g + 1) * wide], PH[:, m % 4, 2 * k:2 * k + 2, :],
                           va(cfg, u)[:, j, g, :], j == 0 and g == 0, False, True)
                        last = mm(PS[:, 6, g * wide:g * wide + 2 * hd + 1], PL[:, m % 4, 2 * k:2 * k + 2, :],
                                  va(cfg, u)[:, j, g, 0:2 * hd + 1], False, j == KJ - 1, True)
                    last.then_inc(sem("p_ready"), 1)

                def max_unit(c):
                    g, third = divmod(c, 3)
                    if c == 0:
                        pe.wait_ge(sem(f"q_in{u1}"), dma_at(L, i1, Q_DMAS))
                        pe.wait_ge(sem(f"k_in{u1}0"), dma_at(L, i1, K_HALF[0]))
                    if c == 12:
                        pe.wait_ge(sem(f"k_in{u1}1"), dma_at(L, i1, K_HALF[1]))
                    pe.wait_ge(sem("m_done"), MAXES.at(L, b + 1, c - 1 + 2))
                    mm(PS[:, c % 2, 0:500], QS[0:cfg["K1"], u1, g * 128:(g + 1) * 128],
                       ks(cfg, u1, cfg["K1"])[:, g, third * 500:(third + 1) * 500]).then_inc(sem("m_ready"), 1)

                if has_d:
                    pe.wait_ge(sem("v_copied"), THREE.at(L, b + 1))
                    pe.wait_ge(sem("sh_copied"), SHIFTS.at(L, b + 1))
                units = 12 * cfg["halves"]
                for scores, maxima, other in slots(cfg):
                    for k in range(max(len(scores), len(maxima))):
                        if has_d and k < len(scores):
                            score_unit(scores[k])
                            if scores[k] >= LAG:
                                pv_unit(scores[k] - LAG)
                        if has_c and k < len(maxima):
                            max_unit(maxima[k])
                    for kind, c in other:
                        if kind != "SH" and {"V": has_c, "F": has_d, "DG": False}.get(kind, has_b):
                            short(kind, c)
                for k in range(LAG):
                    if has_d:
                        pv_unit(units - LAG + k)
                    if has_c and k < cfg["G"] // 4:
                        short("SH", k)

            steps(pe, L, step)
            pe.wait_ge(sem("f_copied"), folds(L, B))
            pe.wait_ge(sem("om_ready"), ONE.at(L, B, CLEAR))
            mm(PS[:, 2, 0:S], OM[:, 1, 1, :], w("fold")).then_inc(sem("f_ready"), 1)

        def x_act(act, L):
            cfg = XL[L]
            nm, banks = cfg["name"], short_banks(cfg)
            norm_act(act, nm, None, 1e-5)
            act.wait_ge(sem("pool_ready"), 1)

            def step(i, u, b, has_d, has_c, has_b):
                i1, u1 = later(i, u, 1)
                i2, u2 = later(i, u, 2)
                for scores, maxima, other in slots(cfg):
                    if has_d:
                        for m in scores:
                            act.wait_ge(sem("s_ready"), UNITS.at(L, b, m + 1 + CLEAR))
                            act.wait_ge(sem("p_ready"), UNITS.at(L, b, m - 3 + 4))
                            A.activation(PH[:, m % 4, :, 0:S],
                                         PS[0:KP, 3 + m % 3, 0:T].rearrange("p (h t) -> p h t", h=8), ACT.Exp)
                            act.wait_ge(sem("l_ready"), UNITS.at(L, b, m - 1 + 2))
                            A.activation(PR[m % 2][0:KP, :], PS[0:KP, 3 + m % 3, 0:T], ACT.Exp
                                         ).then_inc(sem("e_ready"), 1)
                    for kind, c in other:
                        if kind == "T" and has_b:
                            act.wait_ge(sem("t_ready"), THREE.at(L, b + 2, c + 1))
                            if c == 0 and has_c:
                                act.wait_ge(sem("v_ready"), THREE.at(L, b + 1, 3))
                                act.wait_ge(sem("ctt_out"), (b + 2) * 16)
                            A.activation(CTT[:, c * 500:(c + 1) * 500], PS[:, banks[kind, c], 0:500], ACT.Copy
                                         ).then_inc(sem("t_copied"), 1)
                        if kind == "K" and has_b and not cfg["rope"]:
                            act.wait_ge(sem("k_ready"), KUSES.at(L, b + 2, c + 1))
                            if has_d:
                                act.wait_ge(sem(f"k_out{u2}"), dma_at(L, i, C_DMAS))
                            A.activation(KHL[:, u2, 0, c * 500:(c + 1) * 500], PS[:, banks[kind, c], 0:500],
                                         ACT.Identity, bias=w(nm + "_bk")).then_inc(sem("kh_ready"), 1)
                        if kind == "G" and has_b:
                            act.wait_ge(sem("g_ready"), ONE.at(L, b + 3))
                            A.activation(GC[:, one(b + 2), :], PS[:, one(banks[kind, c]), 0:128], ACT.Copy).then_inc(sem("g_copied"), 1)
                        if kind == "SH" and has_c:
                            act.wait_ge(sem("sh_ready"), SHIFTS.at(L, b + 1, c + 1))
                            row = SR[96:97, u1, :] if cfg["rope"] else QS[96:97, u1, c * 512:(c + 1) * 512]
                            A.activation(row, PS[96:97, banks[kind, c], :], ACT.Copy).then_inc(sem("sh_copied"), 1)

            steps(act, L, step)

        def x_dve(dve, L):
            cfg = XL[L]
            nm, G_, hd, banks = cfg["name"], cfg["G"], cfg["hd"], short_banks(cfg)
            wide = 4 * hd + 1
            norm_dve(dve, nm, X, Y[:, :])
            if cfg["rope"]:
                def by_token(k):
                    return bc(ROPE_Q[:, k, :].unsqueeze(1), 128, B, S)
                dve.wait_ge(sem("rope_in"), 48)
                dve.wait_ge(sem("q_proj"), 1)
                link(dve, "dve_chain", V.tensor_tensor(Z[:, :].rearrange("p (b t) -> p b t", b=B),
                     bank(2).rearrange("p (b t) -> p b t", b=B), by_token(0), ALU.mult))
                dve.wait_ge(sem("q_proj"), 2)
                link(dve, "dve_chain", V.tensor_tensor(XC[:, :].rearrange("p (b t) -> p b t", b=B),
                     bank(3).rearrange("p (b t) -> p b t", b=B), by_token(1), ALU.mult))
                link(dve, "dve_chain", V.tensor_tensor(Z[:, :], Z[:, :], XC[:, :], ALU.add))
                link(dve, "dve_chain", V.tensor_scalar(Z[:, :], Z[:, :], cfg["scale"], None, ALU.mult))
            else:
                dve.wait_ge(sem("q_proj"), L + 2)
                link(dve, "dve_chain", V.tensor_scalar(Z[:, :], bank(2), w(nm + "_bq"), cfg["scale"], ALU.add, ALU.mult))
            link(dve, "dve_chain", V.tensor_copy(QH[:, 0, :], Z[:, :]))
            V.tensor_tensor(QH[:, 1, :], Z[:, :], QH[:, 0, :], ALU.subtract).then_inc(sem("q_split"), 1)

            def step(i, u, b, has_d, has_c, has_b):
                i1, u1 = later(i, u, 1)
                i2, u2 = later(i, u, 2)
                for scores, maxima, other in slots(cfg):
                    if has_d and L == 0:
                        for m in scores:
                            low_unit(dve, V, L, b, m)
                    if has_c:
                        for c in maxima:
                            dve.wait_ge(sem("m_ready"), MAXES.at(L, b + 1, c + 1))
                            V.tensor_reduce(MX[:, u1, c:c + 1], PS[:, c % 2, 0:500], AX.X, ALU.max
                                            ).then_inc(sem("m_done"), 1)
                    for kind, c in other:
                        if kind == "V" and has_c:
                            dst = va(cfg, u1)
                            if c == 0:
                                V.tensor_copy(VC[:, u1:u1 + 1, :], VALID[:, cfg["valid"], one(b + 1), :]
                                              ).then_inc(sem("valid_here"), 1)
                                dve.wait_ge(sem("valid_here"), ONE.at(L, b + 2))
                                V.tensor_copy(dst[:, :, :, 2 * hd], bc(VC[:, u1, :].unsqueeze(2), KP, KJ, G_))
                            dve.wait_ge(sem("v_ready"), THREE.at(L, b + 1, c + 1))
                            v = PS[0:KP, banks[kind, c], :].rearrange("p (j g n) -> p j g n", j=4, g=G_)
                            high = dst[:, 4 * c:4 * c + 4, :, 0:2 * hd]
                            V.tensor_tensor(high, v, bc(VC[:, u1, 4 * c:4 * c + 4].unsqueeze(2).unsqueeze(3),
                                                        KP, 4, G_, 2 * hd), ALU.mult).then_inc(sem("v_high"), 1)
                            dve.wait_ge(sem("v_high"), THREE.at(L, b + 1, c + 1))
                            V.tensor_tensor(dst[:, 4 * c:4 * c + 4, :, 2 * hd + 1:wide], v, high, ALU.subtract
                                            ).then_inc(sem("v_copied"), 1)
                        if kind == "F" and has_d:
                            dve.wait_ge(sem("f_ready"), folds(L, b + 1))
                            V.tensor_copy(AO[:, one(b), :], PS[:, one(banks[kind, c]), 0:S]).then_inc(sem("f_copied"), 1)
                        if kind in "KR" and has_b:
                            src = PS[:, banks[kind, c], 0:500]
                            if cfg["rope"]:
                                r = int(kind == "R")
                                if has_c and r == 0:
                                    dve.wait_ge(sem("k_split"), THREE.at(L, b + 1, c + 1))
                                dve.wait_ge(sem("k_ready"), KUSES.at(L, b + 2, 2 * c + r + 1))
                                V.tensor_tensor(KT[:, c, r, :], src, ROPE_K[:, r * SK + c * 500:r * SK + (c + 1) * 500],
                                                ALU.mult).then_inc(sem("k_free"), 1)
                            else:
                                dve.wait_ge(sem("kh_ready"), THREE.at(L - 1, b + 2, c + 1))
                                V.scalar_tensor_tensor(KHL[:, u2, 1, c * 500:(c + 1) * 500], src, w(nm + "_bk"),
                                                       KHL[:, u2, 0, c * 500:(c + 1) * 500], ALU.add, ALU.subtract
                                                       ).then_inc(sem("k_free"), 1)
                        if kind == "DG" and has_c:
                            dve.wait_ge(sem("m_done"), MAXES.at(L, b + 2, 2))
                            V.tensor_reduce(MM[:, u1, 0:G_], MX[:, u1, 0:3 * G_].rearrange("p (g c) -> p g c", c=3),
                                            AX.X, ALU.max, negate=True).then_inc(sem("mm_done"), 1)
                            dve.wait_ge(sem("mm_done"), ONE.at(L, b + 2))
                            V.tensor_tensor(DG[:, 0:G_ * 128].rearrange("p (g n) -> p g n", g=G_),
                                            bc(IDH[:, :].unsqueeze(1), 128, G_, 128),
                                            bc(MM[:, u1, 0:G_].unsqueeze(2), 128, G_, 128), ALU.mult
                                            ).then_inc(sem("dg_ready"), 1)
                if has_d:
                    pv = PS[:, 6, 0:G_ * wide].rearrange("p (g n) -> p g n", g=G_)
                    om = OM[:, u, :, :].rearrange("p a (g n) -> p a g n", g=G_)
                    dve.wait_ge(sem("p_ready"), UNITS.at(L, b + 1, 4))
                    V.reciprocal(RD[:, u, 0:G_], pv[:, :, 2 * hd])
                    V.tensor_copy(om[:, 0], pv[:, :, 0:2 * hd]).then_inc(sem("om_half"), 1)
                    dve.wait_ge(sem("om_half"), OM_STEPS.at(L, b, 1))
                    V.tensor_tensor(om[:, 1], bc(w("blk8" if hd == 8 else "blk16").unsqueeze(1), 128, G_, 2 * hd),
                                    bc(RD[:, u, 0:G_].unsqueeze(2), 128, G_, 2 * hd), ALU.mult)
                    V.tensor_tensor(om[:, 0], om[:, 0], pv[:, :, 2 * hd + 1:wide], ALU.add).then_inc(sem("om_half"), 1)
                    dve.wait_ge(sem("om_half"), OM_STEPS.at(L, b, 2))
                    V.tensor_tensor(om[:, 1], om[:, 0], om[:, 1], ALU.mult).then_inc(sem("om_ready"), 1)

            steps(dve, L, step)
            dve.wait_ge(sem("f_ready"), folds(L, B + 1))
            V.tensor_copy(AO[:, B:B + 1, :], PS[:, 2:3, 0:S]).then_inc(sem("f_copied"), 1)

        def x_pool(pool, L):
            cfg = XL[L]
            if L == 1:
                pool.wait_ge(*x_is(6))
                for u in range(2):
                    link(pool, "pool_chain", G.memset(KS32[64:128, u * 6144:u * 6144 + 4 * SK], 0.0))
                    link(pool, "pool_chain", G.memset(KS32[96:97, u * 6144:u * 6144 + 4 * SK], ONE_ONE))
                    link(pool, "pool_chain", G.memset(QS[:, u, :], 0.0))
                    link(pool, "pool_chain", G.memset(QS[64:65, u, :], BIG))
            if L:
                pool.wait_ge(*x_is((1, 7, 10)[L]))
                pool.sem_inc(sem("qs_clear"), 1)

            def step(i, u, b, has_d, has_c, has_b):
                i2, u2 = later(i, u, 2)
                for scores, maxima, other in slots(cfg):
                    if has_d and L:
                        for m in scores:
                            low_unit(pool, G, L, b, m)
                    for kind, c in other:
                        if kind == "K" and has_b and L == 0:
                            hi, lo = (KHL[:, u2, r, c * 500:(c + 1) * 500] for r in range(2))
                            pool.wait_ge(sem("k_free"), KUSES.at(L, b + 2, 2 * c + 2))
                            if has_d:
                                pool.wait_ge(sem(f"k_out{u2}"), dma_at(L, i, C_DMAS))
                            G.tensor_tensor(hi, KT[:, c, 0, :], KT[:, c, 1, :], ALU.add).then_inc(sem("k_high"), 1)
                            pool.wait_ge(sem("k_high"), THREE.at(L, b + 2, c + 1))
                            G.tensor_tensor(KT[:, c, 0, :], KT[:, c, 0, :], KT[:, c, 1, :], ALU.add
                                            ).then_inc(sem("k_whole"), 1)
                            pool.wait_ge(sem("k_whole"), THREE.at(L, b + 2, c + 1))
                            G.tensor_tensor(lo, KT[:, c, 0, :], hi, ALU.subtract).then_inc(sem("k_split"), 1)

            steps(pool, L, step)

        def l0x_end_pe(pe):
            pe.wait_ge(sem("f_copied"), folds(0, B + 1))
            mm(bank(2), w("l0x_out"), AO[:, 1:, :]).then_inc(sem("l0x_o"), 1)

        def l0x_end_dve(dve):
            dve.wait_ge(sem("l0x_o"), 1)
            V.tensor_tensor(X, X, bank(2), ALU.add).then_inc(sem("x_ready"), 1)

        CF = sb("CF", [8, T])
        GB = KS32[:, 0:E * T].rearrange("p (e t) -> p e t", e=E)
        HR = KS32[:, 4096:4096 + 3 * T].rearrange("p (a t) -> p a t", a=3)
        TK = sb("TK", [TT, 12, NT, 8])
        TI = sb("TI", [TT, NT, 8], u32)
        TS = sb("TS", [TT, 8, NT])

        ROUTER_AT = {"l0f": 1, "l1f": 2, "l3f": 3}
        MOE_AT = {"l0f": 0, "l1f": 1}

        def moe_pe(pe, nm, hin):
            pe.wait_ge(sem("router_cf"), ROUTER_AT[nm])
            for e in range(E):
                if e >= 2:
                    pe.wait_ge(sem("moe_gb"), MOE_AT[nm] * E + e - 1)
                mm(bank(2 + e % 2), bc(w("ident", e, 1, 8), 8, 128), CF[:, :]).then_inc(sem("moe_bc"), 1)

            def down(m):
                pe.wait_ge(sem("moe_hg"), MOE_AT[nm] * E * FC + m + 1)
                mm(bank(6), wb("w2", m * 128, 128), HR[:, m % 3, :], m == 0, False).then_inc(sem("moe_dn"), 1)

            pe.wait_ge(sem("moe_gb"), MOE_AT[nm] * E + E)
            for m in range(E * FC):
                if m >= 4:
                    pe.wait_ge(sem("moe_hid"), MOE_AT[nm] * E * FC + m - 3)
                mm(bank(2 + m % 4), wb("w1", m * 128, 128), hin).then_inc(sem("moe_up"), 1)
                if m >= 2:
                    down(m - 2)
            down(E * FC - 2)
            down(E * FC - 1)
            mm(bank(6), w(nm + "_b2", 0, 128, 8), CF[:, :], False, True).then_inc(sem("moe_sum"), 1)

        def moe_act(act, nm, func):
            for m in range(E * FC):
                act.wait_ge(sem("moe_up"), MOE_AT[nm] * E * FC + m + 1)
                if m >= 3:
                    act.wait_ge(sem("moe_dn"), MOE_AT[nm] * E * FC + m - 2)
                A.activation(HR[:, m % 3, :], bank(2 + m % 4), func, bias=w(nm + "_b1", m, 1)
                             ).then_inc(sem("moe_hid"), 1)

        def moe_dve(dve, nm):
            for e in range(E):
                dve.wait_ge(sem("moe_bc"), MOE_AT[nm] * E + e + 1)
                V.tensor_copy(GB[:, e, :], bank(2 + e % 2)).then_inc(sem("moe_gb"), 1)
            dve.wait_ge(sem("moe_gb"), MOE_AT[nm] * E + E)
            for m in range(E * FC):
                dve.wait_ge(sem("moe_hid"), MOE_AT[nm] * E * FC + m + 1)
                V.tensor_tensor(HR[:, m % 3, :], HR[:, m % 3, :], GB[:, m // FC, :], ALU.mult
                                ).then_inc(sem("moe_hg"), 1)

        def router_pe(pe, nm, hin, weights, bias=None):
            for j in range(NT):
                dst = PS[0:TT, 7, j * 8:(j + 1) * 8]
                last = mm(dst, hin[:, j * TT:(j + 1) * TT], w(weights), True, bias is None)
                if bias is not None:
                    last = mm(dst, w("ones", 0, TT, 1), w(bias, 0, 8, 1), False, True)
            last.then_inc(sem("router_logits"), 1)

        def to_experts_pe(pe, nm, mats):
            pe.wait_ge(sem("router_route"), ROUTER_AT[nm])
            for k, n in enumerate(mats):
                for j in range(NT):
                    last = PE.transpose(PS[0:8, 2 + k, j * TT:(j + 1) * TT], TK[:, n, j, :], IDN[0:TT, 0:TT])
            last.then_inc(sem("router_byexp"), 1)

        def col(k):
            return bc(TS[:, k, :].unsqueeze(2), TT, NT, 8)

        def softmax_dve(dve, nm, top=False):
            dve.wait_ge(sem("router_logits"), ROUTER_AT[nm])
            link(dve, "dve_chain", V.tensor_copy(TK[:, 0], PS[0:TT, 7, 0:32].rearrange("p (j e) -> p j e", j=NT)))
            link(dve, "dve_chain", V.tensor_reduce(TS[:, 0, :], TK[:, 0], AX.X, ALU.max))
            V.tensor_tensor(TK[:, 1], TK[:, 0], col(0), ALU.subtract).then_inc(sem("router_gless"), 1)
            if top:
                for j in range(NT):
                    link(dve, "dve_chain", V.max(TK[:, 4, j, :], TK[:, 0, j, :]))
                    link(dve, "dve_chain", V.max_index(TI[:, j, :], TK[:, 4, j, :], TK[:, 0, j, :]))
                link(dve, "dve_chain", V.tensor_copy(TK[:, 5], TI[:, :, :]))
                for k in range(2):
                    link(dve, "dve_chain", V.tensor_tensor(
                        TK[:, 2 + k], bc(w("iota", p=TT).unsqueeze(1), TT, NT, 8),
                        bc(TK[:, 5, :, k:k + 1], TT, NT, 8), ALU.is_equal))
            dve.wait_ge(sem("router_gexp"), ROUTER_AT[nm])
            link(dve, "dve_chain", V.tensor_reduce(TS[:, 1, :], TK[:, 1], AX.X, ALU.add))
            link(dve, "dve_chain", V.reciprocal(TS[:, 1, :], TS[:, 1, :]))

        def softmax_act(act, nm):
            act.wait_ge(sem("router_gless"), ROUTER_AT[nm])
            A.activation(TK[:, 1], TK[:, 1], ACT.Exp).then_inc(sem("router_gexp"), 1)

        QK = KS32[:, 0:8192].rearrange("p (m b t) -> p m b t", m=16, b=B)
        VS = KS32[0:S, 8192:10240].rearrange("p (a n) -> p a n", a=2)
        PT = KS32[0:S, 10240:12288].rearrange("p (a n) -> p a n", a=2)
        RR = R[:, 0:2 * T].rearrange("p (a n) -> p a n", a=2)
        RQ = R[:, 2 * T:4 * T].rearrange("p (a n) -> p a n", a=2)
        SB2 = R[:, 0:2 * T].rearrange("p (a n) -> p a n", a=2)
        OA = R[:, 2 * T:10 * T].rearrange("p (g t) -> p g t", g=8)

        def l0f_pe(pe):
            norm_pe(pe, "l0f", X, x_is(2))
            norm_pe(pe, "l0f_1", Y[:, :], (sem("norm_ready"), NORM_AT["l0f"]))
            normed(pe, "l0f_1")
            pe.wait_ge(sem("big0_in"), 96)

            def squares(m):
                pe.wait_ge(sem("l0f_sq"), m + 1)
                mm(bank(4 + m % 2), w("half"), RQ[:, m % 2, :]).then_inc(sem("l0f_ss"), 1)

            for m in range(16):
                if m >= 2:
                    pe.wait_ge(sem("l0f_qk"), m - 1)
                mm(bank(2 + m % 2), wb("wq", m * 128, 128), Z[:, :]).then_inc(sem("l0f_raw"), 1)
                if m >= 1:
                    squares(m - 1)
            squares(15)

            def values(b):
                if b:
                    pe.wait_ge(sem("l0f_vs"), b)
                for n in range(2):
                    last = mm(PS[0:S, 6 + n, :], Z[:, b * S:(b + 1) * S], wb("wv", n * 512, 512))
                last.then_inc(sem("l0f_v"), 1)

            def scores(b):
                pe.wait_ge(sem("l0f_qk"), 16)
                pe.wait_ge(sem("l0f_clear"), 1)
                if b >= 2:
                    pe.wait_ge(sem("l0f_sb"), b - 1)
                for g in range(8):
                    for h in range(2):
                        last = mm(PS[64 * h:64 * h + 64, 2 + b % 2, g * S:(g + 1) * S],
                                  QK[64 * h:64 * h + 64, g, b, :], QK[64 * h:64 * h + 64, 8 + g, b, 0:S])
                last.then_inc(sem("l0f_s"), 1)

            values(0)
            scores(0)
            for b in range(B):
                if b + 1 < B:
                    scores(b + 1)
                pe.wait_ge(sem("l0f_p"), b + 1)
                if b:
                    pe.wait_ge(sem("l0f_pt"), b)
                for g in range(8):
                    last = PE.transpose(PS[0:S, 4 + g // 4, g % 4 * 128:g % 4 * 128 + 128],
                                        SB2[:, b % 2, g * S:(g + 1) * S], IDN)
                last.then_inc(sem("l0f_t"), 1)
                if b + 1 < B:
                    values(b + 1)
                pe.wait_ge(sem("l0f_pt"), b + 1)
                pe.wait_ge(sem("l0f_vs"), b + 1)
                if b >= 2:
                    pe.wait_ge(sem("l0f_oc"), b - 1)
                for g in range(8):
                    for h in range(2):
                        last = mm(PS[64 * h:64 * h + 64, b % 2, g * S:(g + 1) * S],
                                  VS[:, b % 2, (2 * g + h) * 64:(2 * g + h + 1) * 64],
                                  PT[:, b % 2, g * 128 + 64 * h:g * 128 + 64 * h + S])
                last.then_inc(sem("l0f_o"), 1)
            pe.wait_ge(sem("l0f_oc"), B)
            for g in range(8):
                last = mm(bank(2), wb("wo", g * 128, 128), OA[:, g, :], g == 0, g == 7)
            last.then_inc(sem("l0f_proj"), 1)
            norm_pe(pe, "l0f_2", Z[:, :], (sem("l0f_z"), 1))
            normed(pe, "l0f_2")
            router_pe(pe, "l0f", Y[:, :], "l0f_gate", "row_gb")
            to_experts_pe(pe, "l0f", (2,))
            moe_pe(pe, "l0f", Y[:, :])
            norm_pe(pe, "l0f_3", Z[:, :], (sem("l0f_z"), 2))

        def l0f_act(act):
            norm_act(act, "l0f", X, 1e-5)
            norm_act(act, "l0f_1", None, 1e-5)

            def inverse(m):
                act.wait_ge(sem("l0f_ss"), m + 1)
                if m >= 2:
                    act.wait_ge(sem("l0f_qk"), m - 1)
                link(act, "act_chain", A.activation(RR[:, m % 2, :], bank(4 + m % 2), ACT.Ln, bias=1e-12))
                A.activation(RR[:, m % 2, :], RR[:, m % 2, :], ACT.Exp, scale=-0.5).then_inc(sem("l0f_rs"), 1)

            for m in range(16):
                act.wait_ge(sem("l0f_raw"), m + 1)
                if m >= 2:
                    act.wait_ge(sem("l0f_ss"), m - 1)
                A.activation(RQ[:, m % 2, :], bank(2 + m % 2), ACT.Square).then_inc(sem("l0f_sq"), 1)
                if m >= 1:
                    inverse(m - 1)
            inverse(15)
            for b in range(B):
                act.wait_ge(sem("l0f_v"), b + 1)
                if b >= 2:
                    act.wait_ge(sem("l0f_o"), b - 1)
                A.activation(VS[:, b % 2, :].rearrange("p (a n) -> p a n", a=2), PS[0:S, 6:8, :], ACT.Copy
                             ).then_inc(sem("l0f_vs"), 1)
                act.wait_ge(sem("l0f_sb"), b + 1)
                A.activation(SB2[:, b % 2, :], SB2[:, b % 2, :], ACT.Exp).then_inc(sem("l0f_e"), 1)
                act.wait_ge(sem("l0f_t"), b + 1)
                A.activation(PT[:, b % 2, :].rearrange("p (a n) -> p a n", a=2), PS[0:S, 4:6, :], ACT.Copy
                             ).then_inc(sem("l0f_pt"), 1)
            norm_act(act, "l0f_2", None, 1e-5)
            softmax_act(act, "l0f")
            moe_act(act, "l0f", ACT.Gelu_apprx_tanh)
            norm_act(act, "l0f_3", None, 1e-5)

        def l0f_pool(pool):
            pool.wait_ge(*x_is(2))
            G.memset(QK[:, 0:8, :, S:SP2], 0.0).then_inc(sem("l0f_clear"), 1)

        def l0f_dve(dve):
            norm_dve(dve, "l0f", X, Y[:, :])
            norm_dve(dve, "l0f_1", Y[:, :], Z[:, :], w("l0f_g"), w("l0f_c"))
            for m in range(16):
                dve.wait_ge(sem("l0f_rs"), m + 1)
                V.scalar_tensor_tensor(QK[:, m, :, 0:S], bank(2 + m % 2).rearrange("p (b t) -> p b t", b=B),
                                       w("l0f_qs" if m < 8 else "l0f_ks", m % 8, 1),
                                       RR[:, m % 2, :].rearrange("p (b t) -> p b t", b=B), ALU.mult, ALU.mult
                                       ).then_inc(sem("l0f_qk"), 1)
            m8, d8 = MM[:, 0, :], RD[:, 0, :]

            def less(b):
                dve.wait_ge(sem("l0f_s"), b + 1)
                if b >= 2:
                    dve.wait_ge(sem("l0f_t"), b - 1)
                s = SB2[:, b % 2, :].rearrange("p (g t) -> p g t", g=8)
                link(dve, "dve_chain", V.scalar_tensor_tensor(
                    s, bank(2 + b % 2).rearrange("p (g t) -> p g t", g=8), 10.0,
                    bc(w("causal").unsqueeze(1), 128, 8, S), ALU.mult, ALU.add))
                link(dve, "dve_chain", V.tensor_reduce(m8, s, AX.X, ALU.max))
                V.tensor_tensor(s, s, bc(m8.unsqueeze(2), 128, 8, S), ALU.subtract).then_inc(sem("l0f_sb"), 1)

            def keep(b):
                dve.wait_ge(sem("l0f_o"), b + 1)
                V.tensor_copy(OA[:, :, b * S:(b + 1) * S], bank(b % 2).rearrange("p (g t) -> p g t", g=8)
                              ).then_inc(sem("l0f_oc"), 1)

            less(0)
            for b in range(B):
                if b + 1 < B:
                    less(b + 1)
                dve.wait_ge(sem("l0f_e"), b + 1)
                s = SB2[:, b % 2, :].rearrange("p (g t) -> p g t", g=8)
                link(dve, "dve_chain", V.tensor_reduce(d8, s, AX.X, ALU.add))
                link(dve, "dve_chain", V.reciprocal(d8, d8))
                V.tensor_tensor(s, s, bc(d8.unsqueeze(2), 128, 8, S), ALU.mult).then_inc(sem("l0f_p"), 1)
                if b:
                    keep(b - 1)
            keep(B - 1)
            dve.wait_ge(sem("l0f_proj"), 1)
            V.tensor_copy(Z[:, :], bank(2)).then_inc(sem("l0f_z"), 1)
            norm_dve(dve, "l0f_2", Z[:, :], Y[:, :], w("l0f_g"), w("l0f_c"))
            softmax_dve(dve, "l0f")
            V.tensor_tensor(TK[:, 2], TK[:, 1], col(1), ALU.mult).then_inc(sem("router_route"), 1)
            dve.wait_ge(sem("router_byexp"), ROUTER_AT["l0f"])
            V.tensor_copy(CF[:, :], bank(2, T, 8)).then_inc(sem("router_cf"), 1)
            moe_dve(dve, "l0f")
            dve.wait_ge(sem("moe_sum"), 1)
            V.tensor_copy(Z[:, :], bank(6)).then_inc(sem("l0f_z"), 1)
            norm_dve(dve, "l0f_3", Z[:, :], Z[:, :], w("l0f_g"), w("l0f_c"))
            normed(dve, "l0f_3")
            V.tensor_tensor(X, X, Z[:, :], ALU.add).then_inc(sem("x_ready"), 1)

        def piece(n, cols=T, p=128):
            return KS32[0:p, n * 512:n * 512 + cols]

        lq, lkn, lkb, lbt, lnr, ld0, ld1, lve = (piece(n) for n in range(8))
        (mN1, mN1T, mE, mQA, mP2, mP2T, mY1, mY2, mP4, mDT, mM, mMT, mM2, mM2T, mM4T) = (
            piece(8 + n, T, TT) for n in range(15))
        RW = R[0:TT, 0:2560].rearrange("p (a n) -> p a n", a=5)
        AL = sb("AL", [128, 4])

        def tile(ap, j, n=TT):
            return ap[:, j * n:(j + 1) * n]

        def l1a_pe(pe):
            norm_pe(pe, "l1a", X, x_is(3))
            norm_pe(pe, "l1a_1", None, None)
            normed(pe, "l1a_1")
            for n, name in enumerate(("l1a_k", "l1a_beta", "l1a_q", "l1a_v")):
                mm(bank(2 + n), w(name), Z[:, :]).then_inc(sem("l1a_proj"), 1)
            pe.wait_ge(sem("l1a_ksq"), 1)
            mm(bank(6), w("ones"), SQ[:, :]).then_inc(sem("l1a_kss"), 1)

            def products(k, *jobs):
                pe.wait_ge(sem("l1a_sb"), k)
                for n, l, r, cols in jobs:
                    for j in range(NT):
                        last = mm(PS[0:TT, n, j * cols:(j + 1) * cols], tile(l, j), tile(r, j, cols))
                last.then_inc(sem("l1a_done"), 1)

            products(1, (2, lkb, lkn, TT), (3, lkn, lkb, TT), (4, lkn, lq, TT))
            pe.wait_ge(sem("l1a_vb"), 1)
            for j in range(NT):
                last = PE.transpose(PS[0:TT, 5, j * 128:(j + 1) * 128], tile(lve, j), IDN)
            last.then_inc(sem("l1a_vt"), 1)
            products(2, (2, mN1T, mN1, TT), (3, mN1, mN1T, TT))
            products(3, (4, mP2, mY1, TT), (6, mP2T, mP2, TT))
            products(4, (2, mP4, mY2, TT))
            products(5, (3, mDT, mE, TT), (4, mE, mDT, TT), (6, mDT, RW[:, 0], 128))
            products(6, (2, mMT, mM, TT), (5, mM, mMT, TT))
            products(7, (3, mM2, mM2T, TT))
            products(8, (4, mM4T, RW[:, 1], 128))
            products(9, (6, mM2T, RW[:, 2], 128))
            products(10, (7, mMT, RW[:, 3], 128))
            pe.wait_ge(sem("l1a_sb"), 11)
            for j in range(NT):
                last = mm(PS[:, 2, j * TT:(j + 1) * TT], tile(RW[:, 4], j, 128), tile(mQA, j))
            last.then_inc(sem("l1a_done"), 1)
            pe.wait_ge(sem("l1a_sb"), 12)
            mm(bank(3), w("l1a_o"), lq).then_inc(sem("l1a_done"), 1)
            norm_pe(pe, "l1a_2", None, None)
            normed(pe, "l1a_2")
            for n in range(2):
                mm(bank(2 + n), w("l1a_gate", n * 128, 128), Y[:, :]).then_inc(sem("l1a_mlp"), 1)
                mm(bank(4 + n), w("l1a_up", n * 128, 128), Y[:, :]).then_inc(sem("l1a_mlp"), 1)
            for n in range(2):
                pe.wait_ge(sem("l1a_hid"), n + 1)
                last = mm(bank(6), w("l1a_down", n * 128, 128), piece(n), n == 0, n == 1)
            last.then_inc(sem("l1a_mlp"), 1)

        def l1a_act(act):
            norm_act(act, "l1a", X, 1e-5)
            norm_act(act, "l1a_1", Y[:, :], 1e-6, (sem("norm_ready"), NORM_AT["l1a"]))
            act.wait_ge(sem("l1a_proj"), 1)
            A.activation(SQ[:, :], bank(2), ACT.Square).then_inc(sem("l1a_ksq"), 1)
            act.wait_ge(sem("l1a_proj"), 2)
            A.activation(AL[:, 0:1], w("l1a_alpha"), ACT.Sigmoid).then_inc(sem("l1a_gates"), 1)
            A.activation(lbt, bank(3), ACT.Sigmoid, bias=w("l1a_bb")).then_inc(sem("l1a_gates"), 1)
            act.wait_ge(sem("l1a_kss"), 1)
            A.activation(lnr, bank(6), ACT.Sqrt).then_inc(sem("l1a_norm"), 1)
            norm_act(act, "l1a_2", Z[:, :], 1e-6, (sem("l1a_sb"), 13))
            for n in range(2):
                act.wait_ge(sem("l1a_mlp"), 2 * n + 2)
                A.activation(piece(n), bank(2 + n), ACT.Silu).then_inc(sem("l1a_silu"), 1)

        def l1a_dve(dve):
            norm_dve(dve, "l1a", X, Y[:, :])
            norm_dve(dve, "l1a_1", Y[:, :], Z[:, :], w("l1a_n1"))
            dve.wait_ge(sem("l1a_gates"), 2)
            link(dve, "dve_chain", V.tensor_scalar(AL[:, 1:2], AL[:, 0:1], -1.0, 1.0, ALU.mult, ALU.add))
            V.tensor_scalar(ld0, w("reset"), AL[:, 1:2], None, ALU.mult)
            dve.wait_ge(sem("l1a_proj"), 4)
            V.tensor_copy(lq, bank(4))
            link(dve, "dve_chain", V.tensor_scalar(ld1, bank(5), AL[:, 0:1], None, ALU.mult))
            link(dve, "dve_chain", V.tensor_tensor_scan(lve, ld0, ld1, 0.0, ALU.mult, ALU.add))
            V.tensor_tensor(lve, lve, lbt, ALU.mult).then_inc(sem("l1a_vb"), 1)
            dve.wait_ge(sem("l1a_norm"), 1)
            link(dve, "dve_chain", V.tensor_scalar(lnr, lnr, 1e-12, None, ALU.max))
            link(dve, "dve_chain", V.reciprocal(lnr, lnr))
            link(dve, "dve_chain", V.tensor_tensor(lkn, bank(2), lnr, ALU.mult))
            V.tensor_tensor(lkb, lkn, lbt, ALU.mult).then_inc(sem("l1a_sb"), 1)

            def masked(dst, n, name):
                return V.tensor_tensor(dst.rearrange("p (j t) -> p j t", j=NT), bank(n, T, TT).rearrange(
                    "p (j t) -> p j t", j=NT), bc(w(name, p=TT).unsqueeze(1), TT, NT, TT), ALU.mult)

            def done(k):
                dve.wait_ge(sem("l1a_done"), k)

            done(1)
            masked(mN1, 2, "inlow")
            masked(mE, 2, "offlow")
            masked(mQA, 4, "upper")
            link(dve, "dve_chain", masked(mN1T, 3, "inup"))
            V.tensor_tensor(mY1.rearrange("p (j t) -> p j t", j=NT), mN1T.rearrange("p (j t) -> p j t", j=NT),
                            bc(w("ident", 0, TT, TT).unsqueeze(1), TT, NT, TT), ALU.add).then_inc(sem("l1a_sb"), 1)
            dve.wait_ge(sem("l1a_vt"), 1)
            V.tensor_copy(RW[:, 0], bank(5, 512, TT))
            done(2)
            V.tensor_copy(mP2, bank(2, T, TT))
            V.tensor_copy(mP2T, bank(3, T, TT)).then_inc(sem("l1a_sb"), 1)
            done(3)
            V.tensor_copy(mP4, bank(6, T, TT))
            V.tensor_tensor(mY2, mY1, bank(4, T, TT), ALU.add).then_inc(sem("l1a_sb"), 1)
            done(4)
            dve.wait_ge(sem("l1a_sb"), 4)
            V.tensor_tensor(mDT, mY2, bank(2, T, TT), ALU.add).then_inc(sem("l1a_sb"), 1)
            done(5)
            V.tensor_copy(mM, bank(3, T, TT))
            V.tensor_copy(RW[:, 1], bank(6, 512, TT))
            V.tensor_copy(mMT, bank(4, T, TT)).then_inc(sem("l1a_sb"), 1)
            done(6)
            V.tensor_copy(mM2, bank(2, T, TT))
            V.tensor_copy(mM2T, bank(5, T, TT)).then_inc(sem("l1a_sb"), 1)
            done(7)
            V.tensor_copy(mM4T, bank(3, T, TT)).then_inc(sem("l1a_sb"), 1)
            for k, n in ((8, 4), (9, 6), (10, 7)):
                done(k)
                dve.wait_ge(sem("l1a_sb"), k)
                V.tensor_tensor(RW[:, k - 6], RW[:, k - 7], bank(n, 512, TT), ALU.add).then_inc(sem("l1a_sb"), 1)
            done(11)
            V.tensor_copy(lq, bank(2)).then_inc(sem("l1a_sb"), 1)
            done(12)
            V.tensor_tensor(Z[:, :], bank(3), Y[:, :], ALU.add).then_inc(sem("l1a_sb"), 1)
            norm_dve(dve, "l1a_2", Z[:, :], Y[:, :], w("l1a_n2"))
            for n in range(2):
                dve.wait_ge(sem("l1a_silu"), n + 1)
                V.tensor_tensor(piece(n), piece(n), bank(4 + n), ALU.mult).then_inc(sem("l1a_hid"), 1)
            link(dve, "dve_chain", V.tensor_tensor(X, X, Z[:, :], ALU.add))
            dve.wait_ge(sem("l1a_mlp"), 5)
            V.tensor_tensor(X, X, bank(6), ALU.add).then_inc(sem("x_ready"), 1)

        LX = R[0:S, 0:1024]
        LX8 = LX.rearrange("p (b n) -> p b n", b=B)
        LXP = PS[0:S, 2:4, :].rearrange("p a (b n) -> p a b n", b=4)

        def l1x_pe(pe):
            norm_pe(pe, "l1x", X, x_is(4))
            normed(pe, "l1x")
            for b in range(B):
                last = mm(PS[0:S, 2 + b // 4, b % 4 * 128:b % 4 * 128 + 128], Y[:, b * S:(b + 1) * S], GC[:, b, :])
            last.then_inc(sem("l1x_o"), 1)
            pe.wait_ge(sem("l1x_p"), 1)
            for b in range(B):
                last = PE.transpose(PS[:, 4, b * S:(b + 1) * S], LX[:, b * 128:(b + 1) * 128], IDN[0:S, 0:S])
            last.then_inc(sem("l1x_t"), 1)

        def l1x_act(act):
            norm_act(act, "l1x", X, 1e-5)
            act.wait_ge(sem("l1x_less"), 1)
            A.activation(LX, LX, ACT.Exp, scale=1 / math.sqrt(D)).then_inc(sem("l1x_e"), 1)

        def l1x_dve(dve):
            norm_dve(dve, "l1x", X, Y[:, :])
            m8, d8 = MM[0:S, 0, :], RD[0:S, 0, :]
            dve.wait_ge(sem("l1x_o"), 1)
            link(dve, "dve_chain", V.tensor_reduce(m8.rearrange("p (a b) -> p a b", a=2), LXP, AX.X, ALU.max))
            V.tensor_tensor(LX.rearrange("p (a b n) -> p a b n", a=2, b=4), LXP,
                            bc(m8.rearrange("p (a b) -> p a b", a=2).unsqueeze(3), S, 2, 4, 128),
                            ALU.subtract).then_inc(sem("l1x_less"), 1)
            dve.wait_ge(sem("l1x_e"), 1)
            link(dve, "dve_chain", V.tensor_reduce(d8, LX8, AX.X, ALU.add))
            link(dve, "dve_chain", V.reciprocal(d8, d8))
            V.tensor_tensor(LX8, LX8, bc(d8.unsqueeze(2), S, B, 128), ALU.mult).then_inc(sem("l1x_p"), 1)
            dve.wait_ge(sem("l1x_t"), 1)
            V.tensor_tensor(X, X, bank(4), ALU.add).then_inc(sem("x_ready"), 1)

        CAP = float(2 * 2 * T // E)
        E8 = R[0:8, 0:6 * T].rearrange("p (a t) -> p a t", a=6)

        def l1f_pe(pe):
            norm_pe(pe, "l1f", X, x_is(5))
            normed(pe, "l1f")
            router_pe(pe, "l1f", Y[:, :], "l1f_g")
            to_experts_pe(pe, "l1f", (2, 3, 6, 7))
            pe.wait_ge(sem("big1_in"), 96)
            moe_pe(pe, "l1f", Y[:, :])

        def l1f_act(act):
            norm_act(act, "l1f", X, 1e-5)
            softmax_act(act, "l1f")
            moe_act(act, "l1f", ACT.Gelu)

        def l1f_dve(dve):
            norm_dve(dve, "l1f", X, Y[:, :])
            V.memset(E8[:, 0, :], 1.0)
            softmax_dve(dve, "l1f", True)
            link(dve, "dve_chain", V.tensor_tensor(TK[:, 1], TK[:, 1], col(1), ALU.mult))
            for k in range(2):
                link(dve, "dve_chain", V.tensor_tensor(TK[:, 6 + k], TK[:, 1], TK[:, 2 + k], ALU.mult))
                link(dve, "dve_chain", V.tensor_reduce(TS[:, 2 + k, :], TK[:, 6 + k], AX.X, ALU.add))
            link(dve, "dve_chain", V.tensor_tensor(TS[:, 4, :], TS[:, 2, :], TS[:, 3, :], ALU.add))
            link(dve, "dve_chain", V.tensor_scalar(TS[:, 4, :], TS[:, 4, :], 1e-9, None, ALU.add))
            link(dve, "dve_chain", V.reciprocal(TS[:, 4, :], TS[:, 4, :]))
            link(dve, "dve_chain", V.tensor_tensor(TK[:, 6], TK[:, 6], col(4), ALU.mult))
            V.tensor_tensor(TK[:, 7], TK[:, 7], col(4), ALU.mult).then_inc(sem("router_route"), 1)
            dve.wait_ge(sem("router_byexp"), ROUTER_AT["l1f"])
            V.tensor_copy(E8[:, 1, :], bank(2, T, 8))
            link(dve, "dve_chain", V.tensor_copy(E8[:, 2, :], bank(3, T, 8)))
            link(dve, "dve_chain", V.tensor_tensor_scan(E8[:, 3, :], E8[:, 0, :], E8[:, 1, :], 0.0, ALU.mult, ALU.add))
            link(dve, "dve_chain", V.tensor_tensor_scan(E8[:, 4, :], E8[:, 0, :], E8[:, 2, :], 0.0, ALU.mult, ALU.add))
            link(dve, "dve_chain", V.tensor_scalar(E8[:, 4, :], E8[:, 4, :], E8[:, 3, T - 1:T], CAP, ALU.add, ALU.is_le))
            link(dve, "dve_chain", V.tensor_tensor(E8[:, 4, :], E8[:, 4, :], bank(5, T, 8), ALU.mult))
            link(dve, "dve_chain", V.scalar_tensor_tensor(E8[:, 3, :], E8[:, 3, :], CAP, bank(4, T, 8),
                                                          ALU.is_le, ALU.mult))
            V.tensor_tensor(CF[:, :], E8[:, 3, :], E8[:, 4, :], ALU.add).then_inc(sem("router_cf"), 1)
            moe_dve(dve, "l1f")
            dve.wait_ge(sem("moe_sum"), 2)
            V.tensor_tensor(X, X, bank(6), ALU.add).then_inc(sem("x_ready"), 1)

        def r(n, k=1):
            return R[:, n * T:(n + k) * T]

        def l2a_pe(pe):
            norm_pe(pe, "l2a", X, x_is(6))
            norm_pe(pe, "l2a_1", None, None)
            normed(pe, "l2a_1")
            for n in range(4):
                mm(bank(2 + n), w("l2a_in", n * 128, 128), Z[:, :]).then_inc(sem("l2a_uz"), 1)
            pe.wait_ge(sem("l2a_silu"), 2)
            for n in range(2):
                for k in range(2):
                    last = mm(bank(6 + n), w("l2a_dt", k * 256 + n * 128, 128), r(k), k == 0, k == 1)
                last.then_inc(sem("l2a_dt"), 1)
            for n in range(2):
                pe.wait_ge(sem("l2a_s"), n + 1)
                last = mm(bank(2), w("l2a_out", n * 128, 128), r(6 + n), n == 0, n == 1)
            last.then_inc(sem("l2a_y"), 1)

        def l2a_act(act):
            norm_act(act, "l2a", X, 1e-5)
            norm_act(act, "l2a_1", Y[:, :], 1e-5, (sem("norm_ready"), NORM_AT["l2a"]))
            for n in range(4):
                act.wait_ge(sem("l2a_uz"), n + 1)
                A.activation(r(n), bank(2 + n), ACT.Silu).then_inc(sem("l2a_silu"), 1)
            for n in range(2):
                act.wait_ge(sem("l2a_dt"), n + 1)
                A.activation(r(4 + n), bank(6 + n), ACT.Sigmoid, bias=w("l2a_bdt", n, 1)).then_inc(sem("l2a_lam"), 1)

        def l2a_dve(dve):
            norm_dve(dve, "l2a", X, Y[:, :])
            norm_dve(dve, "l2a_1", Y[:, :], Z[:, :], w("l2a_n"))
            for n in range(2):
                dve.wait_ge(sem("l2a_lam"), n + 1)
                link(dve, "dve_chain", V.scalar_tensor_tensor(r(6 + n), r(4 + n), 1.0, r(n), ALU.subtract, ALU.mult))
                link(dve, "dve_chain", V.tensor_tensor(r(4 + n), r(4 + n), w("reset"), ALU.mult))
                link(dve, "dve_chain", V.tensor_tensor_scan(r(8 + n), r(4 + n), r(6 + n), 0.0, ALU.mult, ALU.subtract))
                dve.wait_ge(sem("l2a_silu"), 3 + n)
                V.tensor_tensor(r(6 + n), r(8 + n), r(2 + n), ALU.mult).then_inc(sem("l2a_s"), 1)
            link(dve, "dve_chain", V.tensor_tensor(X, X, Y[:, :], ALU.add))
            dve.wait_ge(sem("l2a_y"), 1)
            V.tensor_tensor(X, X, bank(2), ALU.add).then_inc(sem("x_ready"), 1)

        def l2x_end_dve(dve):
            dve.wait_ge(sem("f_copied"), folds(1, B + 1))
            V.scalar_tensor_tensor(X, AO[:, 1:, :].rearrange("p b t -> p (b t)"), w("l2x_bv"), X, ALU.add, ALU.add
                                   ).then_inc(sem("x_ready"), 1)

        MAGIC = float(1.5 * 2 ** 23)
        XQ = R[0:TT, 0:512]
        XQ4 = XQ.rearrange("p (j n) -> p j n", j=NT)

        def l2f_pe(pe):
            norm_pe(pe, "l2f", X, x_is(8))
            normed(pe, "l2f")
            for j in range(NT):
                last = mm(PS[0:TT, 2, j * 128:(j + 1) * 128], Y[:, j * TT:(j + 1) * TT], w("hadamard"))
            last.then_inc(sem("l2f_xh"), 1)
            pe.wait_ge(sem("l2f_wq"), 1)
            PE.transpose(PS[:, 3, 0:128], R[:, 512:640], IDN).then_inc(sem("l2f_t"), 1)
            pe.wait_ge(sem("l2f_xq"), 1)
            for j in range(NT):
                last = PE.transpose(PS[:, 4, j * TT:(j + 1) * TT], XQ[:, j * 128:(j + 1) * 128], IDN[0:TT, 0:TT])
            last.then_inc(sem("l2f_t"), 1)
            pe.wait_ge(sem("l2f_ops"), 2)
            mm(bank(5), R[:, 768:896], R[:, 896:896 + T]).then_inc(sem("l2f_y"), 1)

        def l2f_act(act):
            norm_act(act, "l2f", X, 1e-5)

        def l2f_dve(dve):
            norm_dve(dve, "l2f", X, Y[:, :])
            c = AL
            wt, tq, t2 = w("l2f_w"), R[:, 512:640], R[:, 640:768]
            link(dve, "dve_chain", V.tensor_reduce(c[:, 0:1], wt, AX.X, ALU.add, apply_absolute_value=True))
            link(dve, "dve_chain", V.tensor_scalar(c[:, 0:1], c[:, 0:1], 1 / 128, 1e-5, ALU.mult, ALU.max))
            link(dve, "dve_chain", V.reciprocal(c[:, 1:2], c[:, 0:1]))
            link(dve, "dve_chain", V.tensor_scalar(tq, wt, c[:, 1:2], 0.5, ALU.mult, ALU.is_gt))
            V.tensor_scalar(t2, wt, c[:, 1:2], -0.5, ALU.mult, ALU.is_lt).then_inc(sem("l2f_neg"), 1)
            dve.wait_ge(sem("l2f_neg"), 1)
            link(dve, "dve_chain", V.tensor_tensor(tq, tq, t2, ALU.subtract))
            V.tensor_scalar(tq, tq, c[:, 0:1], None, ALU.mult).then_inc(sem("l2f_wq"), 1)
            dve.wait_ge(sem("l2f_xh"), 1)
            xh = PS[0:TT, 2, :].rearrange("p (j n) -> p j n", j=NT)
            link(dve, "dve_chain", V.tensor_reduce(TS[:, 0, :], xh, AX.X, ALU.max, apply_absolute_value=True))
            link(dve, "dve_chain", V.tensor_scalar(TS[:, 0, :], TS[:, 0, :], 1e-5, 1 / 7, ALU.max, ALU.mult))
            link(dve, "dve_chain", V.reciprocal(TS[:, 1, :], TS[:, 0, :]))
            link(dve, "dve_chain", V.tensor_tensor(XQ4, xh, bc(TS[:, 1, :].unsqueeze(2), TT, NT, 128), ALU.mult))
            link(dve, "dve_chain", V.tensor_scalar(XQ, XQ, MAGIC, MAGIC, ALU.add, ALU.subtract))
            link(dve, "dve_chain", V.tensor_scalar(XQ, XQ, -8.0, 7.0, ALU.max, ALU.min))
            V.tensor_tensor(XQ4, XQ4, bc(TS[:, 0, :].unsqueeze(2), TT, NT, 128), ALU.mult).then_inc(sem("l2f_xq"), 1)
            dve.wait_ge(sem("l2f_t"), 1)
            V.tensor_copy(R[:, 768:896], PS[:, 3, 0:128]).then_inc(sem("l2f_ops"), 1)
            dve.wait_ge(sem("l2f_t"), 2)
            V.tensor_copy(R[:, 896:896 + T], bank(4)).then_inc(sem("l2f_ops"), 1)
            dve.wait_ge(sem("l2f_y"), 1)
            V.tensor_tensor(X, X, bank(5), ALU.add).then_inc(sem("x_ready"), 1)

        ST = 64
        VEC = sb("VEC", [128, 2])
        GD = sb("GD", [128, 4])

        def l3a_pe(pe):
            norm_pe(pe, "l3a", X, x_is(9))
            normed(pe, "l3a")
            mm(bank(2), w("l3a_shift"), Y[:, :]).then_inc(sem("l3a_p"), 1)
            norm_pe(pe, "l3a_1", Z[:, :], (sem("l3a_xs"), 1))
            normed(pe, "l3a_1")
            mm(bank(3, T, ST), w("l3a_key"), Z[:, :]).then_inc(sem("l3a_p"), 1)
            mm(bank(4, T, ST), w("l3a_value"), Z[:, :]).then_inc(sem("l3a_p"), 1)
            pe.wait_ge(sem("l3a_states"), 1)
            mm(bank(5), w("l3a_out", p=ST), R[0:ST, 2 * T:3 * T]).then_inc(sem("l3a_p"), 1)

        def l3a_act(act):
            A.activation(GD[:, 0:1], w("l3a_gate"), ACT.Sigmoid).then_inc(sem("l3a_vecs"), 1)
            A.activation(GD[0:ST, 2:3], w("l3a_first", p=ST), ACT.Exp).then_inc(sem("l3a_vecs"), 1)
            A.activation(GD[0:ST, 3:4], w("l3a_decay", p=ST), ACT.Exp).then_inc(sem("l3a_vecs"), 1)
            norm_act(act, "l3a", X, 1e-5)
            norm_act(act, "l3a_1", None, 1e-5)
            act.wait_ge(sem("l3a_p"), 2)
            A.activation(R[0:ST, 0:T], bank(3, T, ST), ACT.Sigmoid).then_inc(sem("l3a_sig"), 1)
            act.wait_ge(sem("l3a_sig"), 1)
            act.wait_ge(sem("l3a_neg"), 1)
            A.activation(R[0:ST, 0:T], R[0:ST, 0:T], ACT.Exp, scale=VEC[0:ST, 0:1]).then_inc(sem("l3a_sig"), 1)

        def l3a_dve(dve):
            norm_dve(dve, "l3a", X, Y[:, :])
            dve.wait_ge(sem("l3a_vecs"), 3)
            V.tensor_scalar(VEC[0:ST, 0:1], GD[0:ST, 2:3], -1.0, None, ALU.mult).then_inc(sem("l3a_neg"), 1)
            link(dve, "dve_chain", V.tensor_scalar(GD[:, 1:2], GD[:, 0:1], -1.0, 1.0, ALU.mult, ALU.add))
            V.tensor_scalar(R[0:ST, T:2 * T], w("reset", p=ST), GD[0:ST, 3:4], None, ALU.mult)
            link(dve, "dve_chain", V.tensor_scalar(Z[:, :], Y[:, :], GD[:, 1:2], None, ALU.mult))
            dve.wait_ge(sem("l3a_p"), 1)
            z, p = (a.rearrange("p (b h t) -> p b h t", b=B, h=2) for a in (Z[:, :], bank(2)))
            for h in range(2):
                last = V.scalar_tensor_tensor(z[:, :, h], p[:, :, 1 - h], GD[:, 0:1], z[:, :, h], ALU.mult, ALU.add)
            last.then_inc(sem("l3a_xs"), 1)
            norm_dve(dve, "l3a_1", Z[:, :], Z[:, :], w("l3a_g"), w("l3a_c"))
            dve.wait_ge(sem("l3a_p"), 3)
            dve.wait_ge(sem("l3a_sig"), 2)
            link(dve, "dve_chain", V.tensor_tensor(R[0:ST, 0:T], R[0:ST, 0:T], bank(4, T, ST), ALU.mult))
            V.tensor_tensor_scan(R[0:ST, 2 * T:3 * T], R[0:ST, T:2 * T], R[0:ST, 0:T], 0.0, ALU.mult, ALU.add
                                 ).then_inc(sem("l3a_states"), 1)
            dve.wait_ge(sem("l3a_p"), 4)
            V.tensor_tensor(X, X, bank(5), ALU.add).then_inc(sem("x_ready"), 1)

        def l3x_end_pe(pe):
            pe.wait_ge(sem("l3x_a"), 1)
            mm(bank(2), w("l3x_o"), Z[:, :]).then_inc(sem("l3x_y"), 1)

        def l3x_end_dve(dve):
            dve.wait_ge(sem("f_copied"), folds(2, B + 1))
            V.tensor_scalar(Z[:, :], AO[:, 1:, :].rearrange("p b t -> p (b t)"), w("l3x_bv"), None, ALU.add
                            ).then_inc(sem("l3x_a"), 1)
            dve.wait_ge(sem("l3x_y"), 1)
            V.scalar_tensor_tensor(X, bank(2), w("l3x_bo"), X, ALU.add, ALU.add).then_inc(sem("x_ready"), 1)

        def l3f_pe(pe):
            norm_pe(pe, "l3f", X, x_is(11))
            normed(pe, "l3f")
            router_pe(pe, "l3f", Y[:, :], "l3f_router")
            gates = [w("l3f_sg")] + [w("l3f_eg", n * 128, 128) for n in range(4)]
            ups = [w("l3f_su")] + [w("l3f_eu", n * 128, 128) for n in range(4)]
            downs = [w("l3f_sd")] + [w("l3f_ed", n * 128, 128) for n in range(4)]

            def down(n):
                pe.wait_ge(sem("l3f_h"), n + 1)
                mm(bank(0), downs[n], r(2 * (n % 2)), n == 0, n == 4).then_inc(sem("l3f_dn"), 1)

            for n in range(5):
                if n == 1:
                    to_experts_pe(pe, "l3f", (6,))
                    pe.wait_ge(sem("router_cf"), ROUTER_AT["l3f"])
                if n >= 2:
                    pe.wait_ge(sem("l3f_h"), n - 1)
                s = 2 if n % 2 else 5
                mm(bank(s), gates[n], Y[:, :]).then_inc(sem("l3f_g"), 1)
                last = mm(bank(s + 1), ups[n], Y[:, :])
                if n:
                    for k in range(2):
                        last = mm(PS[64 * k:64 * k + 64, s + 2, 0:T], bc(w("ident", 2 * n - 2 + k, 1, 8), 8, 64), CF[:, :])
                last.then_inc(sem("l3f_u"), 1)
                if n:
                    down(n - 1)
            down(4)

        def l3f_act(act):
            norm_act(act, "l3f", X, 1e-5)
            softmax_act(act, "l3f")
            for n in range(5):
                act.wait_ge(sem("l3f_g"), n + 1)
                if n >= 2:
                    act.wait_ge(sem("l3f_dn"), n - 1)
                A.activation(r(2 * (n % 2)), bank(2 if n % 2 else 5), ACT.Silu).then_inc(sem("l3f_silu"), 1)

        def l3f_dve(dve):
            norm_dve(dve, "l3f", X, Y[:, :])
            softmax_dve(dve, "l3f", True)
            link(dve, "dve_chain", V.tensor_tensor(TK[:, 1], TK[:, 1], col(1), ALU.mult))
            link(dve, "dve_chain", V.tensor_tensor(TK[:, 2], TK[:, 2], TK[:, 3], ALU.add))
            V.tensor_tensor(TK[:, 6], TK[:, 1], TK[:, 2], ALU.mult).then_inc(sem("router_route"), 1)

            def hidden(n):
                h, s = r(2 * (n % 2)), 2 if n % 2 else 5
                dve.wait_ge(sem("l3f_silu"), n + 1)
                dve.wait_ge(sem("l3f_u"), n + 1)
                if n:
                    link(dve, "dve_chain", V.tensor_tensor(h, h, bank(s + 1), ALU.mult))
                    V.tensor_tensor(h, h, bank(s + 2), ALU.mult).then_inc(sem("l3f_h"), 1)
                else:
                    V.tensor_tensor(h, h, bank(s + 1), ALU.mult).then_inc(sem("l3f_h"), 1)

            hidden(0)
            dve.wait_ge(sem("router_byexp"), ROUTER_AT["l3f"])
            V.tensor_copy(CF[:, :], bank(2, T, 8)).then_inc(sem("router_cf"), 1)
            for n in range(1, 5):
                hidden(n)
            dve.wait_ge(sem("l3f_dn"), 5)
            V.tensor_tensor(X, X, bank(0), ALU.add).then_inc(sem("x_ready"), 1)

        KT32 = VA[:, 0, 0:2 * B * KJ].bitcast(i32)
        R16 = R[0:8, SK:2 * SK].bitcast(f16).rearrange("p (v k) -> p v k", v=2)

        @block.sync
        def _(sp):
            half = AT["l1a_q"][0]
            sp.dma_start(W[:, 0:half], small[:, 0:half]).then_inc(sem("small_in"), 16)
            sp.dma_start(W[:, half:], small[:, half:]).then_inc(sem("small_in"), 16)
            sp.dma_start(R[0:8, 0:SK].bitcast(i32), mrow).then_inc(sem("mask_in"), 16)
            sp.dma_start(KT32, mcol).then_inc(sem("mask_in"), 16)
            for n in range(2):
                sp.dma_start(ROPE_K[:, n * SK:(n + 1) * SK], rope[:, n * SK:(n + 1) * SK]).then_inc(sem("rope_in"), 16)
            sp.dma_start(ROPE_Q[:, :, :], rope[:, 2 * SK:2 * SK + 2 * S].rearrange("p (a t) -> p a t", a=2)
                         ).then_inc(sem("rope_in"), 16)
            for n in range(6):
                sp.dma_start(WB[:, n * 2048:(n + 1) * 2048], big0[:, n * 2048:(n + 1) * 2048]
                             ).then_inc(sem("big0_in"), 16)
            for v in range(2):
                sp.wait_ge(sem("mask_rows"), v + 1)
            sp.dma_start(mscr.rearrange("v b k -> b v k"), R16).then_inc(sem("mask_out"), 16)
            sp.wait_ge(sem("mask_out"), 16)
            if LAYERS > 1:
                x_sp(sp, 0)
            if LAYERS > 5:
                sp.wait_ge(*x_is(3))
                for n in (2, 3, 4, 5, 0, 1):
                    sp.dma_start(WB[:, n * 2048:(n + 1) * 2048],
                                 big1[:, n * 2048:(n + 1) * 2048]).then_inc(sem("big1_in"), 16)
            if LAYERS > 7:
                x_sp(sp, 1)
            if LAYERS > 10:
                x_sp(sp, 2)
            sp.wait_ge(*x_is(LAYERS))
            sp.dma_start(out, X).then_inc(sem("out_written"), 16)
            sp.wait_ge(sem("out_written"), 16)

        @block.gpsimd
        def _(pool):
            for ap, value in ((SEL96[:, :], 0.0), (ONE16[:, :], 1.0), (QS[:, :, :], 0.0), (PH[:, :, :, :], 1.0),
                              (PL[:, :, :, :], 0.0), (OM[:, 1, :, :], 0.0)):
                link(pool, "pool_chain", G.memset(ap, value))
            G.memset(SEL96[:, 96:97], 1.0).then_inc(sem("sel_ready"), 1)
            pool.wait_ge(sem("sel_ready"), 1)
            pool.sem_inc(sem("pool_ready"), 1)
            pool.sem_inc(sem("om_ready"), 1)
            pool.sem_inc(sem("qs_clear"), 1)
            pool_layers = [l0a_pool, lambda e: x_pool(e, 0), l0f_pool, None, None, None, None,
                           lambda e: x_pool(e, 1), None, None, lambda e: x_pool(e, 2), None]
            for layer in pool_layers[:LAYERS]:
                if layer:
                    layer(pool)

        @block.vector
        def _(dve):
            dve.sem_inc(sem("m_done"), 2)
            dve.sem_inc(sem("l_ready"), 2)
            dve.wait_ge(sem("small_in"), 32)
            dve.sem_inc(sem("x_ready"), 1)
            V.tensor_copy(IDH[:, :], IDN)
            dve.wait_ge(sem("mask_in"), 32)
            V.tensor_scalar(R16[:, 0, :], R[0:8, 0:SK].bitcast(i32), 0.0, -BIG, ALU.is_gt, ALU.mult
                            ).then_inc(sem("mask_rows"), 1)
            V.tensor_scalar(R16[:, 1, :], R[0:8, 0:SK].bitcast(i32), 0.0, -BIG, ALU.is_equal, ALU.mult
                            ).then_inc(sem("mask_rows"), 1)
            cols = KT32.rearrange("p (b j) -> p b j", b=B)
            V.memset(VALID[:, 0], 1.0)
            V.tensor_scalar(VALID[:, 1], cols, 0.0, None, ALU.is_le)
            V.tensor_scalar(VALID[:, 2], cols, 0.0, None, ALU.not_equal).then_inc(sem("valid_ready"), 1)
            dve.wait_ge(sem("valid_ready"), 1)
            dve.wait_ge(sem("mask_out"), 16)
            for layer in (l0a_dve, lambda e: (x_dve(e, 0), l0x_end_dve(e)), l0f_dve, l1a_dve, l1x_dve, l1f_dve,
                          l2a_dve, lambda e: (x_dve(e, 1), l2x_end_dve(e)), l2f_dve, l3a_dve,
                          lambda e: (x_dve(e, 2), l3x_end_dve(e)), l3f_dve)[:LAYERS]:
                layer(dve)

        @block.scalar
        def _(act):
            act.sem_inc(sem("e_ready"), 3)
            A.preload_act_table_set("natural_log_exp_and_others")
            act.wait_ge(*x_is(0))
            for layer in (l0a_act, lambda e: x_act(e, 0), l0f_act, l1a_act, l1x_act, l1f_act, l2a_act,
                          lambda e: x_act(e, 1), l2f_act, l3a_act, lambda e: x_act(e, 2), l3f_act)[:LAYERS]:
                layer(act)

        @block.tensor
        def _(pe):
            pe.sem_inc(sem("s_ready"), CLEAR)
            pe.sem_inc(sem("p_ready"), 4)
            for layer in (l0a_pe, lambda e: (x_pe(e, 0), l0x_end_pe(e)), l0f_pe, l1a_pe, l1x_pe, l1f_pe, l2a_pe,
                          lambda e: x_pe(e, 1), l2f_pe, l3a_pe, lambda e: (x_pe(e, 2), l3x_end_pe(e)),
                          l3f_pe)[:LAYERS]:
                layer(pe)


LAYERS = 12


def constants():
    c = {}
    eye = np.eye(128, dtype=np.float32)
    c["ident"] = eye
    c["mean"] = np.full((128, 128), 1 / 128, np.float32)
    c["ones"] = np.ones((128, 128), np.float32)
    c["half"] = np.kron(np.eye(2), np.ones((64, 64))).astype(np.float32)
    row = np.arange(128)
    c["fold"] = (row[:, None] % SP2 == np.arange(S)[None]).astype(np.float32)
    c["blk8"] = (row[:, None] // SP2 == np.arange(16)[None] // 8).astype(np.float32)
    c["blk16"] = (row[:, None] // SP2 == np.arange(32)[None] // 16).astype(np.float32)
    c["headmask"] = (row[:, None] // 8 == np.arange(16)[None]).astype(np.float32)
    q = row[:, None] % SP2
    c["causal"] = np.where((np.arange(S)[None] > q) & (q < S), -1e9, 0).astype(np.float32)
    c["iota"] = np.tile(np.arange(8, dtype=np.float32), (128, 1))
    c["reset"] = np.tile((np.arange(T) % S != 0).astype(np.float32), (128, 1))
    t, s = row[:, None], np.arange(TT)[None]
    same, near = t // S == s // S, t // 7 == s // 7
    c["inlow"] = -((t > s) & near).astype(np.float32)
    c["inup"] = -((t < s) & near).astype(np.float32)
    c["offlow"] = -((t > s) & same & ~near).astype(np.float32)
    c["upper"] = ((t <= s) & same).astype(np.float32)
    h = np.array([[1.0]])
    while h.shape[0] < 128:
        h = np.block([[h, h], [h, -h]])
    c["hadamard"] = (h / np.sqrt(128)).astype(np.float32)
    return c


def rope_tables():
    half = np.arange(0, 16, 2, dtype=np.float32) / np.float32(16)
    inv = np.float32(1.0) / np.float32(10000.0) ** half
    pos = np.arange(SK, dtype=np.float32)
    freqs = pos[:, None] * inv
    emb = np.concatenate([freqs, freqs], -1)
    sign = np.where(np.arange(16) < 8, -1, 1).astype(np.float32)
    cos, sin = np.cos(emb).T, np.sin(emb).T * sign[:, None]
    order = (np.arange(KP)[None, :] * KJ + np.arange(KJ)[:, None]).reshape(-1)
    parts = [cos[:, order], sin[:, order], cos[:, :S], sin[:, :S]]
    return np.ascontiguousarray(np.concatenate([np.tile(a, (8, 1)) for a in parts], 1), dtype=np.float32)


def kernel(**inputs):
    import concourse.bacc as bacc
    from concourse.bass_utils import run_bass_kernel_spmd

    a = {k: np.asarray(v) for k, v in inputs.items()}
    pieces = dict(constants())

    def vec(v):
        v = v.reshape(-1)
        if v.size < 128:
            return np.concatenate([v, np.zeros(128 - v.size, v.dtype)]).reshape(128, 1)
        return v.reshape(-1, 128).T

    def rows(m):
        return np.concatenate([m, np.zeros((128 - m.shape[0], m.shape[1]), m.dtype)], 0)

    def tall(m):
        return m.reshape(-1, 128, m.shape[-1]).transpose(1, 0, 2).reshape(128, -1)

    swap = np.arange(128).reshape(8, 2, 8)[:, ::-1].reshape(-1)
    p = pieces
    p["x"] = a["x"].transpose(2, 0, 1).reshape(128, T)
    wi = a["L0_attn_in_proj_w"].T
    p["l0a_q"], p["l0a_k"], p["l0a_v"] = wi[:, 0:128], wi[:, 128:256], wi[:, 256:384]
    p["l0a_out"], p["l0a_w1"], p["l0a_w2"] = a["L0_attn_out_w"].T, a["L0_attn_lin1_w"].T, tall(a["L0_attn_lin2_w"].T)
    bi = a["L0_attn_in_proj_b"]
    p["l0a_bq"], p["l0a_bk"], p["row_bv"] = vec(bi[0:128]), vec(bi[128:256]), rows(bi[None, 256:384])
    p["l0a_bout"], p["l0a_b1"], p["l0a_b2"] = (vec(a["L0_attn_" + n]) for n in ("out_b", "lin1_b", "lin2_b"))
    p["l0a_g1"], p["l0a_c1"], p["l0a_g2"], p["l0a_c2"] = (vec(a["L0_attn_ln" + n]) for n in ("1_g", "1_b", "2_g", "2_b"))
    wq, wkv = a["L0_xattn_Wq"].T, a["L0_xattn_Wkv"].T
    p["l0x_q"], p["l0x_qr"], p["l0x_k"], p["l0x_kr"] = wq, wq[:, swap], wkv[:, 0:128], wkv[:, 0:128][:, swap]
    p["l0x_v"], p["l0x_out"] = wkv[:, 128:256], a["L0_xattn_Wout"].T
    p["l0f_gate"], p["row_gb"] = a["L0_ffn_gate_w"], rows(a["L0_ffn_gate_b"][None])
    p["l0f_b1"], p["l0f_b2"] = vec(a["L0_ffn_b1"]), rows(a["L0_ffn_b2"])
    p["l0f_g"], p["l0f_c"] = vec(a["L0_ffn_ln_g"]), vec(a["L0_ffn_ln_b"])
    p["l0f_qs"], p["l0f_ks"] = vec(a["L0_ffn_q_scale"]), vec(a["L0_ffn_k_scale"])
    p["l1a_q"], p["l1a_k"], p["l1a_v"], p["l1a_o"] = (a["L1_attn_W" + n] for n in "qkvo")
    p["l1a_beta"] = np.broadcast_to(a["L1_attn_beta_w"], (128, 128))
    p["l1a_bb"] = np.broadcast_to(a["L1_attn_beta_b"].reshape(1, 1), (128, 1))
    p["l1a_gate"], p["l1a_up"], p["l1a_down"] = a["L1_attn_w_gate"], a["L1_attn_w_up"], tall(a["L1_attn_w_down"])
    p["l1a_n1"], p["l1a_n2"], p["l1a_alpha"] = (vec(a["L1_attn_" + n]) for n in ("norm1_w", "norm2_w", "alpha_logit"))
    p["l1f_g"], p["l1f_b1"], p["l1f_b2"] = a["L1_ffn_Wg"], vec(a["L1_ffn_b1"]), rows(a["L1_ffn_b2"])
    p["l2a_in"], p["l2a_dt"], p["l2a_out"] = a["L2_attn_W_in"].T, tall(a["L2_attn_W_dt"].T), tall(a["L2_attn_W_out"].T)
    p["l2a_n"], p["l2a_bdt"] = vec(a["L2_attn_w_norm"]), vec(a["L2_attn_b_dt"])
    for n in "qkv":
        p["l2x_" + n], p["l2x_b" + n] = a[f"L2_xattn_{n}_w"].T, vec(a[f"L2_xattn_{n}_b"])
        p["l3x_" + n], p["l3x_b" + n] = a["L3_xattn_W" + n], vec(a["L3_xattn_b" + n])
    p["l3x_o"], p["l3x_bo"] = a["L3_xattn_Wo"], vec(a["L3_xattn_bo"])
    p["l2f_w"] = a["L2_ffn_weight"]
    p["l3a_key"], p["l3a_value"], p["l3a_out"] = a["L3_attn_W_key"].T, a["L3_attn_W_value"].T, rows(a["L3_attn_W_output"].T)
    p["l3a_shift"] = a["L3_attn_W_shift"].T
    p["l3a_decay"], p["l3a_first"], p["l3a_gate"] = (vec(a["L3_attn_" + n]) for n in ("time_decay", "time_first", "shift_gate"))
    p["l3a_g"], p["l3a_c"] = vec(a["L3_attn_ln_w"]), vec(a["L3_attn_ln_b"])
    p["l3f_router"] = a["L3_ffn_router"]
    p["l3f_eg"] = a["L3_ffn_experts_gate"].transpose(1, 0, 2).reshape(128, 512)
    p["l3f_eu"] = a["L3_ffn_experts_up"].transpose(1, 0, 2).reshape(128, 512)
    p["l3f_ed"] = tall(a["L3_ffn_experts_down"].reshape(512, 128))
    p["l3f_sg"], p["l3f_su"], p["l3f_sd"] = (a["L3_ffn_shared_" + n] for n in ("gate", "up", "down"))
    small = np.ascontiguousarray(np.concatenate([p[name] for name, _ in SMALL], 1))

    def experts(n):
        w1 = a[f"{n}_w1" if n == "L0_ffn" else f"{n}_W1"].transpose(1, 0, 2).reshape(128, E * F)
        w2 = a[f"{n}_w2" if n == "L0_ffn" else f"{n}_W2"].reshape(E * F, 128)
        return [w1, tall(w2)]

    big0 = np.ascontiguousarray(np.concatenate(
        [a["L0_ffn_Wq"], a["L0_ffn_Wk"], a["L0_ffn_Wv"], tall(a["L0_ffn_Wo"])] + experts("L0_ffn"), 1))
    late = [p[name] for name, _ in LATE]
    big1 = np.ascontiguousarray(np.concatenate(late + experts("L1_ffn"), 1))
    mask = a["mask_BxS2_ik0"].reshape(B, KP, KJ)
    arrays = {
        "small": small, "big0": big0, "big1": big1, "ctx": np.ascontiguousarray(a["ctx_1024"]),
        "mrow": np.ascontiguousarray(mask.transpose(0, 2, 1).reshape(B, SK)),
        "mcol": np.ascontiguousarray(mask.transpose(1, 0, 2).reshape(KP, B * KJ)), "rope": rope_tables(),
    }
    nc = bacc.Bacc("TRN2", target_bir_lowering=False, num_devices=1)
    args = [nc.dram_tensor(k, v.shape, mybir.dt.from_np(v.dtype), kind="ExternalInput").ap() for k, v in arrays.items()]
    out = nc.dram_tensor("out", (128, T), mybir.dt.float32, kind="ExternalOutput").ap()
    f16 = mybir.dt.float16
    scratch = [nc.dram_tensor("k_halves", (2, 128, 2, SK), f16).ap(), nc.dram_tensor("q_halves", (128, 2, T), f16).ap(),
               nc.dram_tensor("mask_rows_dram", (2, B, SK), f16).ap(),
               nc.dram_tensor("ctx_features", (B, D, SK), mybir.dt.float32).ap()]
    build(nc, *args, out, scratch)
    got = run_bass_kernel_spmd(nc, [arrays], core_ids=[0]).results[0]["out"]
    return np.ascontiguousarray(got.reshape(128, B, S).transpose(1, 2, 0))
```

```python
import concourse.bass as bass
from concourse import mybir
from contextlib import ExitStack
import math
import numpy as np

B, S, D = 8, 56, 128
T = B * S
SK = 1500
KP, KJ = 125, 12
E, F = 8, 512
FC = F // 128
TT, NT = 112, 4
SP2 = 64
ONE_ONE = float(np.array([1, 1], np.float16).view(np.float32)[0])
BIG = 60000.0

SMALL = [
    ("x", T), ("mean", 128),
    ("ident", 128), ("ones", 128), ("half", 128),
    ("fold", S), ("blk8", 16), ("blk16", 32), ("headmask", 16), ("causal", S),
    ("iota", 8), ("reset", T), ("inlow", TT), ("inup", TT), ("offlow", TT), ("upper", TT),
    ("hadamard", 128),
    ("l0a_q", 128), ("l0a_k", 128), ("l0a_v", 128), ("l0a_out", 128), ("l0a_w1", F), ("l0a_w2", F),
    ("l0x_q", 128), ("l0x_qr", 128), ("l0x_k", 128), ("l0x_kr", 128), ("l0x_v", 128), ("l0x_out", 128),
    ("l0f_gate", 8), ("l0f_b1", E * FC),
    ("l0a_bq", 1), ("l0a_bk", 1), ("l0a_bout", 1), ("l0a_b1", FC), ("l0a_b2", 1),
    ("l0a_g1", 1), ("l0a_c1", 1), ("l0a_g2", 1), ("l0a_c2", 1),
    ("l0f_g", 1), ("l0f_c", 1), ("l0f_qs", 8), ("l0f_ks", 8),
    ("l1a_n1", 1), ("l1a_n2", 1), ("l1a_bb", 1), ("l1a_alpha", 1),
    ("l2a_n", 1), ("l2a_bdt", 2), ("l2x_bq", 1), ("l2x_bk", 1), ("l2x_bv", 1),
    ("l3a_decay", 1), ("l3a_first", 1), ("l3a_gate", 1), ("l3a_g", 1), ("l3a_c", 1),
    ("l3x_bq", 1), ("l3x_bk", 1), ("l3x_bv", 1), ("l3x_bo", 1),
    ("row_bv", 128), ("row_gb", 8), ("l0f_b2", 128), ("l1f_b2", 128),
    ("l1a_q", 128), ("l1a_k", 128), ("l1a_v", 128), ("l1a_beta", 128), ("l1a_o", 128),
    ("l1a_gate", 256), ("l1a_up", 256), ("l1a_down", 256),
    ("l1f_g", 8), ("l1f_b1", E * FC),
    ("l2f_w", 128), ("l2x_k", 128), ("l3f_sd", 128), ("l3f_router", 8), ("l3x_o", 128),
]
LATE = [
    ("l2a_in", 512), ("l2a_dt", 512), ("l2a_out", 256), ("l2x_q", 128), ("l2x_v", 128),
    ("l3a_key", 64), ("l3a_value", 64), ("l3a_out", 128), ("l3a_shift", 128),
    ("l3x_q", 128), ("l3x_k", 128), ("l3x_v", 128),
    ("l3f_eg", 512), ("l3f_eu", 512), ("l3f_ed", 512), ("l3f_sg", 128), ("l3f_su", 128),
]
LATE_AT, _at = {}, 0
for _name, _n in LATE:
    LATE_AT[_name] = (_at, _n)
    _at += _n
assert _at == 4096
AT, NSMALL = {}, 0
for _name, _n in SMALL:
    AT[_name] = (NSMALL, _n)
    NSMALL += _n
BIG0 = [("wq", 1024), ("wk", 1024), ("wv", 1024), ("wo", 1024), ("w1", E * F), ("w2", E * F)]
NBIG = sum(n for _, n in BIG0)

XL = [
    dict(name="l0x", hd=16, G=4, R=32, K1=128, K2=128, halves=1, rope=True, scale=0.25, valid=0),
    dict(name="l2x", hd=8, G=8, R=16, K1=65, K2=97, halves=2, rope=False, scale=1 / math.sqrt(8), valid=1),
    dict(name="l3x", hd=8, G=8, R=16, K1=65, K2=97, halves=2, rope=False, scale=8 ** -0.5, valid=2),
]
MASKROW = 64


ROPE_PLAN = "V0 F0|V1|V2|T0|T1|T2|K0 R0|K1 R1|K2 R2|G0|DG0||SH0"
PLAIN_PLAN = "V0 F0|V1|V2|K0|K1|K2|||||DG0 DG1||SH0 SH1"


def slots(cfg):
    two = cfg["halves"] == 2
    plan = [[(use[:-1], int(use[-1])) for use in slot.split()]
            for slot in (ROPE_PLAN if cfg["rope"] else PLAIN_PLAN).split("|")]
    out = []
    for s in range(KJ):
        scores = [2 * s, 2 * s + 1] if two else [s]
        if two:
            maxima = list(range(24 * (s - 1) // 9, 24 * s // 9)) if 1 <= s <= 9 else []
        else:
            maxima = [2 * (s - 4) + k for k in range(2)] if 4 <= s <= 9 else []
        out.append((scores, maxima, plan[s]))
    out.append(([], [], plan[KJ]))
    return out


def short_banks(cfg):
    order = [use for _, _, other in slots(cfg) for use in other if use[0] != "DG"]
    return {use: (7, 2)[n % 2] for n, use in enumerate(order)}


class Count:

    def __init__(self, *per):
        self.per = per

    def at(self, L, b, k=0):
        return b * self.per[L] + (B * sum(self.per[:L]) + k)


UNITS = Count(KJ, 2 * KJ, 2 * KJ)
MAXES = Count(12, 24, 24)
ONE, THREE, SHIFTS = Count(1, 1, 1), Count(3, 3, 3), Count(1, 2, 2)
LOW_ON_DVE = (range(12), (18, 20, 22), (18, 20, 22))
LOW = {"d": Count(*(len(n) for n in LOW_ON_DVE)),
       "p": Count(*(KJ * c["halves"] - len(n) for c, n in zip(XL, LOW_ON_DVE)))}
MAX_BANKS, SCORE_BANKS = (0, 1, 5), (3, 4)
LAG = 3
KUSES = Count(6, 3, 3)


NORMS = [("l0a", 1), ("l0a_1", 1), ("l0a_2", 1), ("l0x", 1), ("l0f", 1), ("l0f_1", 1), ("l0f_2", 1), ("l0f_3", 1),
         ("l1a", 1), ("l1a_1", 0), ("l1a_2", 0), ("l1x", 1), ("l1f", 1), ("l2a", 1), ("l2a_1", 0), ("l2x", 1),
         ("l2f", 1), ("l3a", 1), ("l3a_1", 1), ("l3x", 1), ("l3f", 1)]
NORM_AT = {name: 2 * (n + 1) for n, (name, _) in enumerate(NORMS)}
MEAN_AT = {name: 2 * sum(c for _, c in NORMS[:n + 1]) for n, (name, _) in enumerate(NORMS)}


def build(nc, small, big0, big1, ctx, mrow, mcol, rope, out, scratch):
    f32, f16 = mybir.dt.float32, mybir.dt.float16
    i32, u32 = mybir.dt.int32, mybir.dt.uint32
    ALU, ACT, AX = mybir.AluOpType, mybir.ActivationFunctionType, mybir.AxisListType
    kscr, qscr, mscr, cscr = scratch
    es = ExitStack()
    with es:
        def sb(name, shape, dt=f32):
            return es.enter_context(nc.sbuf_tensor(name, shape, dt))

        made = {}

        def sem(name):
            if name not in made:
                made[name] = es.enter_context(nc.semaphore(name))
            return made[name]

        W = sb("W", [128, NSMALL])
        WB = sb("WB", [128, NBIG])

        def w(name, a=0, n=None, p=128, p0=0):
            o, m = LATE_AT[name] if name in LATE_AT else AT[name]
            return (WB if name in LATE_AT else W)[p0:p, o + a:o + a + (m - a if n is None else n)]

        BAT, _o = {}, 0
        for _n, _m in BIG0:
            BAT[_n] = _o
            _o += _m

        def wb(name, a, n):
            return WB[:, BAT[name] + a:BAT[name] + a + n]

        X = w("x")
        IDN = w("ident")
        Y = sb("Y", [128, T])
        Z = sb("Z", [128, T])
        XC = sb("XC", [128, T])
        SQ = sb("SQ", [128, T])
        RS = sb("RS", [128, T])
        KS = sb("KS", [128, 2, 12000 + 288], f16)
        KS32 = KS[:, :, :].rearrange("p a n -> p (a n)").bitcast(f32)
        R = sb("R", [128, 2 * KJ * D + 2 * SK + SK])
        CT = R[0:KP, 0:2 * KJ * D].rearrange("p (a j d) -> p a j d", a=2, j=KJ)
        KHL = R[:, 2 * KJ * D:2 * KJ * D + 2 * SK].bitcast(f16).rearrange(
            "p (a h n) -> p a h n", a=2, h=2)
        CTH = R[:, 2 * KJ * D + 2 * SK:].bitcast(f16).rearrange("p (h n) -> p h n", h=2)
        VA = sb("VA", [KP, 2, KJ * 264], f16)
        QS = sb("QS", [128, 2, 1024], f16)
        QH = sb("QH", [128, 2, T], f16)
        PH = sb("PH", [KP, 4, 8, SP2], f16)
        PL = sb("PL", [KP, 4, 8, SP2], f16)
        PR = (XC, SQ)
        MX = sb("MX", [128, 2, 24])
        MM = sb("MM", [128, 2, 8])
        DG = sb("DG", [128, 1024], f16)
        RD = sb("RD", [128, 2, 8])
        OM = sb("OM", [128, 2, 2, 128])
        VC = sb("VC", [KP, 2, KJ])
        VALID = sb("VALID", [KP, 3, B, KJ])
        AO = sb("AO", [128, 1 + B, S])
        GC = sb("GC", [128, B, 128])
        SEL96 = sb("SEL96", [128, 128], f16)
        ONE16 = sb("ONE16", [128, KP], f16)
        IDH = sb("IDH", [128, 128], f16)
        PS = es.enter_context(nc.psum_tensor("PS", [128, 8, 512], f32))

        def max_bank(c):
            return MAX_BANKS[c % len(MAX_BANKS)]

        def score_bank(m):
            return SCORE_BANKS[m % len(SCORE_BANKS)]

        def bank(n, cols=T, p=128):
            return PS[0:p, n, 0:cols]

        chains = {}

        def link(eng, name, ins):
            chains[name] = chains.get(name, 0) + 1
            ins.then_inc(sem(name), 1)
            eng.wait_ge(sem(name), chains[name])

        def mark(name, ins):
            chains[name] = chains.get(name, 0) + 1
            ins.then_inc(sem(name), 1)
            return chains[name]

        def one(i):
            return bass.ds(i, 1)

        def bc(ap, *shape):
            return ap.broadcast_to(list(shape))

        block = es.enter_context(nc.Block())
        V, A, G, PE = nc.vector, nc.scalar, nc.gpsimd, nc.tensor

        def mm(out_, l, r, start=True, stop=True, skip=False):
            return PE.matmul(out_, l, r, start=start, stop=stop, skip_group_check=skip)

        CLEAR = 1

        def half(ap, h):
            return ap[:, h * (T // 2):(h + 1) * (T // 2)]

        def at(values, name, h):
            return values[name] - 1 + h

        def norm_pe(pe, name, src, ready):
            if dict(NORMS)[name]:
                pe.wait_ge(*ready)
                for h in range(2):
                    mm(bank(h, T // 2), w("mean"), half(src, h)).then_inc(sem("mean_ready"), 1)
            for h in range(2):
                pe.wait_ge(sem("square_ready"), at(NORM_AT, name, h))
                mm(bank(h, T // 2), w("mean"), half(SQ, h)).then_inc(sem("var_ready"), 1)

        def ln_exp():
            A.preload_act_table_set("natural_log_exp_and_others")

        def norm_act(act, name, src, eps, ready=None):
            ln_exp()
            for h in range(2):
                if dict(NORMS)[name]:
                    act.wait_ge(sem("centred"), at(MEAN_AT, name, h))
                    A.activation(half(SQ, h), half(XC, h), ACT.Square).then_inc(sem("square_ready"), 1)
                else:
                    act.wait_ge(*ready)
                    A.activation(half(SQ, h), half(src, h), ACT.Square).then_inc(sem("square_ready"), 1)
            logs = []
            for h in range(2):
                act.wait_ge(sem("var_ready"), at(NORM_AT, name, h))
                logs.append(mark("act_chain", A.activation(half(RS, h), bank(h, T // 2), ACT.Ln, bias=eps)))
            for h in range(2):
                act.wait_ge(sem("act_chain"), logs[h])
                A.activation(half(RS, h), half(RS, h), ACT.Exp, scale=-0.5).then_inc(sem("rstd_ready"), 1)

        def norm_dve(dve, name, src, dst, gain=None, shift=None):
            if dict(NORMS)[name]:
                for h in range(2):
                    dve.wait_ge(sem("mean_ready"), at(MEAN_AT, name, h))
                    V.tensor_tensor(half(XC, h), half(src, h), bank(h, T // 2), ALU.subtract
                                    ).then_inc(sem("centred"), 1)
                src = XC
            scaled = []
            for h in range(2):
                dve.wait_ge(sem("rstd_ready"), at(NORM_AT, name, h))
                if gain is None:
                    V.tensor_tensor(half(dst, h), half(src, h), half(RS, h), ALU.mult).then_inc(sem("norm_ready"), 1)
                elif shift is None:
                    V.scalar_tensor_tensor(half(dst, h), half(src, h), gain, half(RS, h), ALU.mult, ALU.mult
                                           ).then_inc(sem("norm_ready"), 1)
                else:
                    scaled.append(mark("dve_chain", V.tensor_tensor(half(dst, h), half(src, h), half(RS, h), ALU.mult)))
            for h, done in enumerate(scaled):
                dve.wait_ge(sem("dve_chain"), done)
                V.tensor_scalar(half(dst, h), half(dst, h), gain, shift, ALU.mult, ALU.add
                                ).then_inc(sem("norm_ready"), 1)

        def normed(eng, name):
            eng.wait_ge(sem("norm_ready"), NORM_AT[name])

        def x_is(n):
            return sem("x_ready"), n + 1

        q0, k0, v0 = R[:, 0:T], R[:, T:2 * T], R[0:S, 2 * T:2 * T + 1024]
        QB = R[:, 1920:1920 + 1792].rearrange("p (a n) -> p a n", a=2)
        SM = R[:, 3712:3712 + 1792].rearrange("p (a n) -> p a n", a=2)
        VN = Z[0:S, 0:256].rearrange("p (a n) -> p a n", a=2)
        OG = R[0:S, 1920:1920 + 1024]
        H4 = R[:, 0:4 * T].rearrange("p (f t) -> p f t", f=FC)
        M16 = OM[0:S, 0, 0, 0:16]
        D16 = OM[0:S, 0, 0, 16:32]

        def l0a_pe(pe):
            norm_pe(pe, "l0a", X, x_is(0))
            normed(pe, "l0a")
            pe.wait_ge(sem("small_in"), 16)
            mm(bank(2), w("l0a_q"), Y[:, :]).then_inc(sem("l0a_proj"), 1)
            mm(bank(3), w("l0a_k"), Y[:, :]).then_inc(sem("l0a_proj"), 1)
            for b in range(B):
                dst = PS[0:S, 4 + b // 4, b % 4 * 128:b % 4 * 128 + 128]
                mm(dst, Y[:, b * S:(b + 1) * S], w("l0a_v"), True, False)
                last = mm(dst, w("ones", 0, S, 1), w("row_bv", 0, 128, 1), False, True)
            last.then_inc(sem("l0a_proj"), 1)

            def scores(b):
                pe.wait_ge(sem("l0a_qblk"), b + 1)
                pe.wait_ge(sem("l0a_kv"), 2)
                if b:
                    pe.wait_ge(sem("l0a_less"), b)
                for n in range(2):
                    last = mm(PS[0:S, 6 + n, 0:T], k0[:, b * S:(b + 1) * S], QB[:, b % 2, n * T:(n + 1) * T])
                last.then_inc(sem("l0a_scores"), 1)

            scores(0)
            for b in range(B):
                if b + 1 < B:
                    scores(b + 1)
                pe.wait_ge(sem("l0a_vn"), b + 1)
                for h in range(16):
                    last = mm(PS[0:S, 2 + b // 4, b % 4 * 128 + h * 8:b % 4 * 128 + h * 8 + 8],
                              SM[0:S, b % 2, h * S:(h + 1) * S], VN[:, b % 2, h * 8:h * 8 + 8])
                last.then_inc(sem("l0a_pv"), 1)
            pe.wait_ge(sem("l0a_gelu"), 2)
            for b in range(B):
                last = PE.transpose(PS[:, 4, b * S:(b + 1) * S], OG[:, b * 128:(b + 1) * 128], IDN[0:S, 0:S])
            last.then_inc(sem("l0a_ot"), 1)
            pe.wait_ge(sem("l0a_a"), 1)
            mm(bank(5), w("l0a_out"), R[:, 4000:4000 + T]).then_inc(sem("l0a_o"), 1)
            norm_pe(pe, "l0a_1", Z[:, :], (sem("l0a_z"), 1))
            normed(pe, "l0a_1")
            for f in range(FC):
                mm(bank((2, 3, 6, 7)[f]), w("l0a_w1", f * 128, 128), Y[:, :]).then_inc(sem("l0a_up"), 1)
            for f in range(FC):
                pe.wait_ge(sem("l0a_h"), f + 1)
                last = mm(bank(4), w("l0a_w2", f * 128, 128), H4[:, f, :], f == 0, f == FC - 1)
            last.then_inc(sem("l0a_down"), 1)
            norm_pe(pe, "l0a_2", Z[:, :], (sem("l0a_z"), 2))

        def l0a_act(act):
            norm_act(act, "l0a", X, 1e-5)
            act.wait_ge(sem("l0a_proj"), 2)
            A.activation(k0, bank(3), ACT.Identity, bias=w("l0a_bk")).then_inc(sem("l0a_kv"), 1)
            act.wait_ge(sem("l0a_proj"), 3)
            A.activation(v0.rearrange("p (a n) -> p a n", a=2), PS[0:S, 4:6, :], ACT.Copy).then_inc(sem("l0a_kv"), 1)
            for b in range(B):
                act.wait_ge(sem("l0a_less"), b + 1)
                A.activation(SM[0:S, b % 2, :], SM[0:S, b % 2, :], ACT.Exp).then_inc(sem("l0a_exp"), 1)
            act.wait_ge(sem("l0a_pv"), B)
            for n in range(2):
                A.activation(OG[:, n * 512:(n + 1) * 512], PS[0:S, 2 + n, :], ACT.Gelu).then_inc(sem("l0a_gelu"), 1)
            norm_act(act, "l0a_1", None, 1e-5)
            for f in range(FC):
                act.wait_ge(sem("l0a_up"), f + 1)
                A.activation(H4[:, f, :], bank((2, 3, 6, 7)[f]), ACT.Gelu, bias=w("l0a_b1", f, 1)
                             ).then_inc(sem("l0a_h"), 1)
            norm_act(act, "l0a_2", None, 1e-5)

        def l0a_pool(pool):
            pool.wait_ge(sem("l0a_q"), 1)
            for b in range(B):
                if b >= 2:
                    pool.wait_ge(sem("l0a_scores"), b - 1)
                G.tensor_tensor(QB[:, b % 2, :].rearrange("p (h t) -> p h t", h=16),
                                bc(q0[:, b * S:(b + 1) * S].unsqueeze(1), 128, 16, S),
                                bc(w("headmask").unsqueeze(2), 128, 16, S), ALU.mult).then_inc(sem("l0a_qblk"), 1)

        MROW = KS32[0:8, 0:SK].bitcast(i32)
        R16 = KS[0:8, 1, 0:2 * SK].rearrange("p (v k) -> p v k", v=2)
        KT32 = VA[:, 0, 0:2 * B * KJ].bitcast(i32)

        def masks_dve(dve):
            V.tensor_copy(IDH[:, :], IDN)
            dve.wait_ge(sem("mask_in"), 32)
            V.tensor_scalar(R16[:, 0, :], MROW, 0.0, -BIG, ALU.is_gt, ALU.mult).then_inc(sem("mask_rows"), 1)
            V.tensor_scalar(R16[:, 1, :], MROW, 0.0, -BIG, ALU.is_equal, ALU.mult).then_inc(sem("mask_rows"), 1)
            cols = KT32.rearrange("p (b j) -> p b j", b=B)
            V.memset(VALID[:, 0], 1.0)
            V.tensor_scalar(VALID[:, 1], cols, 0.0, None, ALU.is_le)
            link(dve, "dve_chain", V.tensor_scalar(VALID[:, 2], cols, 0.0, None, ALU.not_equal))

        def l0a_dve(dve):
            norm_dve(dve, "l0a", X, Y[:, :])
            dve.wait_ge(sem("l0a_proj"), 1)
            V.tensor_scalar(q0, bank(2), w("l0a_bq"), 1 / math.sqrt(8), ALU.add, ALU.mult).then_inc(sem("l0a_q"), 1)
            masks_dve(dve)

            def less(b):
                dve.wait_ge(sem("l0a_scores"), b + 1)
                ps = PS[0:S, 6:8, 0:T].rearrange("p a (h t) -> p a h t", h=8)
                link(dve, "dve_chain", V.tensor_reduce(M16.rearrange("p (a h) -> p a h", a=2), ps, AX.X, ALU.max))
                if b >= 2:
                    dve.wait_ge(sem("l0a_pv"), b - 1)
                V.tensor_tensor(SM[0:S, b % 2, :].rearrange("p (a h t) -> p a h t", a=2, h=8), ps,
                                bc(M16.rearrange("p (a h) -> p a h", a=2).unsqueeze(3), S, 2, 8, S),
                                ALU.subtract).then_inc(sem("l0a_less"), 1)

            less(0)
            for b in range(B):
                dve.wait_ge(sem("l0a_exp"), b + 1)
                if b:
                    dve.wait_ge(sem("l0a_vn"), b)
                link(dve, "dve_chain", V.tensor_reduce(
                    D16, SM[0:S, b % 2, :].rearrange("p (h t) -> p h t", h=16), AX.X, ALU.add))
                link(dve, "dve_chain", V.reciprocal(D16, D16))
                dve.wait_ge(sem("l0a_kv"), 2)
                V.tensor_tensor(VN[:, b % 2, :].rearrange("p (h d) -> p h d", h=16),
                                v0[:, b * 128:(b + 1) * 128].rearrange("p (h d) -> p h d", h=16),
                                bc(D16.unsqueeze(2), S, 16, 8), ALU.mult).then_inc(sem("l0a_vn"), 1)
                if b + 1 < B:
                    less(b + 1)
            dve.wait_ge(sem("l0a_ot"), 1)
            V.tensor_scalar(R[:, 4000:4000 + T], bank(4), 1 / math.sqrt(S), None, ALU.mult).then_inc(sem("l0a_a"), 1)
            dve.wait_ge(sem("l0a_o"), 1)
            V.scalar_tensor_tensor(Z[:, :], bank(5), w("l0a_bout"), Y[:, :], ALU.add, ALU.add).then_inc(sem("l0a_z"), 1)
            norm_dve(dve, "l0a_1", Z[:, :], Y[:, :], w("l0a_g1"), w("l0a_c1"))
            dve.wait_ge(sem("l0a_down"), 1)
            V.scalar_tensor_tensor(Z[:, :], bank(4), w("l0a_b2"), Y[:, :], ALU.add, ALU.add).then_inc(sem("l0a_z"), 1)
            norm_dve(dve, "l0a_2", Z[:, :], Z[:, :], w("l0a_g2"), w("l0a_c2"))
            normed(dve, "l0a_2")
            V.tensor_tensor(X, X, Z[:, :], ALU.add).then_inc(sem("x_ready"), 1)

        ROPE_K = KS[:, 0, 6144:6144 + 6000].bitcast(f32)
        ROPE_Q = sb("ROPE_Q", [128, 2, S])
        SR = sb("SR", [128, 2, 512], f16)
        KT = KS[:, 1, 6144:6144 + 6000].bitcast(f32).rearrange("p (c r n) -> p c r n", c=3, r=2)

        WS = [RS[:, 0:384].bitcast(f16).rearrange("p (m h n) -> p m h n", m=3, h=2)] + 2 * [
            SR[:, 0, :].rearrange("p (m h n) -> p m h n", m=2, h=2)]
        AHEAD = (1, 6, 9)

        def split_weights(dve, L):
            for m, name in enumerate(("_k", "_v") if L else ("_k", "_v", "_kr")):
                weights = w(XL[L]["name"] + name)
                link(dve, "dve_chain", V.tensor_copy(WS[L][:, m, 0, :], weights))
                last = V.tensor_tensor(WS[L][:, m, 1, :], weights, WS[L][:, m, 0, :], ALU.subtract)
            last.then_inc(sem("w_split"), 1)

        def later(i, u, k):
            return i + (u + k) // 2, (u + k) % 2

        def dma_at(L, i, per):
            return (i + 1) * (16 * per[L]) + 16 * 4 * sum(per[:L])

        OM_STEPS = Count(2, 2, 2)

        def folds(L, n):
            return L * (B + 1) + n

        CTX = R[:, 0:2 * SK].bitcast(f16).rearrange("p (a h k) -> p a h k", a=2, h=2)

        def features(L, u, h):
            return CTX[:, u, h, :] if L else CTH[:, h, :]

        HALVES = [(0, 0), (0, 1), (1, 0)]

        K_HALF = [(4, 5, 5), (0, 5, 5)]
        Q_DMAS, C_DMAS = (8, 8, 8), (1, 1, 1)

        def va(cfg, u):
            return VA[:, u, 0:KJ * cfg["G"] * (4 * cfg["hd"] + 1)].rearrange(
                "p (j g n) -> p j g n", j=KJ, g=cfg["G"])

        def v_halves(cfg, n, u, c):
            dst, hd2 = va(cfg, u)[:, 4 * c:4 * c + 4], 2 * cfg["hd"]
            return (PS[0:KP, n, :].rearrange("p (j g n) -> p j g n", j=4, g=cfg["G"]),
                    dst[:, :, :, 0:hd2], dst[:, :, :, hd2 + 1:2 * hd2 + 1])

        def ks(cfg, u, k=128):
            return KS[0:k, u, 0:cfg["G"] * SK].rearrange("p (g n) -> p g n", g=cfg["G"])

        def qs(cfg, u):
            return QS[:, u, 0:cfg["G"] * 128].rearrange("p (g h t) -> p g h t", g=cfg["G"], h=2)

        def first_k(step):
            step(-1, 0, -2, False, False, True)

        def steps(eng, L, step):
            step(-1, 1, -1, False, True, True)
            with eng.Fori(0, 3) as i:
                for u in range(2):
                    step(i, u, i * 2 + u, True, True, True)
            step(3, 0, 6, True, True, False)
            step(3, 1, 7, True, False, False)

        def low_unit(eng, unit, L, b, m):
            eng.wait_ge(sem("e_ready"), UNITS.at(L, b, m + 1 + 3))
            unit.tensor_tensor(PL[:, m % 4, :, 0:S], PR[m % 2][0:KP, :].rearrange("p (h t) -> p h t", h=8),
                               PH[:, m % 4, :, 0:S], ALU.subtract).then_inc(low_done(L, b, m)[0], 1)

        def low_done(L, b, m):
            units, before = KJ * XL[L]["halves"], 0
            if m < 0:
                m, before = m + units, units
            who = "d" if m in LOW_ON_DVE[L] else "p"
            mine = [n for n in range(units) if (n in LOW_ON_DVE[L]) == (who == "d")]
            k = sum(n <= m for n in mine) - (len(mine) if before else 0)
            return sem("low_" + who), LOW[who].at(L, b, k + 2)

        def x_sp(sp, L):
            cfg = XL[L]

            def queries():
                sp.wait_ge(sem("qs_clear"), L + 1)
                sp.wait_ge(sem("q_split"), L + 1)
                sp.dma_start(qscr, QH[:, :, :]).then_inc(sem("q_out"), 16)
                sp.wait_ge(sem("q_out"), 16 * (L + 1))

            def stack_k(i, u, b, half):
                gs = cfg["G"] // cfg["halves"]
                g0 = half * gs
                done = sem(f"k_in{u}{half}")
                for n in range(4):
                    sp.dma_start(ks(cfg, u)[cfg["R"] * n:cfg["R"] * (n + 1), g0:g0 + gs, :],
                                 kscr[u, :, n % 2, :].rearrange("(g p) n -> p g n", p=cfg["R"])[:, g0:g0 + gs, :]
                                 ).then_inc(done, 16)
                if cfg["valid"]:
                    sp.dma_start(ks(cfg, u)[MASKROW:MASKROW + 1, g0:g0 + gs, :],
                                 bc(mscr[cfg["valid"] - 1, one(b), :].unsqueeze(1), 1, gs, SK)).then_inc(done, 16)

            def step(i, u, b, has_d, has_c, has_b):
                if has_b:
                    ic, uc = later(i, u, 2)
                    if L == 0:
                        if has_d:
                            sp.wait_ge(sem("t_ready"), THREE.at(L, b + 1))
                            sp.wait_ge(sem("g_ready"), ONE.at(L, b + 1))
                        sp.dma_start(CT[:, uc, :, :], ctx[one(b + 2)].rearrange("o (p j) d -> (o p) j d", j=KJ)
                                     ).then_inc(sem(f"ctx_in{uc}"), 16)
                    else:
                        if has_d:
                            sp.wait_ge(sem("v_ready"), THREE.at(L, b + 1))
                        sp.dma_start(CTX[:, uc, :, :], cscr[one(b + 2)].rearrange("o d h k -> (o d) h k")
                                     ).then_inc(sem(f"ctx_in{uc}"), 16)
                if has_c:
                    ic, uc = later(i, u, 1)
                    if has_d:
                        sp.wait_ge(sem("s_ready"), UNITS.at(L, b, CLEAR))
                    for h in range(2):
                        for n in range(4):
                            r0 = cfg["R"] * n + cfg["hd"] * h
                            src = qscr[:, n // 2, bass.ds((b + 1) * S, S)].rearrange(
                                "(g h p) t -> h p g t", h=2, p=cfg["hd"])[h]
                            sp.dma_start(qs(cfg, uc)[r0:r0 + cfg["hd"], :, h, 0:S], src
                                         ).then_inc(sem(f"q_in{uc}"), 16)
                    if cfg["halves"] == 2:
                        stack_k(ic, uc, b + 1, 1)
                    else:
                        sp.wait_ge(sem(f"k_out{uc}"), dma_at(L, ic, C_DMAS))
                        stack_k(ic, uc, b + 1, 0)
                if has_b:
                    ic, uc = later(i, u, 2)
                    if L == 0:
                        sp.wait_ge(sem("t_copied"), THREE.at(L, b + 3))
                        sp.dma_start(cscr[one(b + 2)].rearrange("o d h k -> (o d) h k"), CTH).then_inc(sem("cth_out"), 16)
                    if cfg["rope"]:
                        sp.wait_ge(sem("k_split"), THREE.at(L, b + 3))
                    else:
                        sp.wait_ge(sem("k_free"), KUSES.at(L, b + 3))
                    if has_d:
                        for half in range(cfg["halves"]):
                            sp.wait_ge(sem(f"k_in{u}{half}"), dma_at(L, i, K_HALF[half]))
                    sp.dma_start(kscr[uc], KHL[:, uc, :, :]).then_inc(sem(f"k_out{uc}"), 16)
                    if cfg["halves"] == 2:
                        sp.wait_ge(sem(f"k_out{uc}"), dma_at(L, ic, C_DMAS))
                        if has_d:
                            sp.wait_ge(sem("s_ready"), UNITS.at(L, b, KJ + CLEAR))
                        elif b == -2:
                            sp.wait_ge(sem("qs_clear"), L + 1)
                        stack_k(ic, uc, b + 2, 0)

            sp.wait_ge(*x_is(AHEAD[L]))
            first_k(step)
            queries()
            for b in range(-1, B - 1):
                step(b // 2, b % 2, b, b >= 0, b >= -1, b < B - 2)
            if L == 0:
                sp.wait_ge(sem("cth_out"), 16 * B)

        def x_pe(pe, L, ahead=False):
            cfg = XL[L]
            nm, hd, banks = cfg["name"], cfg["hd"], short_banks(cfg)
            wide = 4 * hd + 1
            if ahead:
                pe.wait_ge(sem("w_split"), L + 1)
            else:
                norm_pe(pe, nm, X, x_is((1, 7, 10)[L]))
                normed(pe, nm)
                mm(bank(3), w(nm + "_q"), Y[:, :]).then_inc(sem("q_proj"), 1)
                if cfg["rope"]:
                    mm(bank(4), w(nm + "_qr"), Y[:, :]).then_inc(sem("q_proj"), 1)
                    pe.wait_ge(sem("sel_ready"), 1)

            def step(i, u, b, has_d, has_c, has_b):
                i1, u1 = later(i, u, 1)
                i2, u2 = later(i, u, 2)
                before = {7: [], 2: []}
                if has_d:
                    before[7] = [(sem("sh_copied"), SHIFTS.at(L, b + 1))]
                    before[2] = [(sem("g_copied"), ONE.at(L, b + 2))] if cfg["rope"] and has_c else before[7][:]
                elif has_c:
                    before[7] = [(sem("k_free"), KUSES.at(L, 1))]
                    before[2] = [(sem("g_copied"), ONE.at(L, 1)) if cfg["rope"] else before[7][0]]

                def short(kind, c):
                    n = banks[kind, c]
                    for k in before[n]:
                        pe.wait_ge(*k)
                    if kind == "V":
                        if L == 0:
                            pe.wait_ge(sem("t_copied"), THREE.at(L, b + 2))
                        for k in range(4):
                            j = 4 * c + k
                            for x, y in HALVES:
                                last = mm(PS[0:KP, n, k * 128:(k + 1) * 128],
                                          features(L, u1, x)[:, j * KP:(j + 1) * KP],
                                          WS[L][:, 1, y, :], (x, y) == HALVES[0], (x, y) == HALVES[-1])
                        last.then_inc(sem("v_ready"), 1)
                        before[n] = [(sem("v_copied"), THREE.at(L, b + 1, c + 1))]
                    elif kind == "T":
                        if c == 0:
                            pe.wait_ge(sem(f"ctx_in{u2}"), dma_at(L, i2, C_DMAS))
                        for k in range(4):
                            last = PE.transpose(PS[:, n, k * KP:(k + 1) * KP], CT[:, u2, 4 * c + k, :], IDN[0:KP, 0:KP])
                        last.then_inc(sem("t_ready"), 1)
                        before[n] = [(sem("t_copied"), THREE.at(L, b + 2, c + 1))]
                    elif kind in "KR":
                        if L == 0:
                            pe.wait_ge(sem("w_split"), 1)
                            pe.wait_ge(sem("t_copied"), THREE.at(L, b + 2, c + 1))
                        elif c == 0:
                            pe.wait_ge(sem(f"ctx_in{u2}"), dma_at(L, i2, C_DMAS))
                        for x, y in HALVES:
                            last = mm(PS[:, n, 0:500], WS[L][:, 0 if kind == "K" else 2, x, :],
                                      features(L, u2, y)[:, c * 500:(c + 1) * 500], (x, y) == HALVES[0],
                                      (x, y) == HALVES[-1])
                        last.then_inc(sem("k_ready"), 1)
                        done = 2 * c + (kind == "R") + 1 if cfg["rope"] else c + 1
                        before[n] = [(sem("k_free"), KUSES.at(L, b + 2, done))]
                    elif kind == "G":
                        for j in range(KJ):
                            last = mm(PS[:, n, 0:128], CT[:, u2, j, :], CT[:, u2, j, :], j == 0, j == KJ - 1)
                        last.then_inc(sem("g_ready"), 1)
                        before[n] = [(sem("g_copied"), ONE.at(L, b + 3))]
                    elif kind == "SH":
                        pe.wait_ge(sem("dg_ready"), SHIFTS.at(L, b + 1, c + 1))
                        mm(PS[:, n, :], SEL96[:, :], DG[:, c * 512:(c + 1) * 512]).then_inc(sem("sh_ready"), 1)
                        before[n] = [(sem("sh_copied"), SHIFTS.at(L, b + 1, c + 1))]
                    elif kind == "F":
                        pe.wait_ge(sem("om_ready"), ONE.at(L, b, CLEAR))
                        mm(PS[:, n, 0:S], OM[:, 1 - u, 1, :], w("fold")).then_inc(sem("f_ready"), 1)
                        before[n] = [(sem("f_copied"), folds(L, b + 1))]

                def score_unit(m):
                    half, j = divmod(m, KJ)
                    pe.wait_ge(sem("e_ready"), UNITS.at(L, b, m + 1 - len(SCORE_BANKS) + 3))
                    for k in range(4):
                        g = half * 4 + k
                        dst = PS[0:KP, score_bank(m), k * 112:(k + 1) * 112].rearrange("p (h t) -> p h t", h=2)
                        last = mm(dst, ks(cfg, u, cfg["K2"])[:, g, j * KP:(j + 1) * KP],
                                  qs(cfg, u)[0:cfg["K2"], g, :, 0:S], True, not cfg["rope"])
                        if cfg["rope"]:
                            last = mm(dst, ONE16[96:97, :], SR[96:97, u, g * 128:(g + 1) * 128].rearrange(
                                "p (h t) -> p h t", h=2)[:, :, 0:S], False, True)
                    last.then_inc(sem("s_ready"), 1)

                def pv_unit(m):
                    half, j = divmod(m, KJ)
                    pe.wait_ge(*low_done(L, b, m))
                    for k in range(4):
                        g = half * 4 + k
                        mm(PS[:, 6, g * wide:(g + 1) * wide], PH[:, m % 4, 2 * k:2 * k + 2, :],
                           va(cfg, u)[:, j, g, :], j == 0 and g == 0, False, True)
                        last = mm(PS[:, 6, g * wide:g * wide + 2 * hd + 1], PL[:, m % 4, 2 * k:2 * k + 2, :],
                                  va(cfg, u)[:, j, g, 0:2 * hd + 1], False, j == KJ - 1, True)
                    last.then_inc(sem("p_ready"), 1)

                def max_unit(c):
                    g, third = divmod(c, 3)
                    if c == 0:
                        pe.wait_ge(sem(f"q_in{u1}"), dma_at(L, i1, Q_DMAS))
                        pe.wait_ge(sem(f"k_in{u1}0"), dma_at(L, i1, K_HALF[0]))
                    if c == 12:
                        pe.wait_ge(sem(f"k_in{u1}1"), dma_at(L, i1, K_HALF[1]))
                    pe.wait_ge(sem("m_done"), MAXES.at(L, b + 1, c + 1 - len(MAX_BANKS) + 3))
                    mm(PS[:, max_bank(c), 0:500], QS[0:cfg["K1"], u1, g * 128:(g + 1) * 128],
                       ks(cfg, u1, cfg["K1"])[:, g, third * 500:(third + 1) * 500]).then_inc(sem("m_ready"), 1)

                if has_d:
                    pe.wait_ge(sem("v_copied"), THREE.at(L, b + 1))
                    pe.wait_ge(sem("sh_copied"), SHIFTS.at(L, b + 1))
                units = 12 * cfg["halves"]
                for scores, maxima, other in slots(cfg):
                    for k in range(max(len(scores), len(maxima))):
                        if has_d and k < len(scores):
                            score_unit(scores[k])
                            if scores[k] >= LAG:
                                pv_unit(scores[k] - LAG)
                        if has_c and k < len(maxima):
                            max_unit(maxima[k])
                    for kind, c in other:
                        if kind != "SH" and {"V": has_c, "F": has_d, "DG": False}.get(kind, has_b):
                            short(kind, c)
                for k in range(LAG):
                    if has_d:
                        pv_unit(units - LAG + k)
                    if has_c and k < cfg["G"] // 4:
                        short("SH", k)

            if ahead or L == 0:
                first_k(step)
            if ahead:
                return
            steps(pe, L, step)
            pe.wait_ge(sem("f_copied"), folds(L, B))
            pe.wait_ge(sem("om_ready"), ONE.at(L, B, CLEAR))
            mm(PS[:, 2, 0:S], OM[:, 1, 1, :], w("fold")).then_inc(sem("f_ready"), 1)

        def x_act(act, L, ahead=False):
            cfg = XL[L]
            nm, banks = cfg["name"], short_banks(cfg)
            if not ahead:
                norm_act(act, nm, None, 1e-5)
                act.wait_ge(sem("pool_ready"), 1)

            def step(i, u, b, has_d, has_c, has_b):
                i1, u1 = later(i, u, 1)
                i2, u2 = later(i, u, 2)
                for scores, maxima, other in slots(cfg):
                    if has_d:
                        for m in scores:
                            act.wait_ge(sem("s_ready"), UNITS.at(L, b, m + 1 + CLEAR))
                            act.wait_ge(sem("p_ready"), UNITS.at(L, b, m - 3 + 4))
                            A.activation(PH[:, m % 4, :, 0:S],
                                         PS[0:KP, score_bank(m), 0:T].rearrange("p (h t) -> p h t", h=8), ACT.Exp)
                            act.wait_ge(*low_done(L, b, m - 2))
                            A.activation(PR[m % 2][0:KP, :], PS[0:KP, score_bank(m), 0:T], ACT.Exp
                                         ).then_inc(sem("e_ready"), 1)
                    for kind, c in other:
                        if kind == "V" and has_c:
                            act.wait_ge(sem("v_ready"), THREE.at(L, b + 1, c + 1))
                            v, high, low = v_halves(cfg, banks[kind, c], u1, c)
                            A.activation(high, v, ACT.Copy).then_inc(sem("v_high"), 1)
                        if kind == "T" and has_b:
                            act.wait_ge(sem("t_ready"), THREE.at(L, b + 2, c + 1))
                            if c == 0 and has_c:
                                act.wait_ge(sem("v_ready"), THREE.at(L, b + 1, 3))
                                act.wait_ge(sem("cth_out"), (b + 2) * 16)
                            A.activation(CTH[:, 0, c * 500:(c + 1) * 500], PS[:, banks[kind, c], 0:500], ACT.Copy
                                         ).then_inc(sem("t_high"), 1)
                        if kind == "K" and has_b and not cfg["rope"]:
                            act.wait_ge(sem("k_ready"), KUSES.at(L, b + 2, c + 1))
                            if has_d:
                                act.wait_ge(sem(f"k_out{u2}"), dma_at(L, i, C_DMAS))
                            A.activation(KHL[:, u2, 0, c * 500:(c + 1) * 500], PS[:, banks[kind, c], 0:500],
                                         ACT.Identity, bias=w(nm + "_bk")).then_inc(sem("kh_ready"), 1)
                        if kind == "G" and has_b:
                            act.wait_ge(sem("g_ready"), ONE.at(L, b + 3))
                            A.activation(GC[:, one(b + 2), :], PS[:, one(banks[kind, c]), 0:128], ACT.Copy
                                         ).then_inc(sem("g_copied"), 1)
                        if kind == "SH" and has_c:
                            act.wait_ge(sem("sh_ready"), SHIFTS.at(L, b + 1, c + 1))
                            row = SR[96:97, u1, :] if cfg["rope"] else QS[96:97, u1, c * 512:(c + 1) * 512]
                            A.activation(row, PS[96:97, banks[kind, c], :], ACT.Copy).then_inc(sem("sh_copied"), 1)

            if ahead or L == 0:
                first_k(step)
            if ahead:
                return
            steps(act, L, step)

        def x_dve(dve, L, ahead=False):
            cfg = XL[L]
            nm, G_, hd, banks = cfg["name"], cfg["G"], cfg["hd"], short_banks(cfg)
            wide = 4 * hd + 1
            def queries():
                if cfg["rope"]:
                    def by_token(k):
                        return bc(ROPE_Q[:, k, :].unsqueeze(1), 128, B, S)
                    dve.wait_ge(sem("q_proj"), 1)
                    link(dve, "dve_chain", V.tensor_tensor(Z[:, :].rearrange("p (b t) -> p b t", b=B),
                         bank(3).rearrange("p (b t) -> p b t", b=B), by_token(0), ALU.mult))
                    dve.wait_ge(sem("q_proj"), 2)
                    link(dve, "dve_chain", V.tensor_tensor(XC[:, :].rearrange("p (b t) -> p b t", b=B),
                         bank(4).rearrange("p (b t) -> p b t", b=B), by_token(1), ALU.mult))
                    link(dve, "dve_chain", V.tensor_tensor(Z[:, :], Z[:, :], XC[:, :], ALU.add))
                    link(dve, "dve_chain", V.tensor_scalar(Z[:, :], Z[:, :], cfg["scale"], None, ALU.mult))
                else:
                    dve.wait_ge(sem("q_proj"), L + 2)
                    link(dve, "dve_chain", V.tensor_scalar(
                        Z[:, :], bank(3), w(nm + "_bq"), cfg["scale"], ALU.add, ALU.mult))
                link(dve, "dve_chain", V.tensor_copy(QH[:, 0, :], Z[:, :]))
                V.tensor_tensor(QH[:, 1, :], Z[:, :], QH[:, 0, :], ALU.subtract).then_inc(sem("q_split"), 1)

            def step(i, u, b, has_d, has_c, has_b):
                i1, u1 = later(i, u, 1)
                i2, u2 = later(i, u, 2)
                for scores, maxima, other in slots(cfg):
                    if has_d:
                        for m in scores:
                            if m in LOW_ON_DVE[L]:
                                low_unit(dve, V, L, b, m)
                    if has_c:
                        for c in maxima:
                            dve.wait_ge(sem("m_ready"), MAXES.at(L, b + 1, c + 1))
                            V.tensor_reduce(MX[:, u1, c:c + 1], PS[:, max_bank(c), 0:500], AX.X, ALU.max
                                            ).then_inc(sem("m_done"), 1)
                    for kind, c in other:
                        if kind == "V" and has_c:
                            dst = va(cfg, u1)
                            if c == 0:
                                V.tensor_copy(VC[:, u1:u1 + 1, :], VALID[:, cfg["valid"], one(b + 1), :]
                                              ).then_inc(sem("valid_here"), 1)
                                dve.wait_ge(sem("valid_here"), ONE.at(L, b + 2))
                                V.tensor_copy(dst[:, :, :, 2 * hd], bc(VC[:, u1, :].unsqueeze(2), KP, KJ, G_))
                            dve.wait_ge(sem("v_ready"), THREE.at(L, b + 1, c + 1))
                            v, high, low = v_halves(cfg, banks[kind, c], u1, c)
                            dve.wait_ge(sem("v_high"), THREE.at(L, b + 1, c + 1))
                            V.tensor_tensor(low, v, high, ALU.subtract).then_inc(sem("v_copied"), 1)
                        if kind == "F" and has_d:
                            dve.wait_ge(sem("f_ready"), folds(L, b + 1))
                            V.tensor_copy(AO[:, one(b), :], PS[:, one(banks[kind, c]), 0:S]).then_inc(sem("f_copied"), 1)
                        if kind == "T" and has_b:
                            dve.wait_ge(sem("t_high"), THREE.at(L, b + 2, c + 1))
                            V.tensor_tensor(CTH[:, 1, c * 500:(c + 1) * 500], PS[:, banks[kind, c], 0:500],
                                            CTH[:, 0, c * 500:(c + 1) * 500], ALU.subtract).then_inc(sem("t_copied"), 1)
                        if kind in "KR" and has_b:
                            src = PS[:, banks[kind, c], 0:500]
                            if cfg["rope"]:
                                r = int(kind == "R")
                                if has_c and r == 0:
                                    dve.wait_ge(sem("k_split"), THREE.at(L, b + 1, c + 1))
                                dve.wait_ge(sem("k_ready"), KUSES.at(L, b + 2, 2 * c + r + 1))
                                V.tensor_tensor(KT[:, c, r, :], src, ROPE_K[:, r * SK + c * 500:r * SK + (c + 1) * 500],
                                                ALU.mult).then_inc(sem("k_free"), 1)
                            else:
                                dve.wait_ge(sem("kh_ready"), THREE.at(L - 1, b + 2, c + 1))
                                V.scalar_tensor_tensor(KHL[:, u2, 1, c * 500:(c + 1) * 500], src, w(nm + "_bk"),
                                                       KHL[:, u2, 0, c * 500:(c + 1) * 500], ALU.add, ALU.subtract
                                                       ).then_inc(sem("k_free"), 1)
                        if kind == "DG" and has_c:
                            if c == 0:
                                dve.wait_ge(sem("m_done"), MAXES.at(L, b + 2, 3))
                                V.tensor_reduce(MM[:, u1, 0:G_], MX[:, u1, 0:3 * G_].rearrange("p (g c) -> p g c", c=3),
                                                AX.X, ALU.max, negate=True).then_inc(sem("mm_done"), 1)
                                dve.wait_ge(sem("mm_done"), ONE.at(L, b + 2))
                            V.tensor_tensor(DG[:, c * 512:(c + 1) * 512].rearrange("p (g n) -> p g n", g=4),
                                            bc(IDH[:, :].unsqueeze(1), 128, 4, 128),
                                            bc(MM[:, u1, 4 * c:4 * c + 4].unsqueeze(2), 128, 4, 128), ALU.mult
                                            ).then_inc(sem("dg_ready"), 1)
                if has_d:
                    pv = PS[:, 6, 0:G_ * wide].rearrange("p (g n) -> p g n", g=G_)
                    om = OM[:, u, :, :].rearrange("p a (g n) -> p a g n", g=G_)
                    dve.wait_ge(sem("p_ready"), UNITS.at(L, b + 1, 4))
                    V.reciprocal(RD[:, u, 0:G_], pv[:, :, 2 * hd])
                    V.tensor_copy(om[:, 0], pv[:, :, 0:2 * hd]).then_inc(sem("om_half"), 1)
                    dve.wait_ge(sem("om_half"), OM_STEPS.at(L, b, 1))
                    V.tensor_tensor(om[:, 1], bc(w("blk8" if hd == 8 else "blk16").unsqueeze(1), 128, G_, 2 * hd),
                                    bc(RD[:, u, 0:G_].unsqueeze(2), 128, G_, 2 * hd), ALU.mult)
                    V.tensor_tensor(om[:, 0], om[:, 0], pv[:, :, 2 * hd + 1:wide], ALU.add).then_inc(sem("om_half"), 1)
                    dve.wait_ge(sem("om_half"), OM_STEPS.at(L, b, 2))
                    V.tensor_tensor(om[:, 1], om[:, 0], om[:, 1], ALU.mult).then_inc(sem("om_ready"), 1)

            if L == 0:
                norm_dve(dve, nm, X, Y[:, :])
                normed(dve, nm)
                split_weights(dve, L)
                dve.wait_ge(sem("rope_in"), 48)
            if ahead or L == 0:
                first_k(step)
            if ahead:
                return
            if L:
                norm_dve(dve, nm, X, Y[:, :])
            queries()
            steps(dve, L, step)
            dve.wait_ge(sem("f_ready"), folds(L, B + 1))
            V.tensor_copy(AO[:, B:B + 1, :], PS[:, 2:3, 0:S]).then_inc(sem("f_copied"), 1)

        def x_pool(pool, L):
            cfg = XL[L]
            if L == 1:
                pool.wait_ge(*x_is(6))
                for u in range(2):
                    link(pool, "pool_chain", G.memset(KS32[64:128, u * 6144:u * 6144 + 4 * SK], 0.0))
                    link(pool, "pool_chain", G.memset(KS32[96:97, u * 6144:u * 6144 + 4 * SK], ONE_ONE))
                    link(pool, "pool_chain", G.memset(QS[:, u, :], 0.0))
                    link(pool, "pool_chain", G.memset(QS[64:65, u, :], BIG))
            if L:
                if L == 2:
                    pool.wait_ge(*x_is(8))
                pool.sem_inc(sem("qs_clear"), 1)

            def step(i, u, b, has_d, has_c, has_b):
                i2, u2 = later(i, u, 2)
                for scores, maxima, other in slots(cfg):
                    if has_d:
                        for m in scores:
                            if m not in LOW_ON_DVE[L]:
                                low_unit(pool, G, L, b, m)
                    for kind, c in other:
                        if kind == "K" and has_b and L == 0:
                            hi, lo = (KHL[:, u2, r, c * 500:(c + 1) * 500] for r in range(2))
                            pool.wait_ge(sem("k_free"), KUSES.at(L, b + 2, 2 * c + 2))
                            if has_d:
                                pool.wait_ge(sem(f"k_out{u2}"), dma_at(L, i, C_DMAS))
                            G.tensor_tensor(hi, KT[:, c, 0, :], KT[:, c, 1, :], ALU.add).then_inc(sem("k_high"), 1)
                            pool.wait_ge(sem("k_high"), THREE.at(L, b + 2, c + 1))
                            G.tensor_tensor(KT[:, c, 0, :], KT[:, c, 0, :], KT[:, c, 1, :], ALU.add
                                            ).then_inc(sem("k_whole"), 1)
                            pool.wait_ge(sem("k_whole"), THREE.at(L, b + 2, c + 1))
                            G.tensor_tensor(lo, KT[:, c, 0, :], hi, ALU.subtract).then_inc(sem("k_split"), 1)

            if L == 0:
                first_k(step)
            steps(pool, L, step)

        def l0x_end_pe(pe):
            pe.wait_ge(sem("f_copied"), folds(0, B + 1))
            mm(bank(2), w("l0x_out"), AO[:, 1:, :]).then_inc(sem("x_out"), 1)

        def l0x_end_dve(dve):
            dve.wait_ge(sem("x_out"), 1)
            V.tensor_tensor(X, X, bank(2), ALU.add).then_inc(sem("x_ready"), 1)

        CF = sb("CF", [8, T])
        HR = KS32[:, 4096:4096 + 3 * T].rearrange("p (a t) -> p a t", a=3)
        TK = sb("TK", [TT, 12, NT, 8])
        TI = sb("TI", [TT, NT, 8], u32)
        TS = sb("TS", [TT, 8, NT])

        ROUTER_AT = {"l0f": 1, "l1f": 2, "l3f": 3}
        MOE_AT = {"l0f": 0, "l1f": 1}

        def moe_pe(pe, nm, hin):
            pe.wait_ge(sem("router_cf"), ROUTER_AT[nm])

            def coefficients(e):
                if e >= 2:
                    pe.wait_ge(sem("moe_hg"), (MOE_AT[nm] * E + e - 1) * FC)
                mm(bank(e % 2), bc(w("ident", e, 1, 8), 8, 128), CF[:, :]).then_inc(sem("moe_bc"), 1)

            def down(m):
                pe.wait_ge(sem("moe_hg"), MOE_AT[nm] * E * FC + m + 1)
                mm(bank(6), wb("w2", m * 128, 128), HR[:, m % 3, :], m == 0, False).then_inc(sem("moe_dn"), 1)

            for m in range(E * FC):
                if m % FC == 0:
                    coefficients(m // FC)
                if m >= 4:
                    pe.wait_ge(sem("moe_hid"), MOE_AT[nm] * E * FC + m - 3)
                mm(bank(2 + m % 4), wb("w1", m * 128, 128), hin).then_inc(sem("moe_up"), 1)
                if m >= 2:
                    down(m - 2)
            down(E * FC - 2)
            down(E * FC - 1)
            mm(bank(6), w(nm + "_b2", 0, 128, 8), CF[:, :], False, True).then_inc(sem("moe_sum"), 1)

        def moe_act(act, nm, func):
            for m in range(E * FC):
                act.wait_ge(sem("moe_up"), MOE_AT[nm] * E * FC + m + 1)
                if m >= 3:
                    act.wait_ge(sem("moe_dn"), MOE_AT[nm] * E * FC + m - 2)
                A.activation(HR[:, m % 3, :], bank(2 + m % 4), func, bias=w(nm + "_b1", m, 1)
                             ).then_inc(sem("moe_hid"), 1)

        def moe_dve(dve, nm):
            for m in range(E * FC):
                if m % FC == 0:
                    dve.wait_ge(sem("moe_bc"), MOE_AT[nm] * E + m // FC + 1)
                dve.wait_ge(sem("moe_hid"), MOE_AT[nm] * E * FC + m + 1)
                V.tensor_tensor(HR[:, m % 3, :], HR[:, m % 3, :], bank(m // FC % 2), ALU.mult
                                ).then_inc(sem("moe_hg"), 1)

        def router_pe(pe, nm, hin, weights, bias=None):
            for j in range(NT):
                dst = PS[0:TT, 7, j * 8:(j + 1) * 8]
                last = mm(dst, hin[:, j * TT:(j + 1) * TT], w(weights), True, bias is None)
                if bias is not None:
                    last = mm(dst, w("ones", 0, TT, 1), w(bias, 0, 8, 1), False, True)
            last.then_inc(sem("router_logits"), 1)

        def to_experts_pe(pe, nm, mats):
            pe.wait_ge(sem("router_route"), ROUTER_AT[nm])
            for k, n in enumerate(mats):
                for j in range(NT):
                    last = PE.transpose(PS[0:8, 2 + k, j * TT:(j + 1) * TT], TK[:, n, j, :], IDN[0:TT, 0:TT])
            last.then_inc(sem("router_byexp"), 1)

        def col(k):
            return bc(TS[:, k, :].unsqueeze(2), TT, NT, 8)

        def softmax_dve(dve, nm, top=False):
            dve.wait_ge(sem("router_logits"), ROUTER_AT[nm])
            link(dve, "dve_chain", V.tensor_copy(TK[:, 0], PS[0:TT, 7, 0:32].rearrange("p (j e) -> p j e", j=NT)))
            link(dve, "dve_chain", V.tensor_reduce(TS[:, 0, :], TK[:, 0], AX.X, ALU.max))
            V.tensor_tensor(TK[:, 1], TK[:, 0], col(0), ALU.subtract).then_inc(sem("router_gless"), 1)
            if top:
                for j in range(NT):
                    link(dve, "dve_chain", V.max(TK[:, 4, j, :], TK[:, 0, j, :]))
                    link(dve, "dve_chain", V.max_index(TI[:, j, :], TK[:, 4, j, :], TK[:, 0, j, :]))
                link(dve, "dve_chain", V.tensor_copy(TK[:, 5], TI[:, :, :]))
                for k in range(2):
                    link(dve, "dve_chain", V.tensor_tensor(
                        TK[:, 2 + k], bc(w("iota", p=TT).unsqueeze(1), TT, NT, 8),
                        bc(TK[:, 5, :, k:k + 1], TT, NT, 8), ALU.is_equal))
            dve.wait_ge(sem("router_gexp"), ROUTER_AT[nm])
            link(dve, "dve_chain", V.tensor_reduce(TS[:, 1, :], TK[:, 1], AX.X, ALU.add))
            link(dve, "dve_chain", V.reciprocal(TS[:, 1, :], TS[:, 1, :]))

        def softmax_act(act, nm):
            act.wait_ge(sem("router_gless"), ROUTER_AT[nm])
            A.activation(TK[:, 1], TK[:, 1], ACT.Exp).then_inc(sem("router_gexp"), 1)

        QK = KS32[:, 0:8192].rearrange("p (m b t) -> p m b t", m=16, b=B)
        VS = KS32[0:S, 8192:10240].rearrange("p (a n) -> p a n", a=2)
        PT = KS32[0:S, 10240:12288].rearrange("p (a n) -> p a n", a=2)
        RR = R[:, 0:4 * T].rearrange("p (a n) -> p a n", a=4)
        RQ = R[:, 4 * T:8 * T].rearrange("p (a n) -> p a n", a=4)
        RAW = (2, 3, 6, 7)
        SB2 = R[:, 0:2 * T].rearrange("p (a n) -> p a n", a=2)
        OA = R[:, 2 * T:10 * T].rearrange("p (g t) -> p g t", g=8)

        def l0f_pe(pe):
            norm_pe(pe, "l0f", X, x_is(2))
            norm_pe(pe, "l0f_1", Y[:, :], (sem("norm_ready"), NORM_AT["l0f"]))
            normed(pe, "l0f_1")
            pe.wait_ge(sem("big0_in"), 96)

            def squares(m):
                pe.wait_ge(sem("l0f_sq"), m + 1)
                if m >= 2:
                    pe.wait_ge(sem("l0f_rs"), m - 1)
                mm(bank(4 + m % 2), w("half"), RQ[:, m % 4, :]).then_inc(sem("l0f_ss"), 1)

            for m in range(16):
                if m >= 4:
                    pe.wait_ge(sem("l0f_qk"), m - 3)
                mm(bank(RAW[m % 4]), wb("wq", m * 128, 128), Z[:, :]).then_inc(sem("l0f_raw"), 1)
                if m >= 2:
                    squares(m - 2)
            squares(14)
            squares(15)
            pe.wait_ge(sem("l0f_qk"), 16)

            def values(b):
                if b:
                    pe.wait_ge(sem("l0f_vs"), b)
                for n in range(2):
                    last = mm(PS[0:S, 6 + n, :], Z[:, b * S:(b + 1) * S], wb("wv", n * 512, 512))
                last.then_inc(sem("l0f_v"), 1)

            def scores(b):
                pe.wait_ge(sem("l0f_clear"), 1)
                if b >= 2:
                    pe.wait_ge(sem("l0f_sb"), b - 1)
                for g in range(8):
                    for h in range(2):
                        last = mm(PS[64 * h:64 * h + 64, 2 + b % 2, g * S:(g + 1) * S],
                                  QK[64 * h:64 * h + 64, g, b, :], QK[64 * h:64 * h + 64, 8 + g, b, 0:S])
                last.then_inc(sem("l0f_s"), 1)

            values(0)
            scores(0)
            for b in range(B):
                if b + 1 < B:
                    scores(b + 1)
                pe.wait_ge(sem("l0f_p"), b + 1)
                if b:
                    pe.wait_ge(sem("l0f_pt"), b)
                for g in range(8):
                    last = PE.transpose(PS[0:S, 4 + g // 4, g % 4 * 128:g % 4 * 128 + 128],
                                        SB2[:, b % 2, g * S:(g + 1) * S], IDN)
                last.then_inc(sem("l0f_t"), 1)
                if b + 1 < B:
                    values(b + 1)
                pe.wait_ge(sem("l0f_pt"), b + 1)
                pe.wait_ge(sem("l0f_vs"), b + 1)
                if b >= 2:
                    pe.wait_ge(sem("l0f_oc"), b - 1)
                for g in range(8):
                    for h in range(2):
                        last = mm(PS[64 * h:64 * h + 64, b % 2, g * S:(g + 1) * S],
                                  VS[:, b % 2, (2 * g + h) * 64:(2 * g + h + 1) * 64],
                                  PT[:, b % 2, g * 128 + 64 * h:g * 128 + 64 * h + S])
                last.then_inc(sem("l0f_o"), 1)
            pe.wait_ge(sem("l0f_oc"), B)
            for g in range(8):
                last = mm(bank(2), wb("wo", g * 128, 128), OA[:, g, :], g == 0, g == 7)
            last.then_inc(sem("l0f_proj"), 1)
            norm_pe(pe, "l0f_2", Z[:, :], (sem("l0f_z"), 1))
            normed(pe, "l0f_2")
            router_pe(pe, "l0f", Y[:, :], "l0f_gate", "row_gb")
            to_experts_pe(pe, "l0f", (2,))
            moe_pe(pe, "l0f", Y[:, :])
            norm_pe(pe, "l0f_3", Z[:, :], (sem("l0f_z"), 2))

        def l0f_act(act):
            norm_act(act, "l0f", X, 1e-5)
            norm_act(act, "l0f_1", None, 1e-5)

            def inverse(m):
                act.wait_ge(sem("l0f_ss"), m + 1)
                if m >= 4:
                    act.wait_ge(sem("l0f_qk"), m - 3)
                link(act, "act_chain", A.activation(RR[:, m % 4, :], bank(4 + m % 2), ACT.Ln, bias=1e-12))
                A.activation(RR[:, m % 4, :], RR[:, m % 4, :], ACT.Exp, scale=-0.5).then_inc(sem("l0f_rs"), 1)

            for m in range(16):
                act.wait_ge(sem("l0f_raw"), m + 1)
                if m >= 4:
                    act.wait_ge(sem("l0f_ss"), m - 3)
                A.activation(RQ[:, m % 4, :], bank(RAW[m % 4]), ACT.Square).then_inc(sem("l0f_sq"), 1)
                if m >= 2:
                    inverse(m - 2)
            inverse(14)
            inverse(15)
            for b in range(B):
                act.wait_ge(sem("l0f_v"), b + 1)
                if b >= 2:
                    act.wait_ge(sem("l0f_o"), b - 1)
                A.activation(VS[:, b % 2, :].rearrange("p (a n) -> p a n", a=2), PS[0:S, 6:8, :], ACT.Copy
                             ).then_inc(sem("l0f_vs"), 1)
                act.wait_ge(sem("l0f_sb"), b + 1)
                A.activation(SB2[:, b % 2, :], SB2[:, b % 2, :], ACT.Exp).then_inc(sem("l0f_e"), 1)
                act.wait_ge(sem("l0f_t"), b + 1)
                A.activation(PT[:, b % 2, :].rearrange("p (a n) -> p a n", a=2), PS[0:S, 4:6, :], ACT.Copy
                             ).then_inc(sem("l0f_pt"), 1)
            norm_act(act, "l0f_2", None, 1e-5)
            softmax_act(act, "l0f")
            moe_act(act, "l0f", ACT.Gelu_apprx_tanh)
            norm_act(act, "l0f_3", None, 1e-5)

        def l0f_pool(pool):
            pool.wait_ge(*x_is(2))
            G.memset(QK[:, 0:8, :, S:SP2], 0.0).then_inc(sem("l0f_clear"), 1)

        def l0f_dve(dve):
            norm_dve(dve, "l0f", X, Y[:, :])
            norm_dve(dve, "l0f_1", Y[:, :], Z[:, :], w("l0f_g"), w("l0f_c"))
            for m in range(16):
                dve.wait_ge(sem("l0f_rs"), m + 1)
                V.scalar_tensor_tensor(QK[:, m, :, 0:S], bank(RAW[m % 4]).rearrange("p (b t) -> p b t", b=B),
                                       w("l0f_qs" if m < 8 else "l0f_ks", m % 8, 1),
                                       RR[:, m % 4, :].rearrange("p (b t) -> p b t", b=B), ALU.mult, ALU.mult
                                       ).then_inc(sem("l0f_qk"), 1)
            m8, d8 = MM[:, 0, :], RD[:, 0, :]

            def less(b):
                dve.wait_ge(sem("l0f_s"), b + 1)
                if b >= 2:
                    dve.wait_ge(sem("l0f_t"), b - 1)
                s = SB2[:, b % 2, :].rearrange("p (g t) -> p g t", g=8)
                link(dve, "dve_chain", V.scalar_tensor_tensor(
                    s, bank(2 + b % 2).rearrange("p (g t) -> p g t", g=8), 10.0,
                    bc(w("causal").unsqueeze(1), 128, 8, S), ALU.mult, ALU.add))
                link(dve, "dve_chain", V.tensor_reduce(m8, s, AX.X, ALU.max))
                V.tensor_tensor(s, s, bc(m8.unsqueeze(2), 128, 8, S), ALU.subtract).then_inc(sem("l0f_sb"), 1)

            def keep(b):
                dve.wait_ge(sem("l0f_o"), b + 1)
                V.tensor_copy(OA[:, :, b * S:(b + 1) * S], bank(b % 2).rearrange("p (g t) -> p g t", g=8)
                              ).then_inc(sem("l0f_oc"), 1)

            less(0)
            for b in range(B):
                dve.wait_ge(sem("l0f_e"), b + 1)
                s = SB2[:, b % 2, :].rearrange("p (g t) -> p g t", g=8)
                link(dve, "dve_chain", V.tensor_reduce(d8, s, AX.X, ALU.add))
                link(dve, "dve_chain", V.reciprocal(d8, d8))
                V.tensor_tensor(s, s, bc(d8.unsqueeze(2), 128, 8, S), ALU.mult).then_inc(sem("l0f_p"), 1)
                if b + 1 < B:
                    less(b + 1)
                if b:
                    keep(b - 1)
            keep(B - 1)
            dve.wait_ge(sem("l0f_proj"), 1)
            V.tensor_copy(Z[:, :], bank(2)).then_inc(sem("l0f_z"), 1)
            norm_dve(dve, "l0f_2", Z[:, :], Y[:, :], w("l0f_g"), w("l0f_c"))
            softmax_dve(dve, "l0f")
            V.tensor_tensor(TK[:, 2], TK[:, 1], col(1), ALU.mult).then_inc(sem("router_route"), 1)
            dve.wait_ge(sem("router_byexp"), ROUTER_AT["l0f"])
            V.tensor_copy(CF[:, :], bank(2, T, 8)).then_inc(sem("router_cf"), 1)
            moe_dve(dve, "l0f")
            dve.wait_ge(sem("moe_sum"), 1)
            V.tensor_copy(Z[:, :], bank(6)).then_inc(sem("l0f_z"), 1)
            norm_dve(dve, "l0f_3", Z[:, :], Z[:, :], w("l0f_g"), w("l0f_c"))
            normed(dve, "l0f_3")
            V.tensor_tensor(X, X, Z[:, :], ALU.add).then_inc(sem("x_ready"), 1)

        def piece(n, cols=T, p=128):
            return KS32[0:p, n * 512:n * 512 + cols]

        lq, lkn, lkb, lbt, lnr, ld0, ld1, lve = (piece(n) for n in range(8))
        (mN1, mN1T, mE, mQA, mP2, mP2T, mY1, mY2, mP4, mDT, mM, mMT, mM2, mM2T, mM4T) = (
            piece(8 + n, T, TT) for n in range(15))
        RW = R[0:TT, 0:2560].rearrange("p (a n) -> p a n", a=5)
        AL = sb("AL", [128, 4])

        def tile(ap, j, n=TT):
            return ap[:, j * n:(j + 1) * n]

        def l1a_pe(pe):
            norm_pe(pe, "l1a", X, x_is(3))
            pe.wait_ge(sem("rest_in"), 16)
            norm_pe(pe, "l1a_1", None, None)
            normed(pe, "l1a_1")
            for n, name in enumerate(("l1a_k", "l1a_beta", "l1a_q", "l1a_v")):
                mm(bank(2 + n), w(name), Z[:, :]).then_inc(sem("l1a_proj"), 1)
            pe.wait_ge(sem("l1a_ksq"), 1)
            mm(bank(6), w("ones"), SQ[:, :]).then_inc(sem("l1a_kss"), 1)

            def products(k, *jobs):
                pe.wait_ge(sem("l1a_sb"), k)
                for n, l, r, cols in jobs:
                    for j in range(NT):
                        last = mm(PS[0:TT, n, j * cols:(j + 1) * cols], tile(l, j), tile(r, j, cols))
                last.then_inc(sem("l1a_done"), 1)

            products(1, (2, lkb, lkn, TT), (3, lkn, lkb, TT), (4, lkn, lq, TT))
            pe.wait_ge(sem("l1a_vb"), 1)
            for j in range(NT):
                last = PE.transpose(PS[0:TT, 5, j * 128:(j + 1) * 128], tile(lve, j), IDN)
            last.then_inc(sem("l1a_vt"), 1)
            products(2, (2, mN1T, mN1, TT), (3, mN1, mN1T, TT))
            products(3, (4, mP2, mY1, TT), (6, mP2T, mP2, TT))
            products(4, (2, mP4, mY2, TT))
            products(5, (3, mDT, mE, TT), (4, mE, mDT, TT), (6, mDT, RW[:, 0], 128))
            products(6, (2, mMT, mM, TT), (5, mM, mMT, TT))
            products(7, (3, mM2, mM2T, TT))
            products(8, (4, mM4T, RW[:, 1], 128))
            products(9, (6, mM2T, RW[:, 2], 128))
            products(10, (7, mMT, RW[:, 3], 128))
            pe.wait_ge(sem("l1a_sb"), 11)
            for j in range(NT):
                last = mm(PS[:, 2, j * TT:(j + 1) * TT], tile(RW[:, 4], j, 128), tile(mQA, j))
            last.then_inc(sem("l1a_done"), 1)
            pe.wait_ge(sem("l1a_sb"), 12)
            mm(bank(3), w("l1a_o"), lq).then_inc(sem("l1a_done"), 1)
            norm_pe(pe, "l1a_2", None, None)
            normed(pe, "l1a_2")
            for n in range(2):
                mm(bank(2 + n), w("l1a_gate", n * 128, 128), Y[:, :]).then_inc(sem("l1a_mlp"), 1)
                mm(bank(4 + n), w("l1a_up", n * 128, 128), Y[:, :]).then_inc(sem("l1a_mlp"), 1)
            for n in range(2):
                pe.wait_ge(sem("l1a_hid"), n + 1)
                last = mm(bank(6), w("l1a_down", n * 128, 128), piece(n), n == 0, n == 1)
            last.then_inc(sem("l1a_mlp"), 1)

        def l1a_act(act):
            norm_act(act, "l1a", X, 1e-5)
            norm_act(act, "l1a_1", Y[:, :], 1e-6, (sem("norm_ready"), NORM_AT["l1a"]))
            act.wait_ge(sem("l1a_proj"), 1)
            A.activation(SQ[:, :], bank(2), ACT.Square).then_inc(sem("l1a_ksq"), 1)
            act.wait_ge(sem("l1a_proj"), 2)
            A.activation(AL[:, 0:1], w("l1a_alpha"), ACT.Sigmoid).then_inc(sem("l1a_gates"), 1)
            A.activation(lbt, bank(3), ACT.Sigmoid, bias=w("l1a_bb")).then_inc(sem("l1a_gates"), 1)
            act.wait_ge(sem("l1a_kss"), 1)
            A.activation(lnr, bank(6), ACT.Sqrt).then_inc(sem("l1a_norm"), 1)
            norm_act(act, "l1a_2", Z[:, :], 1e-6, (sem("l1a_sb"), 13))
            for n in range(2):
                act.wait_ge(sem("l1a_mlp"), 2 * n + 2)
                A.activation(piece(n), bank(2 + n), ACT.Silu).then_inc(sem("l1a_silu"), 1)

        def l1a_dve(dve):
            norm_dve(dve, "l1a", X, Y[:, :])
            norm_dve(dve, "l1a_1", Y[:, :], Z[:, :], w("l1a_n1"))
            dve.wait_ge(sem("l1a_gates"), 2)
            link(dve, "dve_chain", V.tensor_scalar(AL[:, 1:2], AL[:, 0:1], -1.0, 1.0, ALU.mult, ALU.add))
            V.tensor_scalar(ld0, w("reset"), AL[:, 1:2], None, ALU.mult)
            dve.wait_ge(sem("l1a_proj"), 4)
            V.tensor_copy(lq, bank(4))
            link(dve, "dve_chain", V.tensor_scalar(ld1, bank(5), AL[:, 0:1], None, ALU.mult))
            link(dve, "dve_chain", V.tensor_tensor_scan(lve, ld0, ld1, 0.0, ALU.mult, ALU.add))
            V.tensor_tensor(lve, lve, lbt, ALU.mult).then_inc(sem("l1a_vb"), 1)
            dve.wait_ge(sem("l1a_norm"), 1)
            link(dve, "dve_chain", V.tensor_scalar(lnr, lnr, 1e-12, None, ALU.max))
            link(dve, "dve_chain", V.reciprocal(lnr, lnr))
            link(dve, "dve_chain", V.tensor_tensor(lkn, bank(2), lnr, ALU.mult))
            V.tensor_tensor(lkb, lkn, lbt, ALU.mult).then_inc(sem("l1a_sb"), 1)

            def masked(dst, n, name):
                return V.tensor_tensor(dst.rearrange("p (j t) -> p j t", j=NT), bank(n, T, TT).rearrange(
                    "p (j t) -> p j t", j=NT), bc(w(name, p=TT).unsqueeze(1), TT, NT, TT), ALU.mult)

            def done(k):
                dve.wait_ge(sem("l1a_done"), k)

            done(1)
            masked(mN1, 2, "inlow")
            masked(mE, 2, "offlow")
            masked(mQA, 4, "upper")
            link(dve, "dve_chain", masked(mN1T, 3, "inup"))
            V.tensor_tensor(mY1.rearrange("p (j t) -> p j t", j=NT), mN1T.rearrange("p (j t) -> p j t", j=NT),
                            bc(w("ident", 0, TT, TT).unsqueeze(1), TT, NT, TT), ALU.add).then_inc(sem("l1a_sb"), 1)
            dve.wait_ge(sem("l1a_vt"), 1)
            V.tensor_copy(RW[:, 0], bank(5, 512, TT))
            done(2)
            V.tensor_copy(mP2, bank(2, T, TT))
            V.tensor_copy(mP2T, bank(3, T, TT)).then_inc(sem("l1a_sb"), 1)
            done(3)
            V.tensor_copy(mP4, bank(6, T, TT))
            V.tensor_tensor(mY2, mY1, bank(4, T, TT), ALU.add).then_inc(sem("l1a_sb"), 1)
            done(4)
            dve.wait_ge(sem("l1a_sb"), 4)
            V.tensor_tensor(mDT, mY2, bank(2, T, TT), ALU.add).then_inc(sem("l1a_sb"), 1)
            done(5)
            V.tensor_copy(mM, bank(3, T, TT))
            V.tensor_copy(RW[:, 1], bank(6, 512, TT))
            V.tensor_copy(mMT, bank(4, T, TT)).then_inc(sem("l1a_sb"), 1)
            done(6)
            V.tensor_copy(mM2, bank(2, T, TT))
            V.tensor_copy(mM2T, bank(5, T, TT)).then_inc(sem("l1a_sb"), 1)
            done(7)
            V.tensor_copy(mM4T, bank(3, T, TT)).then_inc(sem("l1a_sb"), 1)
            for k, n in ((8, 4), (9, 6), (10, 7)):
                done(k)
                dve.wait_ge(sem("l1a_sb"), k)
                V.tensor_tensor(RW[:, k - 6], RW[:, k - 7], bank(n, 512, TT), ALU.add).then_inc(sem("l1a_sb"), 1)
            done(11)
            V.tensor_copy(lq, bank(2)).then_inc(sem("l1a_sb"), 1)
            done(12)
            V.tensor_tensor(Z[:, :], bank(3), Y[:, :], ALU.add).then_inc(sem("l1a_sb"), 1)
            norm_dve(dve, "l1a_2", Z[:, :], Y[:, :], w("l1a_n2"))
            for n in range(2):
                dve.wait_ge(sem("l1a_silu"), n + 1)
                V.tensor_tensor(piece(n), piece(n), bank(4 + n), ALU.mult).then_inc(sem("l1a_hid"), 1)
            link(dve, "dve_chain", V.tensor_tensor(X, X, Z[:, :], ALU.add))
            dve.wait_ge(sem("l1a_mlp"), 5)
            V.tensor_tensor(X, X, bank(6), ALU.add).then_inc(sem("x_ready"), 1)

        LX = R[0:S, 0:1024]
        LX8 = LX.rearrange("p (b n) -> p b n", b=B)
        LXP = PS[0:S, 2:4, :].rearrange("p a (b n) -> p a b n", b=4)

        def l1x_pe(pe):
            norm_pe(pe, "l1x", X, x_is(4))
            normed(pe, "l1x")
            for b in range(B):
                last = mm(PS[0:S, 2 + b // 4, b % 4 * 128:b % 4 * 128 + 128], Y[:, b * S:(b + 1) * S], GC[:, b, :])
            last.then_inc(sem("l1x_o"), 1)
            pe.wait_ge(sem("l1x_p"), 1)
            for b in range(B):
                last = PE.transpose(PS[:, 4, b * S:(b + 1) * S], LX[:, b * 128:(b + 1) * 128], IDN[0:S, 0:S])
            last.then_inc(sem("l1x_t"), 1)

        def l1x_act(act):
            norm_act(act, "l1x", X, 1e-5)
            act.wait_ge(sem("l1x_less"), 1)
            A.activation(LX, LX, ACT.Exp, scale=1 / math.sqrt(D)).then_inc(sem("l1x_e"), 1)

        def l1x_dve(dve):
            norm_dve(dve, "l1x", X, Y[:, :])
            m8, d8 = MM[0:S, 0, :], RD[0:S, 0, :]
            dve.wait_ge(sem("l1x_o"), 1)
            link(dve, "dve_chain", V.tensor_reduce(m8.rearrange("p (a b) -> p a b", a=2), LXP, AX.X, ALU.max))
            V.tensor_tensor(LX.rearrange("p (a b n) -> p a b n", a=2, b=4), LXP,
                            bc(m8.rearrange("p (a b) -> p a b", a=2).unsqueeze(3), S, 2, 4, 128),
                            ALU.subtract).then_inc(sem("l1x_less"), 1)
            dve.wait_ge(sem("l1x_e"), 1)
            link(dve, "dve_chain", V.tensor_reduce(d8, LX8, AX.X, ALU.add))
            link(dve, "dve_chain", V.reciprocal(d8, d8))
            V.tensor_tensor(LX8, LX8, bc(d8.unsqueeze(2), S, B, 128), ALU.mult).then_inc(sem("l1x_p"), 1)
            dve.wait_ge(sem("l1x_t"), 1)
            V.tensor_tensor(X, X, bank(4), ALU.add).then_inc(sem("x_ready"), 1)

        CAP = float(2 * 2 * T // E)
        E8 = R[0:8, 0:6 * T].rearrange("p (a t) -> p a t", a=6)

        def l1f_pe(pe):
            norm_pe(pe, "l1f", X, x_is(5))
            normed(pe, "l1f")
            router_pe(pe, "l1f", Y[:, :], "l1f_g")
            to_experts_pe(pe, "l1f", (2, 3, 6, 7))
            pe.wait_ge(sem("big1_in"), 96)
            moe_pe(pe, "l1f", Y[:, :])

        def l1f_act(act):
            norm_act(act, "l1f", X, 1e-5)
            softmax_act(act, "l1f")
            moe_act(act, "l1f", ACT.Gelu)

        def l1f_dve(dve):
            norm_dve(dve, "l1f", X, Y[:, :])
            V.memset(E8[:, 0, :], 1.0)
            softmax_dve(dve, "l1f", True)
            link(dve, "dve_chain", V.tensor_tensor(TK[:, 1], TK[:, 1], col(1), ALU.mult))
            for k in range(2):
                link(dve, "dve_chain", V.tensor_tensor(TK[:, 6 + k], TK[:, 1], TK[:, 2 + k], ALU.mult))
                link(dve, "dve_chain", V.tensor_reduce(TS[:, 2 + k, :], TK[:, 6 + k], AX.X, ALU.add))
            link(dve, "dve_chain", V.tensor_tensor(TS[:, 4, :], TS[:, 2, :], TS[:, 3, :], ALU.add))
            link(dve, "dve_chain", V.tensor_scalar(TS[:, 4, :], TS[:, 4, :], 1e-9, None, ALU.add))
            link(dve, "dve_chain", V.reciprocal(TS[:, 4, :], TS[:, 4, :]))
            link(dve, "dve_chain", V.tensor_tensor(TK[:, 6], TK[:, 6], col(4), ALU.mult))
            V.tensor_tensor(TK[:, 7], TK[:, 7], col(4), ALU.mult).then_inc(sem("router_route"), 1)
            dve.wait_ge(sem("router_byexp"), ROUTER_AT["l1f"])
            V.tensor_copy(E8[:, 1, :], bank(2, T, 8))
            link(dve, "dve_chain", V.tensor_copy(E8[:, 2, :], bank(3, T, 8)))
            link(dve, "dve_chain", V.tensor_tensor_scan(E8[:, 3, :], E8[:, 0, :], E8[:, 1, :], 0.0, ALU.mult, ALU.add))
            link(dve, "dve_chain", V.tensor_tensor_scan(E8[:, 4, :], E8[:, 0, :], E8[:, 2, :], 0.0, ALU.mult, ALU.add))
            link(dve, "dve_chain", V.tensor_scalar(
                E8[:, 4, :], E8[:, 4, :], E8[:, 3, T - 1:T], CAP, ALU.add, ALU.is_le))
            link(dve, "dve_chain", V.tensor_tensor(E8[:, 4, :], E8[:, 4, :], bank(5, T, 8), ALU.mult))
            link(dve, "dve_chain", V.scalar_tensor_tensor(E8[:, 3, :], E8[:, 3, :], CAP, bank(4, T, 8),
                                                          ALU.is_le, ALU.mult))
            V.tensor_tensor(CF[:, :], E8[:, 3, :], E8[:, 4, :], ALU.add).then_inc(sem("router_cf"), 1)
            moe_dve(dve, "l1f")
            dve.wait_ge(sem("moe_sum"), 2)
            V.tensor_tensor(X, X, bank(6), ALU.add).then_inc(sem("x_ready"), 1)

        def r(n, k=1):
            return R[:, n * T:(n + k) * T]

        SCAN = [SK + n * T for n in range(3)] + [2 * KJ * D + SK + n * T for n in range(6)]

        def scan(n):
            return R[:, SCAN[n]:SCAN[n] + T] if n < 9 else AO[:, 1:, :].rearrange("p b t -> p (b t)")

        def l2a_pe(pe):
            norm_pe(pe, "l2a", X, x_is(6))
            norm_pe(pe, "l2a_1", None, None)
            normed(pe, "l2a_1")
            for n in range(4):
                mm(bank(2 + n), w("l2a_in", n * 128, 128), Z[:, :]).then_inc(sem("l2a_uz"), 1)
            pe.wait_ge(sem("l2a_silu"), 2)
            for n in range(2):
                for k in range(2):
                    last = mm(bank(6 + n), w("l2a_dt", k * 256 + n * 128, 128), scan(k), k == 0, k == 1)
                last.then_inc(sem("l2a_dt"), 1)
            pe.wait_ge(sem("l2a_lam"), 2)
            pe.wait_ge(sem("l2a_silu"), 4)
            x_pe(pe, 1, ahead=True)
            for n in range(2):
                pe.wait_ge(sem("l2a_s"), n + 1)
                last = mm(bank(3), w("l2a_out", n * 128, 128), scan(6 + n), n == 0, n == 1)
            last.then_inc(sem("l2a_y"), 1)

        def l2a_act(act):
            norm_act(act, "l2a", X, 1e-5)
            norm_act(act, "l2a_1", Y[:, :], 1e-5, (sem("norm_ready"), NORM_AT["l2a"]))
            for n in range(4):
                act.wait_ge(sem("l2a_uz"), n + 1)
                A.activation(scan(n), bank(2 + n), ACT.Silu).then_inc(sem("l2a_silu"), 1)
            for n in range(2):
                act.wait_ge(sem("l2a_dt"), n + 1)
                A.activation(scan(4 + n), bank(6 + n), ACT.Sigmoid, bias=w("l2a_bdt", n, 1)).then_inc(sem("l2a_lam"), 1)
            x_act(act, 1, ahead=True)

        def l2a_dve(dve):
            norm_dve(dve, "l2a", X, Y[:, :])
            norm_dve(dve, "l2a_1", Y[:, :], Z[:, :], w("l2a_n"))
            split_weights(dve, 1)
            for n in range(2):
                dve.wait_ge(sem("l2a_lam"), n + 1)
                link(dve, "dve_chain", V.scalar_tensor_tensor(
                    scan(6 + n), scan(4 + n), 1.0, scan(n), ALU.subtract, ALU.mult))
                link(dve, "dve_chain", V.tensor_tensor(scan(4 + n), scan(4 + n), w("reset"), ALU.mult))
                link(dve, "dve_chain", V.tensor_tensor_scan(
                    scan(8 + n), scan(4 + n), scan(6 + n), 0.0, ALU.mult, ALU.subtract))
                dve.wait_ge(sem("l2a_silu"), 3 + n)
                V.tensor_tensor(scan(6 + n), scan(8 + n), scan(2 + n), ALU.mult).then_inc(sem("l2a_s"), 1)
            link(dve, "dve_chain", V.tensor_tensor(X, X, Y[:, :], ALU.add))
            x_dve(dve, 1, ahead=True)
            dve.wait_ge(sem("l2a_y"), 1)
            V.tensor_tensor(X, X, bank(3), ALU.add).then_inc(sem("x_ready"), 1)

        def l2x_end_dve(dve):
            dve.wait_ge(sem("f_copied"), folds(1, B + 1))
            V.scalar_tensor_tensor(X, AO[:, 1:, :].rearrange("p b t -> p (b t)"), w("l2x_bv"), X, ALU.add, ALU.add
                                   ).then_inc(sem("x_ready"), 1)

        MAGIC = float(1.5 * 2 ** 23)
        XQ = R[0:TT, 0:512]
        XQ4 = XQ.rearrange("p (j n) -> p j n", j=NT)

        def l2f_pe(pe):
            norm_pe(pe, "l2f", X, x_is(8))
            normed(pe, "l2f")
            for j in range(NT):
                last = mm(PS[0:TT, 2, j * 128:(j + 1) * 128], Y[:, j * TT:(j + 1) * TT], w("hadamard"))
            last.then_inc(sem("l2f_xh"), 1)
            pe.wait_ge(sem("l2f_made"), 1)
            PE.transpose(PS[:, 3, 0:128], R[:, 512:640], IDN).then_inc(sem("l2f_t"), 1)
            pe.wait_ge(sem("l2f_made"), 2)
            for j in range(NT):
                last = PE.transpose(PS[:, 4, j * TT:(j + 1) * TT], XQ[:, j * 128:(j + 1) * 128], IDN[0:TT, 0:TT])
            last.then_inc(sem("l2f_t"), 1)
            pe.wait_ge(sem("l2f_made"), 4)
            mm(bank(5), R[:, 768:896], R[:, 896:896 + T]).then_inc(sem("l2f_y"), 1)

        def l2f_act(act):
            norm_act(act, "l2f", X, 1e-5)

        def l2f_dve(dve):
            norm_dve(dve, "l2f", X, Y[:, :])
            c = AL
            wt, tq, t2 = w("l2f_w"), R[:, 512:640], R[:, 640:768]
            link(dve, "dve_chain", V.tensor_reduce(c[:, 0:1], wt, AX.X, ALU.add, apply_absolute_value=True))
            link(dve, "dve_chain", V.tensor_scalar(c[:, 0:1], c[:, 0:1], 1 / 128, 1e-5, ALU.mult, ALU.max))
            link(dve, "dve_chain", V.reciprocal(c[:, 1:2], c[:, 0:1]))
            link(dve, "dve_chain", V.tensor_scalar(tq, wt, c[:, 1:2], 0.5, ALU.mult, ALU.is_gt))
            link(dve, "dve_chain", V.tensor_scalar(t2, wt, c[:, 1:2], -0.5, ALU.mult, ALU.is_lt))
            link(dve, "dve_chain", V.tensor_tensor(tq, tq, t2, ALU.subtract))
            V.tensor_scalar(tq, tq, c[:, 0:1], None, ALU.mult).then_inc(sem("l2f_made"), 1)
            dve.wait_ge(sem("l2f_xh"), 1)
            xh = PS[0:TT, 2, :].rearrange("p (j n) -> p j n", j=NT)
            link(dve, "dve_chain", V.tensor_reduce(TS[:, 0, :], xh, AX.X, ALU.max, apply_absolute_value=True))
            link(dve, "dve_chain", V.tensor_scalar(TS[:, 0, :], TS[:, 0, :], 1e-5, 1 / 7, ALU.max, ALU.mult))
            link(dve, "dve_chain", V.reciprocal(TS[:, 1, :], TS[:, 0, :]))
            link(dve, "dve_chain", V.tensor_tensor(XQ4, xh, bc(TS[:, 1, :].unsqueeze(2), TT, NT, 128), ALU.mult))
            link(dve, "dve_chain", V.tensor_scalar(XQ, XQ, MAGIC, MAGIC, ALU.add, ALU.subtract))
            link(dve, "dve_chain", V.tensor_scalar(XQ, XQ, -8.0, 7.0, ALU.max, ALU.min))
            V.tensor_tensor(XQ4, XQ4, bc(TS[:, 0, :].unsqueeze(2), TT, NT, 128), ALU.mult).then_inc(sem("l2f_made"), 1)
            dve.wait_ge(sem("l2f_t"), 1)
            V.tensor_copy(R[:, 768:896], PS[:, 3, 0:128]).then_inc(sem("l2f_made"), 1)
            dve.wait_ge(sem("l2f_t"), 2)
            V.tensor_copy(R[:, 896:896 + T], bank(4)).then_inc(sem("l2f_made"), 1)
            dve.wait_ge(sem("l2f_y"), 1)
            V.tensor_tensor(X, X, bank(5), ALU.add).then_inc(sem("x_ready"), 1)

        ST = 64
        VEC = sb("VEC", [128, 2])
        GD = sb("GD", [128, 4])

        def state(n):
            return R[0:ST, 2 * KJ * D + SK + n * T:2 * KJ * D + SK + (n + 1) * T]

        def l3a_pe(pe):
            norm_pe(pe, "l3a", X, x_is(9))
            normed(pe, "l3a")
            mm(bank(2), w("l3a_shift"), Y[:, :]).then_inc(sem("l3a_p"), 1)
            norm_pe(pe, "l3a_1", Z[:, :], (sem("l3a_xs"), 1))
            normed(pe, "l3a_1")
            mm(bank(3, T, ST), w("l3a_key"), Z[:, :]).then_inc(sem("l3a_p"), 1)
            mm(bank(4, T, ST), w("l3a_value"), Z[:, :]).then_inc(sem("l3a_p"), 1)
            pe.wait_ge(sem("l3a_xs"), 1)
            x_pe(pe, 2, ahead=True)
            pe.wait_ge(sem("l3a_states"), 1)
            mm(bank(5), w("l3a_out", p=ST), state(2)).then_inc(sem("l3a_p"), 1)

        def l3a_act(act):
            A.activation(GD[:, 0:1], w("l3a_gate"), ACT.Sigmoid).then_inc(sem("l3a_vecs"), 1)
            A.activation(GD[0:ST, 2:3], w("l3a_first", p=ST), ACT.Exp).then_inc(sem("l3a_vecs"), 1)
            A.activation(GD[0:ST, 3:4], w("l3a_decay", p=ST), ACT.Exp).then_inc(sem("l3a_vecs"), 1)
            norm_act(act, "l3a", X, 1e-5)
            norm_act(act, "l3a_1", None, 1e-5)
            act.wait_ge(sem("l3a_p"), 2)
            A.activation(state(0), bank(3, T, ST), ACT.Sigmoid).then_inc(sem("l3a_sig"), 1)
            act.wait_ge(sem("l3a_sig"), 1)
            act.wait_ge(sem("l3a_neg"), 1)
            A.activation(state(0), state(0), ACT.Exp, scale=VEC[0:ST, 0:1]).then_inc(sem("l3a_sig"), 1)
            x_act(act, 2, ahead=True)

        def l3a_dve(dve):
            norm_dve(dve, "l3a", X, Y[:, :])
            dve.wait_ge(sem("l3a_vecs"), 3)
            V.tensor_scalar(VEC[0:ST, 0:1], GD[0:ST, 2:3], -1.0, None, ALU.mult).then_inc(sem("l3a_neg"), 1)
            link(dve, "dve_chain", V.tensor_scalar(GD[:, 1:2], GD[:, 0:1], -1.0, 1.0, ALU.mult, ALU.add))
            V.tensor_scalar(state(1), w("reset", p=ST), GD[0:ST, 3:4], None, ALU.mult)
            link(dve, "dve_chain", V.tensor_scalar(Z[:, :], Y[:, :], GD[:, 1:2], None, ALU.mult))
            dve.wait_ge(sem("l3a_p"), 1)
            z, p = (a.rearrange("p (b h t) -> p b h t", b=B, h=2) for a in (Z[:, :], bank(2)))
            for h in range(2):
                last = V.scalar_tensor_tensor(z[:, :, h], p[:, :, 1 - h], GD[:, 0:1], z[:, :, h], ALU.mult, ALU.add)
            last.then_inc(sem("l3a_xs"), 1)
            norm_dve(dve, "l3a_1", Z[:, :], Z[:, :], w("l3a_g"), w("l3a_c"))
            split_weights(dve, 2)
            dve.wait_ge(sem("l3a_p"), 3)
            dve.wait_ge(sem("l3a_sig"), 2)
            link(dve, "dve_chain", V.tensor_tensor(state(0), state(0), bank(4, T, ST), ALU.mult))
            V.tensor_tensor_scan(state(2), state(1), state(0), 0.0, ALU.mult, ALU.add
                                 ).then_inc(sem("l3a_states"), 1)
            x_dve(dve, 2, ahead=True)
            dve.wait_ge(sem("l3a_p"), 4)
            V.tensor_tensor(X, X, bank(5), ALU.add).then_inc(sem("x_ready"), 1)

        def l3x_end_pe(pe):
            pe.wait_ge(sem("l3x_a"), 1)
            mm(bank(2), w("l3x_o"), Z[:, :]).then_inc(sem("x_out"), 1)

        def l3x_end_dve(dve):
            dve.wait_ge(sem("f_copied"), folds(2, B + 1))
            V.tensor_scalar(Z[:, :], AO[:, 1:, :].rearrange("p b t -> p (b t)"), w("l3x_bv"), None, ALU.add
                            ).then_inc(sem("l3x_a"), 1)
            dve.wait_ge(sem("x_out"), 2)
            V.scalar_tensor_tensor(X, bank(2), w("l3x_bo"), X, ALU.add, ALU.add).then_inc(sem("x_ready"), 1)

        def l3f_pe(pe):
            norm_pe(pe, "l3f", X, x_is(11))
            normed(pe, "l3f")
            router_pe(pe, "l3f", Y[:, :], "l3f_router")
            gates = [w("l3f_sg")] + [w("l3f_eg", n * 128, 128) for n in range(4)]
            ups = [w("l3f_su")] + [w("l3f_eu", n * 128, 128) for n in range(4)]
            downs = [w("l3f_sd")] + [w("l3f_ed", n * 128, 128) for n in range(4)]

            def down(n):
                pe.wait_ge(sem("l3f_h"), n + 1)
                mm(bank(0), downs[n], r(2 * (n % 2)), n == 0, n == 4).then_inc(sem("l3f_dn"), 1)

            for n in range(5):
                if n == 1:
                    to_experts_pe(pe, "l3f", (6,))
                    pe.wait_ge(sem("router_cf"), ROUTER_AT["l3f"])
                if n >= 2:
                    pe.wait_ge(sem("l3f_h"), n - 1)
                s = 2 if n % 2 else 5
                mm(bank(s), gates[n], Y[:, :]).then_inc(sem("l3f_g"), 1)
                last = mm(bank(s + 1), ups[n], Y[:, :])
                if n:
                    for k in range(2):
                        last = mm(PS[64 * k:64 * k + 64, s + 2, 0:T], bc(w("ident", 2 * n - 2 + k, 1, 8), 8, 64),
                                  CF[:, :])
                last.then_inc(sem("l3f_u"), 1)
                if n:
                    down(n - 1)
            down(4)

        def l3f_act(act):
            norm_act(act, "l3f", X, 1e-5)
            softmax_act(act, "l3f")
            for n in range(5):
                act.wait_ge(sem("l3f_g"), n + 1)
                if n >= 2:
                    act.wait_ge(sem("l3f_dn"), n - 1)
                A.activation(r(2 * (n % 2)), bank(2 if n % 2 else 5), ACT.Silu).then_inc(sem("l3f_silu"), 1)

        def l3f_dve(dve):
            norm_dve(dve, "l3f", X, Y[:, :])
            softmax_dve(dve, "l3f", True)
            link(dve, "dve_chain", V.tensor_tensor(TK[:, 1], TK[:, 1], col(1), ALU.mult))
            link(dve, "dve_chain", V.tensor_tensor(TK[:, 2], TK[:, 2], TK[:, 3], ALU.add))
            V.tensor_tensor(TK[:, 6], TK[:, 1], TK[:, 2], ALU.mult).then_inc(sem("router_route"), 1)

            def hidden(n):
                h, s = r(2 * (n % 2)), 2 if n % 2 else 5
                dve.wait_ge(sem("l3f_silu"), n + 1)
                dve.wait_ge(sem("l3f_u"), n + 1)
                if n:
                    link(dve, "dve_chain", V.tensor_tensor(h, h, bank(s + 1), ALU.mult))
                    V.tensor_tensor(h, h, bank(s + 2), ALU.mult).then_inc(sem("l3f_h"), 1)
                else:
                    V.tensor_tensor(h, h, bank(s + 1), ALU.mult).then_inc(sem("l3f_h"), 1)

            hidden(0)
            dve.wait_ge(sem("router_byexp"), ROUTER_AT["l3f"])
            V.tensor_copy(CF[:, :], bank(2, T, 8)).then_inc(sem("router_cf"), 1)
            for n in range(1, 5):
                hidden(n)
            dve.wait_ge(sem("l3f_dn"), 5)
            V.tensor_tensor(X, X, bank(0), ALU.add).then_inc(sem("x_ready"), 1)



        @block.sync
        def _(sp):
            first, half = AT["ident"][0], AT["l1a_q"][0]
            sp.dma_start(W[:, 0:first], small[:, 0:first]).then_inc(sem("x_in"), 16)
            sp.dma_start(W[:, first:half], small[:, first:half]).then_inc(sem("small_in"), 16)
            sp.dma_start(W[:, half:], small[:, half:]).then_inc(sem("rest_in"), 16)
            sp.dma_start(MROW, mrow).then_inc(sem("mask_in"), 16)
            sp.dma_start(KT32, mcol).then_inc(sem("mask_in"), 16)
            for n in range(2):
                sp.dma_start(ROPE_K[:, n * SK:(n + 1) * SK], rope[:, n * SK:(n + 1) * SK]).then_inc(sem("rope_in"), 16)
            sp.dma_start(ROPE_Q[:, :, :], rope[:, 2 * SK:2 * SK + 2 * S].rearrange("p (a t) -> p a t", a=2)
                         ).then_inc(sem("rope_in"), 16)
            for n in range(6):
                sp.dma_start(WB[:, n * 2048:(n + 1) * 2048], big0[:, n * 2048:(n + 1) * 2048]
                             ).then_inc(sem("big0_in"), 16)
            for v in range(2):
                sp.wait_ge(sem("mask_rows"), v + 1)
            sp.dma_start(mscr.rearrange("v b k -> b v k"), R16).then_inc(sem("mask_out"), 16)
            sp.wait_ge(sem("mask_out"), 16)
            if LAYERS > 1:
                x_sp(sp, 0)
            if LAYERS > 5:
                sp.wait_ge(*x_is(3))
                for n in (2, 3, 4, 5, 0, 1):
                    sp.dma_start(WB[:, n * 2048:(n + 1) * 2048],
                                 big1[:, n * 2048:(n + 1) * 2048]).then_inc(sem("big1_in"), 16)
            if LAYERS > 7:
                x_sp(sp, 1)
            if LAYERS > 10:
                x_sp(sp, 2)
            sp.wait_ge(*x_is(LAYERS))
            sp.dma_start(out, X).then_inc(sem("out_written"), 16)
            sp.wait_ge(sem("out_written"), 16)

        @block.gpsimd
        def _(pool):
            for ap, value in ((SEL96[:, :], 0.0), (ONE16[:, :], 1.0), (QS[:, :, :], 0.0), (PH[:, :, :, :], 1.0),
                              (PL[:, :, :, :], 0.0), (OM[:, 1, :, :], 0.0)):
                link(pool, "pool_chain", G.memset(ap, value))
            G.memset(SEL96[:, 96:97], 1.0).then_inc(sem("sel_ready"), 1)
            pool.wait_ge(sem("sel_ready"), 1)
            pool.sem_inc(sem("pool_ready"), 1)
            pool.sem_inc(sem("om_ready"), 1)
            pool.sem_inc(sem("qs_clear"), 1)
            pool_layers = [l0a_pool, lambda e: x_pool(e, 0), l0f_pool, None, None, None, None,
                           lambda e: x_pool(e, 1), None, None, lambda e: x_pool(e, 2), None]
            for layer in pool_layers[:LAYERS]:
                if layer:
                    layer(pool)

        @block.vector
        def _(dve):
            dve.sem_inc(sem("m_done"), 3)
            dve.sem_inc(sem("low_d"), 2)
            dve.sem_inc(sem("low_p"), 2)
            dve.wait_ge(sem("x_in"), 16)
            dve.sem_inc(sem("x_ready"), 1)
            for layer in (l0a_dve, lambda e: (x_dve(e, 0), l0x_end_dve(e)), l0f_dve, l1a_dve, l1x_dve, l1f_dve,
                          l2a_dve, lambda e: (x_dve(e, 1), l2x_end_dve(e)), l2f_dve, l3a_dve,
                          lambda e: (x_dve(e, 2), l3x_end_dve(e)), l3f_dve)[:LAYERS]:
                layer(dve)

        @block.scalar
        def _(act):
            act.sem_inc(sem("e_ready"), 3)
            A.preload_act_table_set("natural_log_exp_and_others")
            act.wait_ge(*x_is(0))
            for layer in (l0a_act, lambda e: x_act(e, 0), l0f_act, l1a_act, l1x_act, l1f_act, l2a_act,
                          lambda e: x_act(e, 1), l2f_act, l3a_act, lambda e: x_act(e, 2), l3f_act)[:LAYERS]:
                layer(act)

        @block.tensor
        def _(pe):
            pe.sem_inc(sem("s_ready"), CLEAR)
            pe.sem_inc(sem("p_ready"), 4)
            for layer in (l0a_pe, lambda e: (x_pe(e, 0), l0x_end_pe(e)), l0f_pe, l1a_pe, l1x_pe, l1f_pe, l2a_pe,
                          lambda e: x_pe(e, 1), l2f_pe, l3a_pe, lambda e: (x_pe(e, 2), l3x_end_pe(e)),
                          l3f_pe)[:LAYERS]:
                layer(pe)


LAYERS = 12


def constants():
    c = {}
    eye = np.eye(128, dtype=np.float32)
    c["ident"] = eye
    c["mean"] = np.full((128, 128), 1 / 128, np.float32)
    c["ones"] = np.ones((128, 128), np.float32)
    c["half"] = np.kron(np.eye(2), np.ones((64, 64))).astype(np.float32)
    row = np.arange(128)
    c["fold"] = (row[:, None] % SP2 == np.arange(S)[None]).astype(np.float32)
    c["blk8"] = (row[:, None] // SP2 == np.arange(16)[None] // 8).astype(np.float32)
    c["blk16"] = (row[:, None] // SP2 == np.arange(32)[None] // 16).astype(np.float32)
    c["headmask"] = (row[:, None] // 8 == np.arange(16)[None]).astype(np.float32)
    q = row[:, None] % SP2
    c["causal"] = np.where((np.arange(S)[None] > q) & (q < S), -1e9, 0).astype(np.float32)
    c["iota"] = np.tile(np.arange(8, dtype=np.float32), (128, 1))
    c["reset"] = np.tile((np.arange(T) % S != 0).astype(np.float32), (128, 1))
    t, s = row[:, None], np.arange(TT)[None]
    same, near = t // S == s // S, t // 7 == s // 7
    c["inlow"] = -((t > s) & near).astype(np.float32)
    c["inup"] = -((t < s) & near).astype(np.float32)
    c["offlow"] = -((t > s) & same & ~near).astype(np.float32)
    c["upper"] = ((t <= s) & same).astype(np.float32)
    h = np.array([[1.0]])
    while h.shape[0] < 128:
        h = np.block([[h, h], [h, -h]])
    c["hadamard"] = (h / np.sqrt(128)).astype(np.float32)
    return c


def rope_tables():
    half = np.arange(0, 16, 2, dtype=np.float32) / np.float32(16)
    inv = np.float32(1.0) / np.float32(10000.0) ** half
    pos = np.arange(SK, dtype=np.float32)
    freqs = pos[:, None] * inv
    emb = np.concatenate([freqs, freqs], -1)
    sign = np.where(np.arange(16) < 8, -1, 1).astype(np.float32)
    cos, sin = np.cos(emb).T, np.sin(emb).T * sign[:, None]
    order = (np.arange(KP)[None, :] * KJ + np.arange(KJ)[:, None]).reshape(-1)
    parts = [cos[:, order], sin[:, order], cos[:, :S], sin[:, :S]]
    return np.ascontiguousarray(np.concatenate([np.tile(a, (8, 1)) for a in parts], 1), dtype=np.float32)


def kernel(**inputs):
    import concourse.bacc as bacc
    from concourse.bass_utils import run_bass_kernel_spmd

    a = {k: np.asarray(v) for k, v in inputs.items()}
    pieces = dict(constants())

    def vec(v):
        v = v.reshape(-1)
        if v.size < 128:
            return np.concatenate([v, np.zeros(128 - v.size, v.dtype)]).reshape(128, 1)
        return v.reshape(-1, 128).T

    def rows(m):
        return np.concatenate([m, np.zeros((128 - m.shape[0], m.shape[1]), m.dtype)], 0)

    def tall(m):
        return m.reshape(-1, 128, m.shape[-1]).transpose(1, 0, 2).reshape(128, -1)

    swap = np.arange(128).reshape(8, 2, 8)[:, ::-1].reshape(-1)
    p = pieces
    p["x"] = a["x"].transpose(2, 0, 1).reshape(128, T)
    wi = a["L0_attn_in_proj_w"].T
    p["l0a_q"], p["l0a_k"], p["l0a_v"] = wi[:, 0:128], wi[:, 128:256], wi[:, 256:384]
    p["l0a_out"], p["l0a_w1"], p["l0a_w2"] = a["L0_attn_out_w"].T, a["L0_attn_lin1_w"].T, tall(a["L0_attn_lin2_w"].T)
    bi = a["L0_attn_in_proj_b"]
    p["l0a_bq"], p["l0a_bk"], p["row_bv"] = vec(bi[0:128]), vec(bi[128:256]), rows(bi[None, 256:384])
    p["l0a_bout"], p["l0a_b1"], p["l0a_b2"] = (vec(a["L0_attn_" + n]) for n in ("out_b", "lin1_b", "lin2_b"))
    p["l0a_g1"], p["l0a_c1"] = vec(a["L0_attn_ln1_g"]), vec(a["L0_attn_ln1_b"])
    p["l0a_g2"], p["l0a_c2"] = vec(a["L0_attn_ln2_g"]), vec(a["L0_attn_ln2_b"])
    wq, wkv = a["L0_xattn_Wq"].T, a["L0_xattn_Wkv"].T
    p["l0x_q"], p["l0x_qr"], p["l0x_k"], p["l0x_kr"] = wq, wq[:, swap], wkv[:, 0:128], wkv[:, 0:128][:, swap]
    p["l0x_v"], p["l0x_out"] = wkv[:, 128:256], a["L0_xattn_Wout"].T
    p["l0f_gate"], p["row_gb"] = a["L0_ffn_gate_w"], rows(a["L0_ffn_gate_b"][None])
    p["l0f_b1"], p["l0f_b2"] = vec(a["L0_ffn_b1"]), rows(a["L0_ffn_b2"])
    p["l0f_g"], p["l0f_c"] = vec(a["L0_ffn_ln_g"]), vec(a["L0_ffn_ln_b"])
    p["l0f_qs"], p["l0f_ks"] = vec(a["L0_ffn_q_scale"]), vec(a["L0_ffn_k_scale"])
    p["l1a_q"], p["l1a_k"], p["l1a_v"], p["l1a_o"] = (a["L1_attn_W" + n] for n in "qkvo")
    p["l1a_beta"] = np.broadcast_to(a["L1_attn_beta_w"], (128, 128))
    p["l1a_bb"] = np.broadcast_to(a["L1_attn_beta_b"].reshape(1, 1), (128, 1))
    p["l1a_gate"], p["l1a_up"], p["l1a_down"] = a["L1_attn_w_gate"], a["L1_attn_w_up"], tall(a["L1_attn_w_down"])
    p["l1a_n1"], p["l1a_n2"], p["l1a_alpha"] = (vec(a["L1_attn_" + n]) for n in ("norm1_w", "norm2_w", "alpha_logit"))
    p["l1f_g"], p["l1f_b1"], p["l1f_b2"] = a["L1_ffn_Wg"], vec(a["L1_ffn_b1"]), rows(a["L1_ffn_b2"])
    p["l2a_in"], p["l2a_dt"], p["l2a_out"] = a["L2_attn_W_in"].T, tall(a["L2_attn_W_dt"].T), tall(a["L2_attn_W_out"].T)
    p["l2a_n"], p["l2a_bdt"] = vec(a["L2_attn_w_norm"]), vec(a["L2_attn_b_dt"])
    for n in "qkv":
        p["l2x_" + n], p["l2x_b" + n] = a[f"L2_xattn_{n}_w"].T, vec(a[f"L2_xattn_{n}_b"])
        p["l3x_" + n], p["l3x_b" + n] = a["L3_xattn_W" + n], vec(a["L3_xattn_b" + n])
    p["l3x_o"], p["l3x_bo"] = a["L3_xattn_Wo"], vec(a["L3_xattn_bo"])
    p["l2f_w"] = a["L2_ffn_weight"]
    p["l3a_key"], p["l3a_value"] = a["L3_attn_W_key"].T, a["L3_attn_W_value"].T
    p["l3a_out"] = rows(a["L3_attn_W_output"].T)
    p["l3a_shift"] = a["L3_attn_W_shift"].T
    p["l3a_decay"], p["l3a_first"] = vec(a["L3_attn_time_decay"]), vec(a["L3_attn_time_first"])
    p["l3a_gate"] = vec(a["L3_attn_shift_gate"])
    p["l3a_g"], p["l3a_c"] = vec(a["L3_attn_ln_w"]), vec(a["L3_attn_ln_b"])
    p["l3f_router"] = a["L3_ffn_router"]
    p["l3f_eg"] = a["L3_ffn_experts_gate"].transpose(1, 0, 2).reshape(128, 512)
    p["l3f_eu"] = a["L3_ffn_experts_up"].transpose(1, 0, 2).reshape(128, 512)
    p["l3f_ed"] = tall(a["L3_ffn_experts_down"].reshape(512, 128))
    p["l3f_sg"], p["l3f_su"], p["l3f_sd"] = (a["L3_ffn_shared_" + n] for n in ("gate", "up", "down"))
    small = np.ascontiguousarray(np.concatenate([p[name] for name, _ in SMALL], 1))

    def experts(n):
        w1 = a[f"{n}_w1" if n == "L0_ffn" else f"{n}_W1"].transpose(1, 0, 2).reshape(128, E * F)
        w2 = a[f"{n}_w2" if n == "L0_ffn" else f"{n}_W2"].reshape(E * F, 128)
        return [w1, tall(w2)]

    big0 = np.ascontiguousarray(np.concatenate(
        [a["L0_ffn_Wq"], a["L0_ffn_Wk"], a["L0_ffn_Wv"], tall(a["L0_ffn_Wo"])] + experts("L0_ffn"), 1))
    late = [p[name] for name, _ in LATE]
    big1 = np.ascontiguousarray(np.concatenate(late + experts("L1_ffn"), 1))
    mask = a["mask_BxS2_ik0"].reshape(B, KP, KJ)
    arrays = {
        "small": small, "big0": big0, "big1": big1, "ctx": np.ascontiguousarray(a["ctx_1024"]),
        "mrow": np.ascontiguousarray(mask.transpose(0, 2, 1).reshape(B, SK)),
        "mcol": np.ascontiguousarray(mask.transpose(1, 0, 2).reshape(KP, B * KJ)), "rope": rope_tables(),
    }
    nc = bacc.Bacc("TRN2", target_bir_lowering=False, num_devices=1)
    args = [nc.dram_tensor(k, v.shape, mybir.dt.from_np(v.dtype), kind="ExternalInput").ap() for k, v in arrays.items()]
    out = nc.dram_tensor("out", (128, T), mybir.dt.float32, kind="ExternalOutput").ap()
    f16 = mybir.dt.float16
    scratch = [nc.dram_tensor("k_halves", (2, 128, 2, SK), f16).ap(), nc.dram_tensor("q_halves", (128, 2, T), f16).ap(),
               nc.dram_tensor("mask_rows_dram", (2, B, SK), f16).ap(),
               nc.dram_tensor("ctx_halves", (B, D, 2, SK), f16).ap()]
    build(nc, *args, out, scratch)
    got = run_bass_kernel_spmd(nc, [arrays], core_ids=[0]).results[0]["out"]
    return np.ascontiguousarray(got.reshape(128, B, S).transpose(1, 2, 0))
```
